# Optimizing a Trainium2 kernel written in Bass

```python
import numpy as np
import jax
import jax.numpy as jnp

def _softmax(x, axis=-1):
    return jax.nn.softmax(x, axis=axis)

def _gelu(x):
    return jax.nn.gelu(x, approximate=True)

def _silu(x):
    return jax.nn.silu(x)

def _sigmoid(x):
    return jax.nn.sigmoid(x)

def _layernorm(x, axis=-1, eps=1e-05):
    m = jnp.mean(x, axis=axis, keepdims=True)
    v = jnp.var(x, axis=axis, keepdims=True)
    return (x - m) / jnp.sqrt(v + eps)

def _scatter_add(tgt, idx, src, axis=0):
    return tgt.at[idx].add(src)

def _segment_sum(src, seg, n):
    return jax.ops.segment_sum(src, seg, n)
kernel_name = 'mk_gps_d1_gnn_r8_1f338c'

def setup_inputs(seed: int=0):
    np.random.seed(seed)
    _w = jnp.asarray

    def _rec_inputs():
        import jax
        import jax.numpy as jnp
        _gk = jax.random.key(seed)
        x = -7.329e-05 + 0.9999 * jax.random.normal(jax.random.fold_in(_gk, 1), (6250, 512), jnp.float32)
        src = jax.random.randint(jax.random.fold_in(_gk, 2), (100000,), 0, 6250, jnp.int32)
        dst = jnp.minimum((6250 * jax.random.uniform(jax.random.fold_in(_gk, 3), (100000,)) ** 2.0).astype(jnp.int32), 49999)
        _o = jnp.argsort(dst, stable=True)
        src = src[_o]
        dst = dst[_o]
        edge_weight = jax.random.uniform(jax.random.fold_in(_gk, 12), (100000,), jnp.float32, 0.0, 0.999999)
        return (x, src, dst, edge_weight)
    x, src, dst, edge_weight = _rec_inputs()

    def _L0_gnn_setup():
        import jax, jax.numpy as jnp
        import numpy as np
        N_NODES = 12500
        N_EDGES = 100000
        D_IN = 512
        D_OUT = 512
        key = jax.random.key(seed)
        k1, k2, k3, k4, k5, k6 = jax.random.split(key, 6)
        x = jax.random.normal(k1, (N_NODES, D_IN), dtype=jnp.float32)
        src = jax.random.randint(k2, (N_EDGES,), 0, N_NODES)
        dst = jax.random.randint(k3, (N_EDGES,), 0, N_NODES)
        adj_vals = jax.random.uniform(k4, (N_EDGES,), dtype=jnp.float32)
        stdv = 1.0 / float(np.sqrt(D_OUT))
        weight = jax.random.uniform(k5, (D_IN, D_OUT), dtype=jnp.float32, minval=-stdv, maxval=stdv)
        bias = jax.random.uniform(k6, (D_OUT,), dtype=jnp.float32, minval=-stdv, maxval=stdv)
        return {'x': x, 'adj_vals': adj_vals, 'weight': weight, 'bias': bias, 'src': src, 'dst': dst}
    _L0_gnn_all = _L0_gnn_setup()
    _L0_gnn_in = {k: v for k, v in _L0_gnn_all.items() if k in ('weight', 'bias')}
    del _L0_gnn_all

    def _L0_mix_setup():
        import jax, jax.numpy as jnp
        import numpy as np
        B, S, DM = (4, 1024, 512)
        H = 8
        D = DM // H

        def _feature_map(t):
            return jax.nn.elu(t) + 1.0
        key = jax.random.key(seed)
        ks = jax.random.split(key, 9)
        s = 1.0 / np.sqrt(DM)
        x = jax.random.normal(ks[0], (B, S, DM), dtype=jnp.float32)
        Wq = jax.random.normal(ks[1], (DM, DM), dtype=jnp.float32) * s
        bq = jnp.zeros((DM,), dtype=jnp.float32)
        Wk = jax.random.normal(ks[2], (DM, DM), dtype=jnp.float32) * s
        bk = jnp.zeros((DM,), dtype=jnp.float32)
        Wv = jax.random.normal(ks[3], (DM, DM), dtype=jnp.float32) * s
        bv = jnp.zeros((DM,), dtype=jnp.float32)
        Wp = jax.random.normal(ks[4], (DM, DM), dtype=jnp.float32) * s
        bp = jnp.zeros((DM,), dtype=jnp.float32)
        return {'x': x, 'Wq': Wq, 'bq': bq, 'Wk': Wk, 'bk': bk, 'Wv': Wv, 'bv': bv, 'Wp': Wp, 'bp': bp}
    _L0_mix_all = _L0_mix_setup()
    _L0_mix_in = {k: v for k, v in _L0_mix_all.items() if k in ('Wq', 'bq', 'Wk', 'bk', 'Wv', 'bv', 'Wp', 'bp')}
    del _L0_mix_all

    def _L0_ffn_setup():
        import jax, jax.numpy as jnp
        import numpy as np
        B, S, D, F, E = (8, 512, 512, 256, 8)
        INIT_LAMBDA = 0.2
        LN_EPS = 1e-05
        LN_MERGE = 0.03
        key = jax.random.key(seed)
        ks = jax.random.split(key, 12)
        n = lambda k, shp, s=1.0: jax.random.normal(k, shp, dtype=jnp.float32) * s
        return {'hidden_states': n(ks[0], (B, S, D)), 'gfc1_w': n(ks[1], (D, D), 0.01), 'gfc1_b': jnp.zeros((D,), jnp.float32), 'gfc2_w': n(ks[2], (E, D), 0.01), 'gfc2_b': jnp.full((E,), INIT_LAMBDA, dtype=jnp.float32), 'W1': n(ks[3], (F, D), 0.02), 'b1': jnp.zeros((F,), jnp.float32), 'W2': n(ks[4], (D, F), 0.02), 'b2': jnp.zeros((D,), jnp.float32), 'ln_g': jnp.ones((D,), jnp.float32), 'ln_b': jnp.zeros((D,), jnp.float32), 'tv_W1': n(ks[5], (E, F, D), 0.02), 'tv_b1': n(ks[6], (E, F), 0.02), 'tv_W2': n(ks[7], (E, D, F), 0.02), 'tv_b2': n(ks[8], (E, D), 0.02), 'tv_ln_g': n(ks[9], (E, D), 0.02), 'tv_ln_b': n(ks[10], (E, D), 0.02)}
    _L0_ffn_all = _L0_ffn_setup()
    _L0_ffn_in = {k: v for k, v in _L0_ffn_all.items() if k in ('gfc1_w', 'gfc1_b', 'gfc2_w', 'gfc2_b', 'W1', 'b1', 'W2', 'b2', 'ln_g', 'ln_b', 'tv_W1', 'tv_b1', 'tv_W2', 'tv_b2', 'tv_ln_g', 'tv_ln_b')}
    del _L0_ffn_all
    return {'x': x, 'src': src, 'dst': dst, 'edge_weight': edge_weight, 'L0_gnn_weight': _L0_gnn_in['weight'], 'L0_gnn_bias': _L0_gnn_in['bias'], 'L0_mix_Wq': _L0_mix_in['Wq'], 'L0_mix_bq': _L0_mix_in['bq'], 'L0_mix_Wk': _L0_mix_in['Wk'], 'L0_mix_bk': _L0_mix_in['bk'], 'L0_mix_Wv': _L0_mix_in['Wv'], 'L0_mix_bv': _L0_mix_in['bv'], 'L0_mix_Wp': _L0_mix_in['Wp'], 'L0_mix_bp': _L0_mix_in['bp'], 'L0_ffn_gfc1_w': _L0_ffn_in['gfc1_w'], 'L0_ffn_gfc1_b': _L0_ffn_in['gfc1_b'], 'L0_ffn_gfc2_w': _L0_ffn_in['gfc2_w'], 'L0_ffn_gfc2_b': _L0_ffn_in['gfc2_b'], 'L0_ffn_W1': _L0_ffn_in['W1'], 'L0_ffn_b1': _L0_ffn_in['b1'], 'L0_ffn_W2': _L0_ffn_in['W2'], 'L0_ffn_b2': _L0_ffn_in['b2'], 'L0_ffn_ln_g': _L0_ffn_in['ln_g'], 'L0_ffn_ln_b': _L0_ffn_in['ln_b'], 'L0_ffn_tv_W1': _L0_ffn_in['tv_W1'], 'L0_ffn_tv_b1': _L0_ffn_in['tv_b1'], 'L0_ffn_tv_W2': _L0_ffn_in['tv_W2'], 'L0_ffn_tv_b2': _L0_ffn_in['tv_b2'], 'L0_ffn_tv_ln_g': _L0_ffn_in['tv_ln_g'], 'L0_ffn_tv_ln_b': _L0_ffn_in['tv_ln_b']}

def reference(x, src, dst, edge_weight, L0_gnn_weight, L0_gnn_bias, L0_mix_Wq, L0_mix_bq, L0_mix_Wk, L0_mix_bk, L0_mix_Wv, L0_mix_bv, L0_mix_Wp, L0_mix_bp, L0_ffn_gfc1_w, L0_ffn_gfc1_b, L0_ffn_gfc2_w, L0_ffn_gfc2_b, L0_ffn_W1, L0_ffn_b1, L0_ffn_W2, L0_ffn_b2, L0_ffn_ln_g, L0_ffn_ln_b, L0_ffn_tv_W1, L0_ffn_tv_b1, L0_ffn_tv_W2, L0_ffn_tv_b2, L0_ffn_tv_ln_g, L0_ffn_tv_ln_b):
    import jax
    import jax.numpy as jnp

    def _L0_gnn_ref(x, adj_vals, weight, bias, src, dst):
        import jax, jax.numpy as jnp
        import numpy as np
        N_NODES = 12500
        N_EDGES = 100000
        D_IN = 512
        D_OUT = 512
        support = jax.ops.segment_sum(adj_vals[:, None] * x[src], dst, num_segments=x.shape[0])
        return support @ weight + bias

    def _L0_mix_ref(x, Wq, bq, Wk, bk, Wv, bv, Wp, bp):
        import jax, jax.numpy as jnp
        import numpy as np
        B, S, DM = (4, 1024, 512)
        H = 8
        D = DM // H

        def _feature_map(t):
            return jax.nn.elu(t) + 1.0
        b, s, _ = x.shape
        q = _feature_map(x @ Wq + bq).reshape(b, s, H, D)
        k = _feature_map(x @ Wk + bk).reshape(b, s, H, D)
        v = (x @ Wv + bv).reshape(b, s, H, D)
        kv = jnp.einsum('bshd,bshe->bhde', k, v)
        z = 1.0 / jnp.einsum('bshd,bhd->bsh', q, k.sum(axis=1))
        out = jnp.einsum('bshd,bhde,bsh->bshe', q, kv, z)
        out = out.reshape(b, s, H * D)
        return out @ Wp + bp

    def _L0_ffn_ref(hidden_states, gfc1_w, gfc1_b, gfc2_w, gfc2_b, W1, b1, W2, b2, ln_g, ln_b, tv_W1, tv_b1, tv_W2, tv_b2, tv_ln_g, tv_ln_b):
        import jax, jax.numpy as jnp
        import numpy as np
        B, S, D, F, E = (8, 512, 512, 256, 8)
        INIT_LAMBDA = 0.2
        LN_EPS = 1e-05
        LN_MERGE = 0.03
        x = hidden_states
        gh = jax.nn.relu(jnp.einsum('bsd,hd->bsh', x, gfc1_w) + gfc1_b)
        g = (jnp.einsum('bsh,eh->bse', gh, gfc2_w) + gfc2_b).mean(axis=1)
        W1m = W1 + jnp.einsum('be,efd->bfd', g, tv_W1)
        b1m = b1 + g @ tv_b1
        W2m = W2 + jnp.einsum('be,edf->bdf', g, tv_W2)
        b2m = b2 + g @ tv_b2
        lng = ln_g + LN_MERGE * (tv_ln_g - ln_g).sum(axis=0)
        lnb = ln_b + LN_MERGE * (tv_ln_b - ln_b).sum(axis=0)
        h = jax.nn.relu(jnp.einsum('bsd,bfd->bsf', x, W1m) + b1m[:, None, :])
        out = jnp.einsum('bsf,bdf->bsd', h, W2m) + b2m[:, None, :]
        res = x + out
        mu = res.mean(axis=-1, keepdims=True)
        var = res.var(axis=-1, keepdims=True)
        return (res - mu) * jax.lax.rsqrt(var + LN_EPS) * lng + lnb
    xn = _layernorm(x, axis=-1)
    x = x + _L0_gnn_ref(xn, edge_weight, L0_gnn_weight, L0_gnn_bias, src, dst) + _L0_mix_ref(xn[None], L0_mix_Wq, L0_mix_bq, L0_mix_Wk, L0_mix_bk, L0_mix_Wv, L0_mix_bv, L0_mix_Wp, L0_mix_bp)[0]
    x = x + _L0_ffn_ref(_layernorm(x, axis=-1)[None], L0_ffn_gfc1_w, L0_ffn_gfc1_b, L0_ffn_gfc2_w, L0_ffn_gfc2_b, L0_ffn_W1, L0_ffn_b1, L0_ffn_W2, L0_ffn_b2, L0_ffn_ln_g, L0_ffn_ln_b, L0_ffn_tv_W1, L0_ffn_tv_b1, L0_ffn_tv_W2, L0_ffn_tv_b2, L0_ffn_tv_ln_g, L0_ffn_tv_ln_b)[0]
    return x

_drawn_inputs = setup_inputs


def setup_inputs(seed=0):
    import zlib

    import numpy as np

    out = dict(_drawn_inputs(seed))
    spreads = {'L0_mix_bq': (0.0, 2.0),
     'L0_mix_bk': (0.0, 2.0),
     'L0_mix_bv': (0.0, 0.1),
     'L0_mix_bp': (0.0, 0.1),
     'L0_ffn_gfc1_b': (0.0, 0.8),
     'L0_ffn_gfc2_b': (0.20000000298023224, 0.6),
     'L0_ffn_b1': (0.0, 0.8),
     'L0_ffn_b2': (0.0, 0.8),
     'L0_ffn_ln_g': (1.0, 0.2),
     'L0_ffn_ln_b': (0.0, 0.1)}
    factors = {'L0_gnn_bias': 3.542,
     'L0_mix_Wq': 8.0,
     'L0_mix_Wk': 8.0,
     'L0_mix_Wv': 6.742,
     'L0_ffn_gfc1_w': 8.0,
     'L0_ffn_gfc2_w': 8.0,
     'L0_ffn_tv_W1': 2.978,
     'L0_ffn_tv_b1': 8.0,
     'L0_ffn_tv_b2': 8.0,
     'L0_ffn_tv_ln_g': 62.51,
     'L0_ffn_tv_ln_b': 64.0}
    for name, (base, spread) in spreads.items():
        noise = np.random.default_rng([zlib.crc32(name.encode()), seed]).standard_normal(out[name].shape)
        drawn = base * np.exp(spread * noise) if base else spread * noise
        out[name] = jnp.asarray(drawn.astype(out[name].dtype))
    for name, factor in factors.items():
        out[name] = (out[name] * factor).astype(out[name].dtype)
    return out
```

```python
from contextlib import ExitStack

import concourse.bass as bass
from concourse import mybir

F32 = mybir.dt.float32
F16 = mybir.dt.float16
BF16 = mybir.dt.bfloat16
I32 = mybir.dt.int32
ALU = mybir.AluOpType
ACT = mybir.ActivationFunctionType
AX_X = mybir.AxisListType.X
RMAX = bass.bass_isa.ReduceOp.max
RADD = bass.bass_isa.ReduceOp.add

P = 128
N, D = 6250, 512
E = 100000
C = D // P
T = -(-N // P)
LAST = N - (T - 1) * P
H = 8
HD = D // H
F = 256
FC = F // P
NE = 8
EG = 2 * P
NG = -(-E // EG)
GFULL = E // EG
SA, SB = 6, 3
S2 = SA * T
SC = -(-(SA + SB) * T // P)
SLOTS = 2 * SA
OHS = 3
BLOCKS = -(-NG * T // P)
DR, DW = 125, E // 125
OUTSIDE = float(1 << 20)
XS = 1024.0
EPS = 1e-5
LN_MERGE = 0.03
Q4 = 4
U = 2 * Q4
NQ = -(-T // Q4)
EXPONENT = 0x7F800000
PASSES = ((0, 0), (0, 1), (1, 0))


def at_least(eng, sem, n):
    if not isinstance(n, int) or n > 0:
        eng.wait_ge(sem, n)


def size_of(shape, dt):
    n = mybir.dt.size(dt)
    for s in shape[1:]:
        n *= s
    return -(-n // 32) * 32


def build(nc, x, src, dst, edge_weight, gnn_w, gnn_b, Wq, bq, Wk, bk, Wv, bv, Wp, bp,
          gfc1_w, gfc1_b, gfc2_w, gfc2_b, W1, b1, W2, b2, ln_g, ln_b,
          tv_W1, tv_b1, tv_W2, tv_b2, tv_ln_g, tv_ln_b, out):
    packed = nc.dram_tensor("packed", (NG, 3 * EG), I32, kind="Internal").ap()
    y_rows = nc.dram_tensor("y_rows", (T * P, 2 * D), F16, kind="Internal").ap()
    xn_rows = nc.dram_tensor("xn_rows", (T * P, D), F32, kind="Internal").ap()
    xt_rows = nc.dram_tensor("xt_rows", (T * P, 2 * D), F16, kind="Internal").ap()
    zt_rows = nc.dram_tensor("zt_rows", (T * P, 2 * D), F16, kind="Internal").ap()

    def row_tile(ap, t):
        return ap.rearrange("(t p) d -> t p d", p=P)[bass.ds(t, 1)].rearrange("a p d -> (a p) d")

    with ExitStack() as ctx:
        ctx.enter_context(nc.allow_non_contiguous_dma(reason="small columns: group starts, biases"))
        base, top = -(-nc.sbuf_base // 32) * 32, nc.sbuf_usable_end
        cursor = [base]

        def put(name, shape, dt):
            at = cursor[0]
            cursor[0] += size_of(shape, dt)
            assert cursor[0] <= top, (name, cursor[0], top)
            return nc.alloc_sbuf_tensor_at(name, shape, dt, offset=at)

        def over(at, *specs):
            made = []
            for name, shape, dt in specs:
                made.append(nc.alloc_sbuf_tensor_at(name, shape, dt, offset=at))
                at += size_of(shape, dt)
                assert at <= top, (name, at, top)
            return made if len(made) > 1 else made[0]

        def region(size):
            cursor[0] += size
            return cursor[0] - size

        sem = lambda name: ctx.enter_context(nc.semaphore(name))

        acc = put("acc", [P, T, D], F32)
        ident = put("ident", [P, P], F32)
        ident16 = put("ident16", [P, P], F16)
        iota16 = put("iota16", [P, P], F16)
        ones = put("ones", [P, P], F32)
        ones3 = put("ones3", [3, P], BF16)
        headmask = put("headmask", [P, P], F32)
        rs = put("rs", [P, T + Q4 - 1], F32)
        nb = put("nb", [P, T + Q4 - 1], F32)
        var4 = put("var4", [P, 2, Q4, 2], F32)
        st6 = put("st6", [P, Q4, 6], F32)
        sd4 = put("sd4", [P, Q4], F32)
        rsr = put("rsr", [P, 2, Q4], F32)
        nbr = put("nbr", [P, 2, Q4], F32)
        epsc = put("epsc", [P, 1], F32)
        minus1 = put("minus1", [P, 1], F32)
        valid = put("valid", [P, 1], F32)
        mx = put("mx", [P, 8], F32)
        mxa = put("mxa", [P, 8], F32)
        pw = put("pw", [P, 8], I32)
        sc = put("sc", [P, 8], I32)
        inv = put("inv", [P, 8], I32)
        cols = put("cols", [P, 8], F32)
        stepi = put("stepi", [P, SC], I32)
        stepf = put("stepf", [P, SC], F32)
        cnt = put("cnt", [P, SC], F32)
        gidx = put("gidx", [P, SC], I32)
        ntile = put("ntile", [P, SC], F32)
        negd = put("negd", [P, SC], F32)
        late = put("late", [P, SC], F32)
        viol = put("viol", [P, 1], F32)
        uns = put("uns", [P, 1], F32)
        srt = put("srt", [P, 1], F32)
        flag = put("flag", [1, 1], I32)
        tileof = put("tileof", [1, SC * P], I32)
        krows = put("krows", [3, D], BF16)
        qrows = put("qrows", [3, D], BF16)
        mrows = put("mrows", [3, D], BF16)
        ksum = put("ksum", [P, C], F32)
        bvrow = put("bvrow", [1, D], F32)
        rA, rB, rQ, rV, rP = (region(4 * C * D) for _ in range(5))
        rTab, rIdx, rG = region(SC * P * 24), region(SC * P * 8), region(SLOTS * 4 * D)
        rW = cursor[0]
        Wg16 = over(rA, ("Wg16", [P, 2, C, D], F16))
        Wk16 = over(rB, ("Wk16", [P, 2, C, D], F16))
        Wq16 = over(rQ, ("Wq16", [P, 2, C, D], F16))
        Wv32 = over(rV, ("Wv32", [P, C, D], F32))
        Wp32 = over(rP, ("Wp32", [P, C, D], F32))
        M32 = over(rA, ("M32", [P, C, D], F32))
        MT32 = over(rB, ("MT32", [P, C, D], F32))
        KVP = over(rA, ("KVP", [P, C, D], F32))
        tab = over(rTab, ("tab", [P, SC * P, 2, 3], F32))
        idx = over(rIdx, ("idx", [P, SC * P, 2], I32))
        rows = over(rG, ("rows", [P, SLOTS, 2, D], F16))
        stage = over(rG, ("stage", [P, 3, C, D], F32))
        pk, srcf, rel, ok, wlo, whi = over(
            rV, ("pk", [P, 3, EG], I32), ("srcf", [P, EG], F32), ("rel", [P, EG], F32),
            ("ok", [P, EG], F32), ("wlo", [P, EG], F32), ("whi", [P, EG], F16))
        startb, pad = over(rP, ("startb", [P, NG], F32), ("pad", [1, 3, EG], I32))
        dsts, ews, junk = over(rTab, ("dsts", [P, DW + 1], I32), ("ews", [P, DW], F32), ("junk", [P, NG], F32))
        brow = over(rTab + 8000, ("brow", [1, 4, D], F32))
        srow, srowf, irow, bf, b16 = over(
            rW, ("srow", [1, NG], I32),
            ("srowf", [1, NG], F32), ("irow", [1, NG], I32), ("bf", [1, D], F32), ("b16", [1, 3, 3, D], BF16))
        xnb, xh, xl, xtb, yb = over(
            rW, ("xnb", [P, 2, D], F32), ("xh", [P, 2, D], F16), ("xl", [P, 2, D], F16),
            ("xtb", [P, 2, 2, C, P], F16), ("yb", [P, 2, 2, D], F16))
        xta, xna, kf, mb, oneh, idxc, tabc = over(
            rW, ("xta", [P, 2, 2, C, P], F16), ("xna", [P, 2, D], F32), ("kf", [P, 2, D], F32),
            ("mb", [P, D], F32), ("oneh", [P, OHS, 2, 2, P], F16),
            ("idxc", [P, 2, 2 * SA], I32), ("tabc", [P, 2, 2 * SA, 3], F32))
        kvt, krow = over(rW + 2 * 4 * D + 2 * 4 * D, ("kvt", [P, C, P], F32), ("krow", [1, D], F32))
        qz, rz, kden = over(rV, ("qz", [P, 2, D], F32), ("rz", [P, D], F32), ("kden", [P, C, P], F32))
        graw = over(rB, ("graw", [P, C, D], F32))
        tvW1 = over(rA, ("tvW1", [P, NE, FC, D], F32))
        xd, hT, zq, zr = over(
            rA, ("xd", [P, 2, Q4, 2, C, P], F16), ("hT", [P, 2, FC, D], F32), ("zq", [P, 2, D], F32),
            ("zr", [P, 2, D], F32))
        G16, ztg = over(rP, ("G16", [P, 2, C, D], F16), ("ztg", [P, 2, Q4, 2, C, P], F16))
        tvW2 = over(rP, ("tvW2", [P, NE, C, F], F32))
        res, ob = over(rP, ("res", [P, U, D], F32), ("ob", [P, 2, D], F32))
        rN = rP + 4 * NE * C * F
        zn, zh, zl = over(rN, ("zn", [P, 2, D], F32), ("zh", [P, 2, D], F16), ("zl", [P, 2, D], F16))
        W1m, W2m = over(rN, ("W1m", [P, 2, C, F], F16), ("W2m", [P, FC, D], F32))
        (W1raw, W2raw, lnrows, lbrows, g2raw, lngb, lnbb, lncoef, gjunk, gsum, gsq, gcol, gbias, g2T,
         gall, gT, gbr, gones, b1c, tvb1, b1m, tvb2, geye) = over(
            rN + 16 * D, ("W1raw", [P, FC, D], F32), ("W2raw", [P, C, F], F32),
            ("lnrows", [NE + 1, D], F32), ("lbrows", [NE + 1, D], F32), ("g2raw", [NE, D], F32),
            ("lngb", [P, D], F32), ("lnbb", [P, D], F32), ("lncoef", [NE + 1, P], F32), ("gjunk", [P, D], F16),
            ("gsum", [P, C, NQ], F32), ("gsq", [P, C], F32), ("gcol", [P, C], F32), ("gbias", [P, C], F32),
            ("g2T", [P, C, NE], F32), ("gall", [P, NE], F32), ("gT", [NE, 1], F32),
            ("gbr", [1, NE], F32), ("gones", [P, P], F32), ("b1c", [P, FC], F32), ("tvb1", [P, FC, NE], F32),
            ("b1m", [P, FC], F32), ("tvb2", [NE, D], F32), ("geye", [P, NE, P], F32))
        b2f, b216 = over(rN + 16 * D + 8 * F * 4 + 0, ("b2f", [1, D], F32), ("b216", [1, 3, D], BF16))
        b2rows, b2r = mrows, bvrow

        bank = [ctx.enter_context(nc.psum_tensor(f"bank{i}", [P, D], F32)) for i in range(8)]

        pool_set = sem("pool_set")
        consts_made = sem("consts_made")
        edges_loaded, start_loaded, bias_loaded = sem("edges_loaded"), sem("start_loaded"), sem("bias_loaded")
        w_loaded = [sem(f"w_loaded{k}") for k in range(3)]
        edges_packed, vp_loaded = sem("edges_packed"), sem("vp_loaded")
        x_loaded = [sem(f"x_loaded{j}") for j in range(Q4)]
        maxes_made, maxes_all = sem("maxes_made"), sem("maxes_all")
        scales_made, high_made, low_made = sem("scales_made"), sem("high_made"), sem("low_made")
        chain = sem("chain")
        start_made, start_spread = sem("start_made"), sem("start_spread")
        groups_made, tiles_turned = sem("groups_made"), sem("tiles_turned")
        bias_split, bias_spread = sem("bias_split"), sem("bias_spread")
        pk_ready, picked, turned, tabled = sem("pk_ready"), sem("picked"), sem("turned"), sem("tabled")

        class RowLoop:

            def __init__(self, name):
                self.vars_made = sem(name + "_vars_made")
                self.std_made = sem(name + "_std_made")
                self.scale_made = sem(name + "_scale_made")
                self.normed = sem(name + "_normed")
                self.high = sem(name + "_high")
                self.low = sem(name + "_low")
                self.turned = sem(name + "_turned")
                self.high_out = sem(name + "_high_out")
                self.low_out = sem(name + "_low_out")
                self.rows_kept = [sem(f"{name}_rows_kept{b}") for b in range(2)] if name == "head" else None
                self.turned_kept = [sem(f"{name}_turned_kept{b}") for b in range(2)]

                self.six = sem(name + "_six")
                self.rec = sem(name + "_rec")

        head, tail = RowLoop("head"), RowLoop("tail")
        y_made, y_high, y_low = sem("y_made"), sem("y_high"), sem("y_low")
        y_kept = [sem(f"y_kept{b}") for b in range(2)]
        copied = sem("copied")
        gathered = [sem(f"gathered{q}") for q in range(SLOTS)]
        onehot, stepped, edge_added = sem("onehot"), sem("stepped"), sem("edge_added")
        xt_in = [sem(f"xt_in{b}") for b in range(2)]
        xn_in = [sem(f"xn_in{b}") for b in range(2)]
        f_done, f_min, f_exp, f_used, m_done = (sem(n) for n in ("f_done", "f_min", "f_exp", "f_used", "m_done"))
        m_out, m_turned, mt_out = (sem(n) for n in ("m_out", "m_turned", "mt_out"))
        kv_done, kv_out, kvp_done, kvp_out = (sem(n) for n in ("kv_done", "kv_out", "kvp_done", "kvp_out"))
        den_done, rz_made, qz_made, mix_done, mix_added = (sem(n) for n in (
            "den_done", "rz_made", "qz_made", "mix_done", "mix_added"))
        graw_loaded = sem("graw_loaded")
        u_chain, u_group, u_pk, u_picked, u_turned, u_index, u_gathered, u_onehot, u_stepped, u_added = (
            sem(n) for n in ("u_chain", "u_group", "u_pk", "u_picked", "u_turned", "u_index", "u_gathered",
                             "u_onehot", "u_stepped", "u_added"))
        edges_done, u_start = sem("edges_done"), sem("u_start")
        small_loaded, tv1_loaded, tv2_loaded = sem("small_loaded"), sem("tv1_loaded"), sem("tv2_loaded")
        ln_coefs, g2_turned, g2_out, gate_in = sem("ln_coefs"), sem("g2_turned"), sem("g2_out"), sem("gate_in")
        graw_turned = sem("graw_turned")
        ln_done, ln_out = sem("ln_done"), sem("ln_out")
        gf_done, gf_out = sem("gf_done"), sem("gf_out")
        gate_done, gate_out, b2_done = sem("gate_done"), sem("gate_out"), sem("b2_done")
        w1_done, w2_done, w2_out = sem("w1_done"), sem("w2_done"), sem("w2_out")
        zd_in = [sem(f"zd_in{b}") for b in range(2)]
        h_done, h_out, o_done, zq_made, res_made, six_made, two_made, r_std, r_rec, r_scale = (sem(n) for n in (
            "h_done", "h_out", "o_done", "zq_made", "res_made", "six_made", "two_made", "r_std", "r_rec", "r_scale"))
        zr_made, gained, based, ob_made = sem("zr_made"), sem("gained"), sem("based"), sem("ob_made")
        out_kept = [sem(f"out_kept{b}") for b in range(2)]

        block = ctx.enter_context(nc.Block())
        flat = lambda ap, t: ap[:, bass.ds(t, 1), :].rearrange("p a d -> p (a d)")

        def back(g, j, n):
            return g + (j - n) // U, (j - n) % U

        def tile_at(g, j):
            return U * g + j

        def half_at(g, j):
            return U // 2 * g + j // 2

        def quad_at(g, j):
            return 2 * g + j // Q4

        def row_ticks(eng, tick, last):
            for j in range(U):
                tick(0, j)
            with eng.Fori(1, T // U - 1) as g:
                for j in range(U):
                    tick(g, j)
            for t in range((T // U - 1) * U, last):
                tick(t // U, t % U)

        def exists(g, j):
            return not isinstance(g, int) or 0 <= tile_at(g, j) < T

        def first_tiles(eng, tile):
            tile(0, 0, 0)
            tile(1, 0, 1)
            with eng.Fori(1, T // 2) as h:
                tile(2 * h, h, 0)
                tile(2 * h + 1, h, 1)
            tile(T - 1, T // 2, (T - 1) % 2)

        def second_tiles(eng, tile):
            for t in range(5):
                tile(t, t // 2, t % 2)
            with eng.Fori(1, (T - 1) // 4) as g:
                for j in range(1, 5):
                    tile(4 * g + j, 2 * g + j // 2, j % 2)

        def head_kept(eng):
            for b in range(2):
                n = 16 * ((T + 1 - b) // 2)
                eng.wait_ge(head.rows_kept[b], n)
                eng.wait_ge(head.turned_kept[b], n)
                eng.wait_ge(y_kept[b], n)

        def gate_at(g, j):
            m = (j - 1) % Q4
            return 2 * g + (j - Q4 - 1 - m) // Q4, m

        def gate_exists(g, j):
            return not isinstance(g, int) or 0 <= gate_at(g, j)[0] < NQ

        def free_group(eng, g, j):
            at_least(eng, tail.turned_kept[j % 2], 16 * (half_at(g, j) - Q4 + 2))
            if j % Q4 == 0:
                at_least(eng, gf_done, C * (quad_at(g, j) - 1))

        def waited(eng):
            eng.nop(nofuse=True)

        turned16 = [[bank[6 * part + b][:, 0:D // 2].bitcast(F16).rearrange("p (c m) -> p c m", c=C)
                     for part in range(2)] for b in range(2)]
        scf, invf = sc[:, :].bitcast(F32), inv[:, :].bitcast(F32)
        by_half = lambda ap: ap.rearrange("p (j s) -> p j s", j=2)

        @block.sync
        def _(sp):
            flat_dst = dst.rearrange("(a n) -> a n", a=1)
            by_row = dst.rearrange("(p w) -> p w", w=DW)
            sp.dma_start(dsts[0:DR, 0:DW], by_row).then_inc(edges_loaded, 16)
            sp.dma_start(dsts[0:DR - 1, DW:DW + 1], by_row[1:DR, 0:1]).then_inc(edges_loaded, 16)
            sp.dma_start(dsts[DR - 1:DR, DW:DW + 1], flat_dst[:, E - 1:E]).then_inc(edges_loaded, 16)
            sp.dma_start(ews[0:DR, :], edge_weight.rearrange("(p w) -> p w", w=DW)).then_inc(edges_loaded, 16)
            for k, w in enumerate((gnn_w, Wk, Wq)):
                sp.dma_start(stage[:, k], w.rearrange("(c p) n -> p c n", p=P)).then_inc(w_loaded[k], 16)
            sp.dma_start(srow[:, :], flat_dst[:, 0:E:EG]).then_inc(start_loaded, 16)
            for r, b in enumerate((bk, bq, bp, gnn_b)):
                sp.dma_start(brow[:, r, :], b.rearrange("(a n) -> a n", a=1)).then_inc(bias_loaded, 16)
            sp.dma_start(bvrow[:, :], bv.rearrange("(a n) -> a n", a=1)).then_inc(bias_loaded, 16)

            def load_x(g, j):
                t = Q4 * g + j
                at_least(sp, x_loaded[j], 16 * g)
                sp.dma_start(flat(acc, t), row_tile(x[0:(T - 1) * P, :], t)).then_inc(x_loaded[j], 16)

            for j in range(Q4):
                load_x(0, j)
            with sp.Fori(1, (T - 1) // Q4) as g:
                for j in range(Q4):
                    load_x(g, j)
            sp.wait_ge(consts_made, 1)
            sp.dma_start(acc[0:LAST, T - 1, :], x[(T - 1) * P:N, :]).then_inc(x_loaded[0], 16)

            sp.wait_ge(bias_split, 3)
            for r, dest in enumerate((krows, qrows, mrows)):
                for part in range(3):
                    sp.dma_start(dest[part:part + 1, :], b16[:, r, part, :]).then_inc(bias_spread, 16)
            sp.wait_ge(tabled, SC)
            sp.dma_start(Wv32[:, :, :], Wv.rearrange("(c p) n -> p c n", p=P)).then_inc(vp_loaded, 16)
            sp.dma_start(Wp32[:, :, :], Wp.rearrange("(c p) n -> p c n", p=P)).then_inc(vp_loaded, 16)

            def head_stores(g, j):
                b = j % 2
                if exists(g, j):
                    t = tile_at(g, j)
                    sp.wait_ge(head.normed, t + 1)
                    sp.dma_start(row_tile(xn_rows, t), xnb[:, b, :]).then_inc(head.rows_kept[b], 16)
                g1, j1 = back(g, j, 1)
                if exists(g1, j1):
                    t, b1 = tile_at(g1, j1), 1 - b
                    sp.wait_ge(head.high_out, t + 1)
                    sp.wait_ge(head.low_out, t + 1)
                    sp.dma_start(row_tile(xt_rows, t), xtb[:, b1].rearrange("p a c m -> p (a c m)")
                                 ).then_inc(head.turned_kept[b1], 16)
                g2, j2 = back(g, j, 2)
                if exists(g2, j2):
                    t = tile_at(g2, j2)
                    sp.wait_ge(y_high, t + 1)
                    sp.wait_ge(y_low, t + 1)
                    sp.dma_start(row_tile(y_rows, t), yb[:, b].rearrange("p a d -> p (a d)")
                                 ).then_inc(y_kept[b], 16)

            row_ticks(sp, head_stores, T + 2)
            head_kept(sp)
            sp.wait_ge(head.turned, T)

            def first_loads(t, h, b):
                at_least(sp, f_done, t - 1)
                sp.dma_start(xta[:, b].rearrange("p a c m -> p (a c m)"), row_tile(xt_rows, t)
                             ).then_inc(xt_in[b], 16)
                at_least(sp, m_done, t - 1)
                sp.dma_start(xna[:, b, :], row_tile(xn_rows, t)).then_inc(xn_in[b], 16)

            first_tiles(sp, first_loads)
            sp.wait_ge(kv_done, 1)
            sp.dma_start(graw[:, :, :], gfc1_w.rearrange("(c p) n -> p c n", p=P)).then_inc(graw_loaded, 16)

            def second_loads(t, h, b):
                if isinstance(t, int) and t < 2:
                    sp.wait_ge(f_done, T)
                else:
                    sp.wait_ge(f_done, T + t - 1)
                sp.dma_start(xta[:, b].rearrange("p a c m -> p (a c m)"), row_tile(xt_rows, t)
                             ).then_inc(xt_in[b], 16)

            second_tiles(sp, second_loads)

            sp.wait_ge(edges_done, 1)
            one = lambda ap: ap.rearrange("(a n) -> a n", a=1)
            for dest, source in (
                    (lnrows[0:1, :], one(ln_g)), (lnrows[1:NE + 1, :], tv_ln_g),
                    (lbrows[0:1, :], one(ln_b)), (lbrows[1:NE + 1, :], tv_ln_b),
                    (g2raw[:, :], gfc2_w), (gbr[:, :], one(gfc2_b)), (gbias[:, :], gfc1_b.rearrange("(c p) -> p c", p=P)),
                    (tvb2[:, :], tv_b2), (b2r[:, :], one(b2)), (b1c[:, :], b1.rearrange("(c p) -> p c", p=P)),
                    (W1raw[:, :, :], W1.rearrange("(c p) d -> p c d", p=P)),
                    (W2raw[:, :, :], W2.rearrange("(c p) f -> p c f", p=P))):
                sp.dma_start(dest, source).then_inc(small_loaded, 16)
            for c in range(FC):
                sp.dma_start(tvb1[:, c, :], tv_b1[:, c * P:(c + 1) * P].rearrange("e p -> p e")
                             ).then_inc(small_loaded, 16)
            sp.wait_ge(graw_turned, 1)
            sp.wait_ge(maxes_made, 2)
            for e in range(NE):
                sp.dma_start(tvW1[:, e], tv_W1[e].rearrange("(c p) d -> p c d", p=P)).then_inc(tv1_loaded, 16)

            def tail_stores(g, j):
                g1, j1 = back(g, j, 1)
                if exists(g1, j1):
                    t, b1 = tile_at(g1, j1), j1 % 2
                    sp.wait_ge(tail.high_out, t + 1)
                    sp.wait_ge(tail.low_out, t + 1)
                    at_least(sp, tail.turned_kept[b1], 16 * half_at(g1, j1))
                    sp.dma_start(row_tile(zt_rows, t), ztg[:, j1 // Q4, j1 % Q4].rearrange("p a c m -> p (a c m)")
                                 ).then_inc(tail.turned_kept[b1], 16)

            row_ticks(sp, tail_stores, T + 1)
            for b in range(2):
                sp.wait_ge(tail.turned_kept[b], 16 * ((T + 1 - b) // 2))
            sp.wait_ge(gf_done, C * NQ)
            for e in range(NE):
                sp.dma_start(tvW2[:, e], tv_W2[e].rearrange("(c p) f -> p c f", p=P)).then_inc(tv2_loaded, 16)
            sp.wait_ge(w1_done, 1)

            def load_zd(q, b, n):
                sp.dma_start(xd[:, b, 0:n].rearrange("p t a c m -> p t (a c m)"),
                             zt_rows.rearrange("(t p) d -> p t d", p=P)[:, bass.ds(Q4 * q, n), :]
                             ).then_inc(zd_in[b], 16)

            load_zd(0, 0, Q4)
            load_zd(1, 1, Q4)
            sp.wait_ge(bias_split, 4)
            for part in range(3):
                sp.dma_start(b2rows[part:part + 1, :], b216[:, part, :]).then_inc(bias_spread, 16)

            def out_stores(g, j):
                q = quad_at(g, j)
                if j % Q4 == 0 and not (isinstance(q, int) and q + 2 >= NQ):
                    sp.wait_ge(h_done, FC * (q + 1))
                    load_zd(q + 2, j // Q4, 1 if isinstance(q, int) and q + 2 == NQ - 1 else Q4)
                g4, j4 = back(g, j, Q4)
                if exists(g4, j4):
                    t, b = tile_at(g4, j4), j4 % 2
                    sp.wait_ge(ob_made, t + 1)
                    if isinstance(t, int) and t == T - 1:
                        sp.dma_start(out[t * P:N, :], ob[0:LAST, b, :]).then_inc(out_kept[b], 16)
                    else:
                        sp.dma_start(row_tile(out[0:(T - 1) * P, :], t), ob[:, b, :]).then_inc(out_kept[b], 16)

            row_ticks(sp, out_stores, T + Q4)
            for b in range(2):
                sp.wait_ge(out_kept[b], 16 * ((T + 1 - b) // 2))

        @block.scalar
        def _(act):
            for i, a in enumerate((src, dst, edge_weight.bitcast(I32))):
                act.dma_start(packed[0:GFULL, i * EG:(i + 1) * EG],
                              a[0:GFULL * EG].rearrange("(g e) -> g e", e=EG)).then_inc(edges_packed, 16)
                act.dma_start(packed[GFULL:NG, i * EG:i * EG + E - GFULL * EG],
                              a[GFULL * EG:E].rearrange("(g e) -> g e", g=1)).then_inc(edges_packed, 16)
            act.wait_ge(consts_made, 1)
            act.dma_start(packed[GFULL:NG, :].rearrange("g (i e) -> g i e", i=3)[:, :, E - GFULL * EG:EG],
                          pad[:, :, 0:NG * EG - E]).then_inc(edges_packed, 16)
            for k, w16 in enumerate((Wg16, Wk16, Wq16)):
                act.wait_ge(scales_made, 1)
                nc.scalar.activation(w16[:, 0], stage[:, k], ACT.Copy, scale=scf[:, k:k + 1]).then_inc(high_made, 1)

            def deviations(loop, quad, par, n):
                act.wait_ge(loop.vars_made, quad + 1)
                at_least(act, loop.rec, 2 * quad)
                nc.scalar.activation(sd4[:, 0:n], var4[:, par, 0:n, 1], ACT.Sqrt, bias=epsc[:, :]
                                     ).then_inc(loop.std_made, 1)

            def normalise(loop, g, j, dest):
                t, b = tile_at(g, j), j % 2
                act.wait_ge(loop.scale_made, quad_at(g, j) + 1)
                at_least(act, loop.high, t - 1)
                at_least(act, loop.low, t - 1)
                if loop is head:
                    at_least(act, loop.rows_kept[b], 16 * half_at(g, j))
                waited(act)
                nc.scalar.activation(dest[:, b, :], flat(acc, t), ACT.Identity, scale=rs[:, bass.ds(t, 1)],
                                     bias=nb[:, bass.ds(t, 1)]).then_inc(loop.normed, 1)
                quad = quad_at(g, j)
                if j % Q4 == 1 and not (isinstance(quad, int) and quad + 1 >= NQ):
                    n = 1 if isinstance(quad, int) and quad + 1 == NQ - 1 else Q4
                    deviations(loop, quad + 1, (j // Q4 + 1) % 2, n)

            def head_tick(g, j):
                if exists(g, j):
                    normalise(head, g, j, xnb)
                g1, j1 = back(g, j, 1)
                if exists(g1, j1):
                    t, b = tile_at(g1, j1), j1 % 2
                    act.wait_ge(head.turned, t + 1)
                    at_least(act, y_made, t - 1)
                    at_least(act, head.turned_kept[b], 16 * half_at(g1, j1))
                    nc.scalar.copy(xtb[:, b, 1], turned16[b][1]).then_inc(head.low_out, 1)
                g2, j2 = back(g, j, 2)
                if exists(g2, j2):
                    t, b = tile_at(g2, j2), j2 % 2
                    act.wait_ge(y_made, t + 1)
                    at_least(act, y_kept[b], 16 * half_at(g2, j2))
                    nc.scalar.activation(yb[:, b, 0, :], bank[2 + b][:, :], ACT.Copy, scale=cols[:, 0:1]
                                         ).then_inc(y_high, 1)

            deviations(head, 0, 0, Q4)
            row_ticks(act, head_tick, T + 2)

            def copy_columns(first, n, b, after):
                at_least(act, stepped, after)
                waited(act)
                nc.scalar.copy(idxc[:, b, 0:2 * n], idx[:, bass.ds(first, n), :].rearrange("p s j -> p (s j)")
                               ).then_inc(copied, 1)
                nc.scalar.copy(tabc[:, b, 0:2 * n, :], tab[:, bass.ds(first, n)].rearrange("p s j k -> p (s j) k")
                               ).then_inc(copied, 1)

            act.wait_ge(tabled, SC)
            copy_columns(0, SA, 0, 0)

            def first_act(t, h, b):
                if isinstance(t, int) and t == T - 1:
                    copy_columns(S2, SB, 1 - b, SA * t)
                else:
                    copy_columns(SA * (t + 1), SA, 1 - b, SA * t)
                act.wait_ge(f_min, t + 1)
                nc.scalar.activation(mb[:, :], mb[:, :], ACT.Exp, bias=minus1[:, :]).then_inc(f_exp, 1)

            first_tiles(act, first_act)
            act.wait_ge(m_done, T)
            for c in (1, 3):
                nc.scalar.activation(M32[:, c, :], bank[c][:, :], ACT.Copy, scale=1.0 / XS).then_inc(m_out, 1)
            act.wait_ge(m_turned, 1)
            for c in (1, 3):
                nc.scalar.copy(MT32[:, c, :], bank[c][:, :]).then_inc(mt_out, 1)
            act.wait_ge(kvp_done, 1)
            for c in (1, 3):
                nc.scalar.copy(KVP[:, c, :], bank[c][:, :]).then_inc(kvp_out, 1)

            def second_act(t, h, b):
                if not (isinstance(t, int) and t == T - 1):
                    copy_columns(S2 + SB * (t + 1), SB, b, S2 + SB * t)
                act.wait_ge(f_min, T + t + 1)
                nc.scalar.activation(mb[:, :], mb[:, :], ACT.Exp, bias=minus1[:, :]).then_inc(f_exp, 1)

            second_tiles(act, second_act)

            act.wait_ge(edges_done, 1)
            act.wait_ge(scales_made, 2)
            act.wait_ge(graw_turned, 1)
            for f in range(C):
                nc.scalar.activation(G16[:, 0, f, :], bank[2 + f][:, :], ACT.Copy, scale=scf[:, 0:1]
                                     ).then_inc(high_made, 1)

            def tail_tick(g, j):
                if exists(g, j):
                    normalise(tail, g, j, zn)
                g1, j1 = back(g, j, 1)
                if exists(g1, j1):
                    t, b = tile_at(g1, j1), j1 % 2
                    act.wait_ge(tail.turned, t + 1)
                    free_group(act, g1, j1)
                    nc.scalar.copy(ztg[:, j1 // Q4, j1 % Q4, 1], turned16[b][1]).then_inc(tail.low_out, 1)
                if gate_exists(g1, j1):
                    q, m = gate_at(g1, j1)
                    act.wait_ge(gf_done, C * q + m + 1)
                    at_least(act, gf_out, C * q + m)
                    waited(act)
                    n = LAST if isinstance(q, int) and q == NQ - 1 else D
                    nc.scalar.activation(gjunk[:, 0:n], bank[2 + m][:, 0:n], ACT.Relu, scale=cols[:, 0:1],
                                         bias=gbias[:, m:m + 1], accum_out=gsum[:, m, bass.ds(q, 1)]
                                         ).then_inc(gf_out, 1)

            act.wait_ge(small_loaded, 16 * 14)
            deviations(tail, 0, 0, Q4)
            row_ticks(act, tail_tick, Q4 * NQ + 6)
            act.wait_ge(scales_made, 3)
            for f in range(C):
                nc.scalar.activation(W1m[:, 0, f, :], bank[2 + f // 2][:, (f % 2) * F:(f % 2 + 1) * F], ACT.Copy,
                                     scale=scf[:, 1:2]).then_inc(high_made, 1)

            def hidden(q, par, n):
                for o in range(FC):
                    act.wait_ge(h_done, FC * q + o + 1)
                    if not (isinstance(q, int) and q < 2):
                        act.wait_ge(o_done, Q4 * (q - 1))
                    nc.scalar.activation(hT[:, par, o, 0:n], bank[2 + o][:, 0:n], ACT.Relu, scale=cols[:, 1:2],
                                         bias=b1m[:, o:o + 1]).then_inc(h_out, 1)

            def out_tick(g, j):
                quad = quad_at(g, j)
                if exists(g, j):
                    t, b = tile_at(g, j), j % 2
                    at_least(act, res_made, t - 1)
                    waited(act)
                    nc.scalar.activation(zq[:, b, :], flat(acc, t), ACT.Identity, scale=rs[:, bass.ds(t, 1)],
                                         bias=nb[:, bass.ds(t, 1)]).then_inc(zq_made, 1)
                if j % Q4 == 0 and not (isinstance(quad, int) and quad == 0):
                    n = 1 if isinstance(quad, int) and quad == NQ else Q4
                    act.wait_ge(two_made, quad)
                    at_least(act, r_rec, quad - 1)
                    nc.scalar.activation(sd4[:, 0:n], var4[:, (j // Q4 + 1) % 2, 0:n, 1], ACT.Sqrt, bias=epsc[:, :]
                                         ).then_inc(r_std, 1)
                if j % Q4 == 1 and not (isinstance(quad, int) and quad + 1 >= NQ):
                    hidden(quad + 1, (j // Q4 + 1) % 2, P if isinstance(quad, int) and quad + 1 == NQ - 1 else Q4 * P)
                g4, j4 = back(g, j, Q4)
                if exists(g4, j4):
                    t, b = tile_at(g4, j4), j4 % 2
                    act.wait_ge(r_scale, quad_at(g4, j4) + 1)
                    at_least(act, ob_made, t - 1)
                    nc.scalar.activation(zr[:, b, :], res[:, j4, :], ACT.Identity, scale=rsr[:, j4 // Q4, j4 % Q4:j4 % Q4 + 1],
                                         bias=nbr[:, j4 // Q4, j4 % Q4:j4 % Q4 + 1]).then_inc(zr_made, 1)

            act.wait_ge(bias_split, 4)
            hidden(0, 0, Q4 * P)
            row_ticks(act, out_tick, T + Q4)

        @block.gpsimd
        def _(pool):
            pool.memset(ident[:, :], 0.0).then_inc(pool_set, 1)
            pool.memset(ident16[:, :], 0.0).then_inc(pool_set, 1)
            pool.memset(ones[:, :], 1.0).then_inc(pool_set, 1)
            pool.memset(ones3[:, :], 1.0).then_inc(pool_set, 1)
            pool.memset(headmask[:, :], 0.0).then_inc(pool_set, 1)
            pool.memset(epsc[:, :], EPS).then_inc(pool_set, 1)
            pool.memset(minus1[:, :], -1.0).then_inc(pool_set, 1)
            pool.memset(acc[:, T - 1, :], 0.0).then_inc(pool_set, 1)
            pool.memset(pad[:, 0, :], 0).then_inc(pool_set, 1)
            pool.memset(pad[:, 1, :], int(OUTSIDE)).then_inc(pool_set, 1)
            pool.memset(pad[:, 2, :], 0).then_inc(pool_set, 1)
            pool.memset(valid[:, :], 1.0).then_inc(pool_set, 1)
            pool.iota(stepi[:, :], pattern=[[P, SC]], base=0, channel_multiplier=1).then_inc(pool_set, 1)
            pool.iota(iota16[:, :], pattern=[[1, P]], base=0, channel_multiplier=0,
                      allow_small_or_imprecise_dtypes=True).then_inc(pool_set, 1)
            pool.iota(irow[:, :], pattern=[[1, NG]], base=0, channel_multiplier=0).then_inc(pool_set, 1)
            pool.wait_ge(pool_set, 15)
            for m in (ident, ident16):
                pool.affine_select(out=m[:, :], in_=m[:, :], compare_op=ALU.not_equal, fill=1.0, base=0,
                                   pattern=[[-1, P]], channel_multiplier=1).then_inc(pool_set, 1)
            pool.affine_select(out=valid[:, :], in_=valid[:, :], compare_op=ALU.is_ge, fill=0.0, base=LAST - 1,
                               pattern=[[0, 1]], channel_multiplier=-1).then_inc(pool_set, 1)
            pool.wait_ge(pool_set, 18)
            for b in range(2):
                pool.memset(headmask[b * HD:(b + 1) * HD, b * HD:(b + 1) * HD], 1.0).then_inc(pool_set, 1)
            pool.wait_ge(pool_set, 20)
            pool.nop(nofuse=True).then_inc(consts_made, 1)

            pool.wait_ge(maxes_made, 1)
            pool.partition_all_reduce(mxa[:, 0:4], mx[:, 0:4], P, RMAX).then_inc(maxes_all, 1)
            pool.partition_all_reduce(uns[:, :], viol[:, :], P, RADD).then_inc(maxes_all, 1)

            pool.wait_ge(groups_made, 1)
            pool.wait_ge(edges_packed, 16 * 7)
            for n in range(SC):
                at_least(pool, turned, n)
                at_least(pool, picked, n)
                pool.indirect_dma_start(out=pk[:, :, :].rearrange("p i e -> p (i e)"), out_offset=None, in_=packed,
                                        in_offset=bass.IndirectOffsetOnAxis(ap=gidx[:, n:n + 1], axis=0)
                                        ).then_inc(pk_ready, 16)

            def high_parts(loop, rowbuf, dest):
                def tick(g, j):
                    if exists(g, j):
                        t, b = tile_at(g, j), j % 2
                        pool.wait_ge(loop.normed, t + 1)
                        at_least(pool, loop.turned, t - 1)
                        at_least(pool, loop.low, t - 1)
                        waited(pool)
                        pool.tensor_copy(dest[:, b, :], rowbuf[:, b, :]).then_inc(loop.high, 1)
                return tick

            row_ticks(pool, high_parts(head, xnb, xh), T)

            pool.wait_ge(high_made, 3)
            pool.wait_ge(low_made, 3)
            pool.memset(rows[:, :, :, :], 0.0).then_inc(pool_set, 1)
            pool.wait_ge(pool_set, 21)
            head_kept(pool)
            limit = pool.to_reg(T * P - 1)

            def gather(slot, column):
                waited(pool)
                pool.indirect_dma_start(out=rows[:, slot].rearrange("p a d -> p (a d)"), out_offset=None, in_=y_rows,
                                        in_offset=bass.IndirectOffsetOnAxis(ap=column, axis=0),
                                        bounds_check=limit, oob_is_err=False).then_inc(gathered[slot], 16)

            def first_gathers(t, h, b):
                pool.wait_ge(copied, 2 * t + 1)
                for r in range(SA):
                    at_least(pool, stepped, SA * t + r - SA + 1)
                    for i in range(2):
                        gather(2 * r + i, idxc[:, b, 2 * r + i:2 * r + i + 1])

            def second_gathers(t, h, b):
                pool.wait_ge(copied, 2 * (T + t) + 1)
                for r in range(SB):
                    pool.wait_ge(stepped, S2 + SB * t + r - SA + 1)
                    for i in range(2):
                        gather(2 * (SB * b + r) + i, idxc[:, 1 - b, 2 * r + i:2 * r + i + 1])

            first_tiles(pool, first_gathers)
            second_tiles(pool, second_gathers)

            pool.wait_ge(edge_added, S2 + SB * T)
            unordered = pool.value_load(flag[0:1, 0:1], min_val=0, max_val=1)
            with pool.If(unordered > 0):
                with pool.Fori(0, NG) as n:
                    pool.wait_ge(u_group, n + 1)
                    waited(pool)
                    pool.indirect_dma_start(out=pk[:, :, :].rearrange("p i e -> p (i e)"), out_offset=None, in_=packed,
                                            in_offset=bass.IndirectOffsetOnAxis(ap=gidx[:, 0:1], axis=0)
                                            ).then_inc(u_pk, 16)
                    with pool.Fori(0, T) as d:
                        pool.wait_ge(u_index, T * n + d + 1)
                        waited(pool)
                        for i in range(2):
                            pool.indirect_dma_start(
                                out=rows[:, i].rearrange("p a d -> p (a d)"), out_offset=None, in_=y_rows,
                                in_offset=bass.IndirectOffsetOnAxis(ap=idxc[:, 0, i:i + 1], axis=0),
                                bounds_check=limit, oob_is_err=False).then_inc(u_gathered, 16)

            pool.wait_ge(maxes_made, 2)
            pool.partition_all_reduce(mxa[:, 0:1], mx[:, 0:1], P, RMAX).then_inc(maxes_all, 1)
            row_ticks(pool, high_parts(tail, zn, zh), T)
            pool.wait_ge(maxes_made, 3)
            pool.partition_all_reduce(mxa[:, 1:2], mx[:, 1:2], P, RMAX).then_inc(maxes_all, 1)

            def out_tick(g, j):
                if exists(g, j):
                    t = tile_at(g, j)
                    pool.wait_ge(zq_made, t + 1)
                    waited(pool)
                    pool.tensor_tensor(flat(acc, t), flat(acc, t), lnbb[:, :], ALU.add).then_inc(based, 1)
                g4, j4 = back(g, j, Q4)
                if exists(g4, j4):
                    t, b = tile_at(g4, j4), j4 % 2
                    pool.wait_ge(gained, t + 1)
                    pool.wait_ge(based, t + 1)
                    at_least(pool, out_kept[b], 16 * half_at(g4, j4))
                    waited(pool)
                    pool.tensor_tensor(ob[:, b, :], zr[:, b, :], flat(acc, t), ALU.add).then_inc(ob_made, 1)

            row_ticks(pool, out_tick, T + Q4)

        @block.vector
        def _(dve):
            links = [0]

            def link(ins):
                links[0] += 1
                ins.then_inc(chain, 1)
                dve.wait_ge(chain, links[0])

            def powers(first, n, link):
                s = slice(first, first + n)
                link(nc.vector.tensor_scalar(mxa[:, s], mxa[:, s], 1e-30, None, ALU.max))
                link(nc.vector.tensor_scalar(pw[:, s], mxa[:, s].bitcast(I32), EXPONENT, None, ALU.bitwise_and))
                link(nc.vector.tensor_scalar(sc[:, s], pw[:, s], -1.0, float(268 << 23), ALU.mult, ALU.add))
                link(nc.vector.tensor_scalar(inv[:, s], sc[:, s], -1.0, float(254 << 23), ALU.mult, ALU.add))

            def pick(gate, negtile, link, ready, count):
                dve.wait_ge(ready, count)
                link(nc.vector.tensor_scalar(rel[:, :], pk[:, 1, :], negtile, None, ALU.add))
                link(nc.vector.tensor_scalar(ok[:, :], rel[:, :], 0.0, gate, ALU.is_ge, ALU.mult))
                link(nc.vector.scalar_tensor_tensor(out=ok[:, :], in0=rel[:, :], scalar=float(P), in1=ok[:, :],
                                                    op0=ALU.is_lt, op1=ALU.mult))
                link(nc.vector.tensor_scalar(ok[:, :], ok[:, :], -OUTSIDE, OUTSIDE, ALU.mult, ALU.add))
                link(nc.vector.tensor_tensor(srcf[:, :], pk[:, 0, :], ok[:, :], ALU.add))
                link(nc.vector.tensor_tensor(rel[:, :], rel[:, :], ok[:, :], ALU.add))

            def tabulate(s, link):
                span = slice(s, s + P)
                link(nc.vector.tensor_copy(idx[:, span, :].rearrange("p s j -> p j s"), by_half(bank[4][:, 0:EG])))
                link(nc.vector.tensor_copy(tab[:, span, :, 0].rearrange("p s j -> p j s"), by_half(bank[4][:, EG:2 * EG])))
                link(nc.vector.tensor_scalar(whi[:, :], bank[5][:, 0:EG], scf[:, 3:4], None, ALU.mult))
                link(nc.vector.scalar_tensor_tensor(out=wlo[:, :], in0=bank[5][:, 0:EG], scalar=scf[:, 3:4],
                                                    in1=whi[:, :], op0=ALU.mult, op1=ALU.subtract))
                link(nc.vector.tensor_copy(tab[:, span, :, 1].rearrange("p s j -> p j s"), by_half(whi[:, :])))
                link(nc.vector.tensor_copy(tab[:, span, :, 2].rearrange("p s j -> p j s"), by_half(wlo[:, :])))

            link(nc.vector.memset(mx[:, :], 0.0))
            link(nc.vector.memset(viol[:, :], 0.0))
            for k in range(3):
                dve.wait_ge(w_loaded[k], 16)
                link(nc.vector.tensor_reduce(mx[:, k:k + 1], stage[:, k].rearrange("p c n -> p (c n)"), AX_X, ALU.max,
                                             apply_absolute_value=True))
            dve.wait_ge(edges_loaded, 64)
            link(nc.vector.tensor_reduce(mx[0:DR, 3:4], ews[0:DR, :], AX_X, ALU.max, apply_absolute_value=True))
            link(nc.vector.tensor_tensor(ews[0:DR, :], dsts[0:DR, 1:DW + 1], dsts[0:DR, 0:DW], ALU.is_lt))
            nc.vector.tensor_reduce(viol[0:DR, :], ews[0:DR, :], AX_X, ALU.add).then_inc(maxes_made, 1)

            dve.wait_ge(start_loaded, 16)
            dve.wait_ge(consts_made, 1)
            link(nc.vector.tensor_scalar(srow[:, :], srow[:, :], 7, None, ALU.logical_shift_right))
            link(nc.vector.tensor_copy(srowf[:, :], srow[:, :]))
            link(nc.vector.memset(srowf[:, 0:1], 0.0))
            nc.vector.tensor_tensor(srowf[:, :], srowf[:, :], irow[:, :], ALU.add).then_inc(start_made, 1)

            dve.wait_ge(maxes_all, 2)
            link(nc.vector.tensor_scalar(mxa[:, 4:5], mxa[:, 0:1], float(D), None, ALU.mult))
            powers(0, 5, link)
            scale = 1.0 / XS
            link(nc.vector.tensor_scalar(cols[:, 0:1], invf[:, 0:1], scf[:, 4:5], scale, ALU.mult, ALU.mult))
            link(nc.vector.tensor_scalar(cols[:, 1:3], invf[:, 1:3], scale, None, ALU.mult))
            link(nc.vector.tensor_tensor(cols[:, 3:4], invf[:, 3:4], invf[:, 4:5], ALU.mult))
            link(nc.vector.tensor_scalar(cols[:, 4:6], scf[:, 1:3], XS, None, ALU.mult))
            link(nc.vector.tensor_scalar(uns[:, :], uns[:, :], 1.0, None, ALU.min))
            link(nc.vector.tensor_scalar(srt[:, :], uns[:, :], -1.0, 1.0, ALU.mult, ALU.add))
            link(nc.vector.tensor_copy(flag[:, :], uns[0:1, :]))
            nc.vector.tensor_copy(stepf[:, :], stepi[:, :]).then_inc(scales_made, 1)

            dve.wait_ge(start_spread, 1)
            link(nc.vector.tensor_copy(startb[:, :], bank[4][:, 0:NG]))
            dve.wait_ge(scales_made, 1)
            for c in range(SC):
                link(nc.vector.tensor_scalar(junk[:, :], startb[:, :], stepf[:, c:c + 1], None, ALU.is_le, ALU.add,
                                             accum_out=cnt[:, c:c + 1]))
            link(nc.vector.tensor_tensor(ntile[:, :], stepf[:, :], cnt[:, :], ALU.subtract))
            link(nc.vector.tensor_scalar(ntile[:, :], ntile[:, :], 1.0, None, ALU.add))
            link(nc.vector.tensor_scalar(late[:, :], ntile[:, :], float(T - 1), -OUTSIDE, ALU.is_gt, ALU.mult))
            link(nc.vector.scalar_tensor_tensor(out=negd[:, :], in0=ntile[:, :], scalar=-float(P), in1=late[:, :],
                                                op0=ALU.mult, op1=ALU.add))
            link(nc.vector.tensor_scalar(ntile[:, :], ntile[:, :], float(T - 1), 0.0, ALU.min, ALU.max))
            nc.vector.tensor_scalar(gidx[:, :], cnt[:, :], -1.0, None, ALU.add).then_inc(groups_made, 1)
            dve.wait_ge(tiles_turned, 1)
            link(nc.vector.tensor_copy(tileof[:, :], bank[5][0:1, :]))

            for k, w16 in enumerate((Wg16, Wk16, Wq16)):
                dve.wait_ge(high_made, k + 1)
                nc.vector.scalar_tensor_tensor(out=w16[:, 1], in0=stage[:, k], scalar=scf[:, k:k + 1], in1=w16[:, 0],
                                               op0=ALU.mult, op1=ALU.subtract).then_inc(low_made, 1)

            def split(row, dest, link):
                link(nc.vector.tensor_copy(dest[:, 0, :], row[:, :]))
                link(nc.vector.tensor_tensor(row[:, :], row[:, :], dest[:, 0, :], ALU.subtract))
                link(nc.vector.tensor_copy(dest[:, 1, :], row[:, :]))
                link(nc.vector.tensor_tensor(row[:, :], row[:, :], dest[:, 1, :], ALU.subtract))
                return nc.vector.tensor_copy(dest[:, 2, :], row[:, :])

            dve.wait_ge(bias_loaded, 16 * 5)
            for r in range(3):
                if r < 2:
                    link(nc.vector.tensor_scalar(bf[:, :], brow[:, r, :], 1.0, cols[0:1, 4 + r:5 + r], ALU.add, ALU.mult))
                else:
                    link(nc.vector.tensor_tensor(bf[:, :], brow[:, 2, :], brow[:, 3, :], ALU.add))
                split(bf, b16[:, r], link).then_inc(bias_split, 1)
                dve.wait_ge(bias_split, r + 1)

            for n in range(SC):
                pick(srt[:, 0:1], negd[:, n:n + 1], link, pk_ready, 16 * (n + 1))
                dve.nop(nofuse=True).then_inc(picked, 1)
                dve.wait_ge(turned, n + 1)
                tabulate(n * P, link)
                dve.nop(nofuse=True).then_inc(tabled, 1)

            def statistics(loop, quad, par, n):
                at_least(dve, loop.vars_made, quad)
                for i in range(n):
                    if loop is head:
                        dve.wait_ge(x_loaded[i], 16 * (quad + 1))
                    waited(dve)
                    nc.vector.bn_stats(st6[:, i, :], flat(acc, Q4 * quad + i)).then_inc(loop.six, 1)
                dve.wait_ge(loop.six, Q4 * quad + n)
                waited(dve)
                for i in range(n):
                    ins = nc.vector.bn_aggr(var4[:, par, i, :], st6[:, i, :])
                ins.then_inc(loop.vars_made, 1)

            def scales(loop, quad, par, n):
                s = bass.ds(Q4 * quad, n)
                dve.wait_ge(loop.std_made, quad + 1)
                nc.vector.reciprocal(rs[:, s], sd4[:, 0:n]).then_inc(loop.rec, 1)
                dve.wait_ge(loop.rec, 2 * quad + 1)
                nc.vector.tensor_scalar(rs[:, s], rs[:, s], XS, None, ALU.mult).then_inc(loop.rec, 1)
                dve.wait_ge(loop.rec, 2 * quad + 2)
                nc.vector.scalar_tensor_tensor(out=nb[:, s], in0=var4[:, par, 0:n, 0], scalar=-1.0, in1=rs[:, s],
                                               op0=ALU.mult, op1=ALU.mult).then_inc(loop.scale_made, 1)

            def group_work(loop, g, j, what, at):
                quad = quad_at(g, j)
                if j % Q4 == at and not (isinstance(quad, int) and quad + 1 >= NQ):
                    what(loop, quad + 1, (j // Q4 + 1) % 2, 1 if isinstance(quad, int) and quad + 1 == NQ - 1 else Q4)

            def low_parts(loop, g, j, full, high, dest):
                t, b = tile_at(g, j), j % 2
                dve.wait_ge(loop.high, t + 1)
                at_least(dve, loop.turned, t - 1)
                nc.vector.tensor_tensor(dest[:, b, :], full[:, b, :], high[:, b, :], ALU.subtract).then_inc(loop.low, 1)

            def head_tick(g, j):
                group_work(head, g, j, statistics, 0)
                if exists(g, j):
                    low_parts(head, g, j, xnb, xh, xl)
                g1, j1 = back(g, j, 1)
                if exists(g1, j1):
                    t, b = tile_at(g1, j1), j1 % 2
                    dve.wait_ge(head.turned, t + 1)
                    at_least(dve, y_made, t - 1)
                    at_least(dve, head.turned_kept[b], 16 * half_at(g1, j1))
                    nc.vector.tensor_copy(xtb[:, b, 0], turned16[b][0]).then_inc(head.high_out, 1)
                group_work(head, g, j, scales, 2)
                g2, j2 = back(g, j, 2)
                if exists(g2, j2):
                    t, b = tile_at(g2, j2), j2 % 2
                    dve.wait_ge(y_high, t + 1)
                    at_least(dve, y_kept[b], 16 * half_at(g2, j2))
                    nc.vector.scalar_tensor_tensor(out=yb[:, b, 1, :], in0=bank[2 + b][:, :], scalar=cols[:, 0:1],
                                                   in1=yb[:, b, 0, :], op0=ALU.mult, op1=ALU.subtract
                                                   ).then_inc(y_low, 1)

            statistics(head, 0, 0, Q4)
            dve.wait_ge(bias_spread, 16 * 9)
            scales(head, 0, 0, Q4)
            row_ticks(dve, head_tick, T + 2)
            head_kept(dve)

            def hot(s, r, oslot, par):
                at_least(dve, stepped, s - OHS + 1)
                for i in range(2):
                    for part in range(2):
                        col = tabc[:, par, 2 * r + i]
                        ins = nc.vector.tensor_scalar(oneh[:, oslot, i, part, :], iota16[:, :], col[:, 0:1],
                                                      col[:, 1 + part:2 + part], ALU.is_equal, ALU.mult)
                ins.then_inc(onehot, 1)

            def add_step(s, ebank, mixed):
                tile = dve.value_load(tileof[0:1, bass.ds(s, 1)], min_val=0, max_val=T - 1)
                dve.wait_ge(stepped, s + 1)
                at_least(dve, edge_added, s)
                at_least(dve, mix_added, mixed)
                waited(dve)
                nc.vector.scalar_tensor_tensor(out=flat(acc, tile), in0=bank[ebank][:, :], scalar=cols[:, 3:4],
                                               in1=flat(acc, tile), op0=ALU.mult, op1=ALU.add).then_inc(edge_added, 1)

            def first_dve(t, h, b):
                s = lambda r: SA * t + r
                dve.wait_ge(copied, 2 * t + 2)
                hot(s(0), 0, 0, b)
                hot(s(1), 1, 1, b)
                dve.wait_ge(f_done, t + 1)
                at_least(dve, f_used, t)
                nc.vector.tensor_scalar(mb[:, :], bank[4][:, :], cols[:, 1:2], 1.0, ALU.mult, ALU.min).then_inc(f_min, 1)
                hot(s(2), 2, 2, b)
                add_step(s(0), 6, 0)
                dve.wait_ge(f_exp, t + 1)
                at_least(dve, m_done, t - 1)
                nc.vector.scalar_tensor_tensor(out=kf[:, b, :], in0=bank[4][:, :], scalar=cols[:, 1:2], in1=mb[:, :],
                                               op0=ALU.mult, op1=ALU.max).then_inc(f_used, 1)
                hot(s(3), 3, 0, b)
                add_step(s(1), 7, 0)
                hot(s(4), 4, 1, b)
                add_step(s(2), 6, 0)
                hot(s(5), 5, 2, b)
                for r in (3, 4, 5):
                    add_step(s(r), 6 + r % 2, 0)

            first_tiles(dve, first_dve)

            dve.wait_ge(m_done, T)
            for c in (0, 2):
                nc.vector.tensor_scalar(M32[:, c, :], bank[c][:, :], 1.0 / XS, None, ALU.mult).then_inc(m_out, 1)
            nc.vector.tensor_copy(ksum[:, :], bank[5][:, 0:C]).then_inc(m_out, 1)
            dve.wait_ge(m_turned, 1)
            for c in (0, 2):
                nc.vector.tensor_copy(MT32[:, c, :], bank[c][:, :]).then_inc(mt_out, 1)
            nc.vector.tensor_copy(krow[:, :], bank[5][0:1, :]).then_inc(mt_out, 1)
            dve.wait_ge(kv_done, 1)
            for c in range(C):
                nc.vector.tensor_tensor(kvt[:, c, :], bank[4][:, c * P:(c + 1) * P], headmask[:, :], ALU.mult
                                        ).then_inc(kv_out, 1)
            dve.wait_ge(m_out, C + 1)
            for c in range(C):
                nc.vector.tensor_scalar(kden[:, c, :], headmask[:, :], ksum[:, c:c + 1], None, ALU.mult
                                        ).then_inc(kv_out, 1)
            dve.wait_ge(kvp_done, 1)
            for c in (0, 2):
                nc.vector.tensor_copy(KVP[:, c, :], bank[c][:, :]).then_inc(kvp_out, 1)

            def add_mix(t, b):
                dve.wait_ge(mix_done, t + 1)
                dve.wait_ge(edge_added, S2 + SB * (t + 1))
                waited(dve)
                nc.vector.tensor_tensor(flat(acc, t), bank[3 + b][:, :], flat(acc, t), ALU.add).then_inc(mix_added, 1)

            def second_dve(t, h, b):
                s = lambda r: S2 + SB * t + r
                dve.wait_ge(copied, 2 * (T + t) + 2)
                hot(s(0), 0, 0, 1 - b)
                dve.wait_ge(f_done, T + t + 1)
                dve.wait_ge(f_used, T + t)
                nc.vector.tensor_scalar(mb[:, :], bank[b][:, :], cols[:, 2:3], 1.0, ALU.mult, ALU.min).then_inc(f_min, 1)
                hot(s(1), 1, 1, 1 - b)
                if not (isinstance(t, int) and t == 0):
                    add_mix(t - 1, 1 - b)
                dve.wait_ge(f_exp, T + t + 1)
                at_least(dve, den_done, t - 1)
                nc.vector.scalar_tensor_tensor(out=kf[:, b, :], in0=bank[b][:, :], scalar=cols[:, 2:3], in1=mb[:, :],
                                               op0=ALU.mult, op1=ALU.max).then_inc(f_used, 1)
                add_step(s(0), 6 + b, t)
                hot(s(2), 2, 2, 1 - b)
                add_step(s(1), 7 - b, t)
                dve.wait_ge(den_done, t + 1)
                at_least(dve, qz_made, t)
                nc.vector.reciprocal(rz[:, :], bank[2][:, :]).then_inc(rz_made, 1)
                dve.wait_ge(rz_made, t + 1)
                at_least(dve, mix_done, t - 1)
                nc.vector.tensor_tensor(qz[:, b, :], kf[:, b, :], rz[:, :], ALU.mult).then_inc(qz_made, 1)
                add_step(s(2), 6 + b, t)

            second_tiles(dve, second_dve)
            add_mix(T - 1, (T - 1) % 2)
            dve.wait_ge(mix_added, T)

            unordered = dve.value_load(flag[0:1, 0:1], min_val=0, max_val=1)
            with dve.If(unordered > 0):
                K = 15

                def linked(n):
                    k = [0]

                    def one(ins):
                        k[0] += 1
                        ins.then_inc(u_chain, 1)
                        dve.wait_ge(u_chain, K * n + k[0])
                    return one, k

                nc.vector.tensor_scalar(negd[:, 0:1], stepf[:, 0:1], -float(P), None, ALU.mult).then_inc(u_start, 1)
                nc.vector.memset(cnt[:, 0:1], 0.0).then_inc(u_start, 1)
                dve.wait_ge(u_start, 2)
                with dve.Fori(0, NG) as n:
                    one, k = linked(n)
                    one(nc.vector.tensor_copy(gidx[:, 0:1], cnt[:, 0:1]))
                    one(nc.vector.tensor_scalar(cnt[:, 0:1], cnt[:, 0:1], 1.0, None, ALU.add))
                    dve.nop(nofuse=True).then_inc(u_group, 1)
                    pick(1.0, negd[:, 0:1], one, u_pk, 16 * n + 16)
                    dve.nop(nofuse=True).then_inc(u_picked, 1)
                    dve.wait_ge(u_turned, n + 1)
                    tabulate(0, one)
                    one(nc.vector.tensor_copy(late[:, 0:1], cnt[:, 0:1]))
                    assert k[0] == K
                    waited(dve)
                    with dve.Fori(0, T) as d:
                        s = T * n + d
                        waited(dve)
                        nc.vector.tensor_copy(idxc[:, 0, 0:2], idx[:, bass.ds(d, 1), :].rearrange("p s j -> p (s j)")
                                              ).then_inc(u_index, 1)
                        nc.vector.tensor_copy(tabc[:, 0, 0:2, :], tab[:, bass.ds(d, 1)].rearrange("p s j k -> p (s j) k")
                                              ).then_inc(u_onehot, 1)
                        dve.wait_ge(u_onehot, 2 * s + 1)
                        for i in range(2):
                            for part in range(2):
                                ins = nc.vector.tensor_scalar(oneh[:, 0, i, part, :], iota16[:, :], tabc[:, 0, i, 0:1],
                                                              tabc[:, 0, i, 1 + part:2 + part], ALU.is_equal, ALU.mult)
                        ins.then_inc(u_onehot, 1)
                        dve.wait_ge(u_stepped, s + 1)
                        waited(dve)
                        nc.vector.scalar_tensor_tensor(out=flat(acc, d), in0=bank[6][:, :], scalar=cols[:, 3:4],
                                                       in1=flat(acc, d), op0=ALU.mult, op1=ALU.add).then_inc(u_added, 1)
                        dve.wait_ge(u_added, s + 1)
                        waited(dve)
            dve.nop(nofuse=True).then_inc(edges_done, 1)

            dve.wait_ge(graw_loaded, 16)
            nc.vector.tensor_reduce(mx[:, 0:1], graw[:, :, :].rearrange("p c n -> p (c n)"), AX_X, ALU.max,
                                    apply_absolute_value=True).then_inc(maxes_made, 1)
            statistics(tail, 0, 0, Q4)
            link(nc.vector.memset(lncoef[:, :], LN_MERGE))
            nc.vector.memset(lncoef[0:1, :], 1.0 - LN_MERGE * NE).then_inc(ln_coefs, 1)
            dve.wait_ge(maxes_all, 3)
            powers(0, 1, link)
            nc.vector.tensor_scalar(cols[:, 0:1], invf[:, 0:1], 1.0 / XS, None, ALU.mult).then_inc(scales_made, 1)
            scales(tail, 0, 0, Q4)
            for f in range(C):
                dve.wait_ge(high_made, 3 + f + 1)
                nc.vector.scalar_tensor_tensor(out=G16[:, 1, f, :], in0=bank[2 + f][:, :], scalar=scf[:, 0:1],
                                               in1=G16[:, 0, f, :], op0=ALU.mult, op1=ALU.subtract).then_inc(low_made, 1)
            dve.wait_ge(ln_done, 2)
            nc.vector.tensor_copy(lngb[:, :], bank[6][:, :]).then_inc(ln_out, 1)
            nc.vector.tensor_copy(lnbb[:, :], bank[7][:, :]).then_inc(ln_out, 1)
            dve.wait_ge(g2_turned, 1)
            nc.vector.tensor_copy(g2T[:, :, :].rearrange("p c e -> p (c e)"), bank[6][:, 0:C * NE]).then_inc(g2_out, 1)

            def tail_tick(g, j):
                group_work(tail, g, j, statistics, 0)
                if exists(g, j):
                    low_parts(tail, g, j, zn, zh, zl)
                g1, j1 = back(g, j, 1)
                if exists(g1, j1):
                    t, b = tile_at(g1, j1), j1 % 2
                    dve.wait_ge(tail.turned, t + 1)
                    free_group(dve, g1, j1)
                    nc.vector.tensor_copy(ztg[:, j1 // Q4, j1 % Q4, 0], turned16[b][0]).then_inc(tail.high_out, 1)
                group_work(tail, g, j, scales, 2)

            row_ticks(dve, tail_tick, T + 1)

            dve.wait_ge(gf_out, C * NQ)
            link(nc.vector.tensor_reduce(gsq[:, :], gsum[:, :, :], AX_X, ALU.add))
            link(nc.vector.tensor_scalar(gcol[:, :], gsq[:, :], 1.0 / N, None, ALU.mult))
            for c in range(C):
                nc.vector.tensor_scalar(geye[:, c, :], ones[:, :], gcol[:, c:c + 1], None, ALU.mult).then_inc(gate_in, 1)
            dve.wait_ge(gate_done, 2)
            link(nc.vector.tensor_copy(gall[:, :], bank[6][:, 0:NE]))
            link(nc.vector.tensor_copy(gT[:, :], bank[6][0:NE, NE:NE + 1]))
            for e in range(NE):
                nc.vector.tensor_scalar(geye[:, e, :], ident[:, :], gall[:, e:e + 1], None, ALU.mult).then_inc(gate_out, 1)
            for o in range(FC):
                link(nc.vector.tensor_tensor(tvb1[:, o, :], tvb1[:, o, :], gall[:, :], ALU.mult))
            link(nc.vector.tensor_reduce(b1m[:, :], tvb1[:, :, :], AX_X, ALU.add))
            link(nc.vector.tensor_tensor(b1m[:, :], b1m[:, :], b1c[:, :], ALU.add))
            dve.wait_ge(b2_done, 1)
            link(nc.vector.tensor_copy(b2f[:, :], bank[7][0:1, :]))
            split(b2f, b216, link).then_inc(bias_split, 1)
            dve.wait_ge(w1_done, 1)
            link(nc.vector.tensor_reduce(mx[:, 1:2], bank[2][:, :], AX_X, ALU.max, apply_absolute_value=True))
            link(nc.vector.tensor_reduce(mx[:, 2:3], bank[3][:, :], AX_X, ALU.max, apply_absolute_value=True))
            nc.vector.tensor_tensor(mx[:, 1:2], mx[:, 1:2], mx[:, 2:3], ALU.max).then_inc(maxes_made, 1)
            dve.wait_ge(maxes_all, 4)
            powers(1, 1, link)
            nc.vector.tensor_scalar(cols[:, 1:2], invf[:, 1:2], 1.0 / XS, None, ALU.mult).then_inc(scales_made, 1)
            dve.wait_ge(scales_made, 3)
            for f in range(C):
                dve.wait_ge(high_made, 3 + C + f // 2 * 2 + 2)
                nc.vector.scalar_tensor_tensor(out=W1m[:, 1, f, :], in0=bank[2 + f // 2][:, (f % 2) * F:(f % 2 + 1) * F],
                                               scalar=scf[:, 1:2], in1=W1m[:, 0, f, :], op0=ALU.mult, op1=ALU.subtract
                                               ).then_inc(low_made, 1)
            dve.wait_ge(w2_done, 1)
            for o in range(FC):
                nc.vector.tensor_copy(W2m[:, o, :], bank[4 + o][:, :]).then_inc(w2_out, 1)

            def out_tick(g, j):
                quad = quad_at(g, j)
                if exists(g, j):
                    t, b = tile_at(g, j), j % 2
                    dve.wait_ge(zq_made, t + 1)
                    dve.wait_ge(o_done, t + 1)
                    at_least(dve, zr_made, t - U + 1)
                    nc.vector.scalar_tensor_tensor(out=res[:, j, :], in0=zq[:, b, :], scalar=1.0 / XS,
                                                   in1=bank[4 + b][:, :], op0=ALU.mult, op1=ALU.add).then_inc(res_made, 1)
                    dve.wait_ge(res_made, t + 1)
                    if not (isinstance(quad, int) and quad == 0):
                        dve.wait_ge(two_made, quad)
                    nc.vector.bn_stats(st6[:, j % Q4, :], res[:, j, :]).then_inc(six_made, 1)
                if j % Q4 == 0 and not (isinstance(quad, int) and quad == 0):
                    n, par = 1 if isinstance(quad, int) and quad == NQ else Q4, (j // Q4 + 1) % 2
                    dve.wait_ge(r_std, quad)
                    nc.vector.reciprocal(rsr[:, par, 0:n], sd4[:, 0:n]).then_inc(r_rec, 1)
                    dve.wait_ge(r_rec, quad)
                    nc.vector.scalar_tensor_tensor(out=nbr[:, par, 0:n], in0=var4[:, par, 0:n, 0], scalar=-1.0,
                                                   in1=rsr[:, par, 0:n], op0=ALU.mult, op1=ALU.mult).then_inc(r_scale, 1)
                last = isinstance(quad, int) and quad == NQ - 1
                if exists(g, j) and (j % Q4 == Q4 - 1 or last):
                    n = 1 if last else Q4
                    dve.wait_ge(six_made, Q4 * quad + n)
                    waited(dve)
                    for i in range(n):
                        ins = nc.vector.bn_aggr(var4[:, j // Q4, i, :], st6[:, i, :])
                    ins.then_inc(two_made, 1)
                g4, j4 = back(g, j, Q4)
                if exists(g4, j4):
                    t, b = tile_at(g4, j4), j4 % 2
                    dve.wait_ge(zr_made, t + 1)
                    nc.vector.tensor_tensor(zr[:, b, :], zr[:, b, :], lngb[:, :], ALU.mult).then_inc(gained, 1)

            row_ticks(dve, out_tick, T + Q4)

        @block.tensor
        def _(pe):
            def accumulate(dest, pairs, first=None, only=True):
                pairs = ([first] if first else []) + pairs
                for n, (lhs, rhs) in enumerate(pairs):
                    ins = nc.tensor.matmul(dest, lhs, rhs, start=(n == 0 and only), stop=(n == len(pairs) - 1),
                                           skip_group_check=not only)
                return ins

            pe.wait_ge(consts_made, 1)
            pe.wait_ge(start_made, 1)
            nc.tensor.matmul(bank[4][:, 0:NG], ones[0:1, :], srowf[:, :], start=True, stop=True).then_inc(start_spread, 1)
            pe.wait_ge(groups_made, 1)
            for c in range(SC):
                ins = nc.tensor.matmul(bank[5][0:1, c * P:(c + 1) * P], ntile[:, c:c + 1], ident[:, :],
                                       start=True, stop=True)
            ins.then_inc(tiles_turned, 1)

            def turn_picked():
                for i in range(2):
                    nc.tensor.transpose(bank[4][:, i * P:(i + 1) * P], srcf[:, i * P:(i + 1) * P], ident[:, :])
                    nc.tensor.transpose(bank[4][:, (2 + i) * P:(3 + i) * P], rel[:, i * P:(i + 1) * P], ident[:, :])
                    ins = nc.tensor.transpose(bank[5][:, i * P:(i + 1) * P],
                                              pk[:, 2, i * P:(i + 1) * P].bitcast(F32), ident[:, :])
                return ins

            for n in range(SC):
                pe.wait_ge(picked, n + 1)
                turn_picked().then_inc(turned, 1)

            def turn_rows(loop, g, j, high, low):
                t, b = tile_at(g, j), j % 2
                pe.wait_ge(loop.high, t + 1)
                pe.wait_ge(loop.low, t + 1)
                at_least(pe, loop.high_out, t - 1)
                at_least(pe, loop.low_out, t - 1)
                for part, rows_ in enumerate((high, low)):
                    for c in range(C):
                        ins = nc.tensor.transpose(turned16[b][part][:, c, :], rows_[:, b, c * P:(c + 1) * P], ident16[:, :])
                ins.then_inc(loop.turned, 1)

            def head_tick(g, j):
                if exists(g, j):
                    turn_rows(head, g, j, xh, xl)
                g1, j1 = back(g, j, 1)
                if exists(g1, j1):
                    t, b = tile_at(g1, j1), j1 % 2
                    pe.wait_ge(head.high_out, t + 1)
                    pe.wait_ge(head.low_out, t + 1)
                    at_least(pe, low_made, 1)
                    at_least(pe, y_low, t - 1)
                    accumulate(bank[2 + b][:, :], [(xtb[:, b, p, c, :], Wg16[:, q, c, :]) for c in range(C)
                                                   for p, q in PASSES]).then_inc(y_made, 1)

            row_ticks(pe, head_tick, T + 1)

            def step(s, slot, oslot, ebank, use):
                pe.wait_ge(onehot, s + 1)
                at_least(pe, edge_added, s - 1)
                for i in range(2):
                    pe.wait_ge(gathered[slot + i], 16 * use)
                accumulate(bank[ebank][:, :], [(oneh[:, oslot, i, p, :], rows[:, slot + i, q, :]) for i in range(2)
                                               for p, q in PASSES]).then_inc(stepped, 1)

            pe.wait_ge(y_low, T)
            pe.wait_ge(y_high, T)
            pe.wait_ge(low_made, 3)
            pe.wait_ge(bias_spread, 16 * 9)

            def first_pe(t, h, b):
                pe.wait_ge(xt_in[b], 16 * h + 16)
                at_least(pe, f_used, t)
                accumulate(bank[4][:, :], [(xta[:, b, p, c, :], Wk16[:, q, c, :]) for c in range(C) for p, q in PASSES],
                           first=(ones3[:, :], krows[:, :])).then_inc(f_done, 1)
                for r in range(3):
                    step(SA * t + r, 2 * r, r % OHS, 6 + r % 2, t + 1)
                pe.wait_ge(f_used, t + 1)
                pe.wait_ge(xn_in[b], 16 * h + 16)
                start = isinstance(t, int) and t == 0
                stop = isinstance(t, int) and t == T - 1
                for c in range(C):
                    nc.tensor.matmul(bank[c][:, :], kf[:, b, c * P:(c + 1) * P], xna[:, b, :], start=start, stop=stop,
                                     skip_group_check=True)
                for c in range(C):
                    ins = nc.tensor.matmul(bank[5][:, c:c + 1], kf[:, b, c * P:(c + 1) * P],
                                           valid[:, :] if stop else ones[:, 0:1], start=start and c == 0, stop=stop,
                                           skip_group_check=True)
                ins.then_inc(m_done, 1)
                for r in range(3, SA):
                    step(SA * t + r, 2 * r, r % OHS, 6 + r % 2, t + 1)

            first_tiles(pe, first_pe)

            pe.wait_ge(m_out, C + 1)
            for f in range(C):
                for c in range(C):
                    nc.tensor.transpose(bank[f][:, c * P:(c + 1) * P], M32[:, c, f * P:(f + 1) * P], ident[:, :])
            for c in range(C):
                ins = nc.tensor.transpose(bank[5][0:1, c * P:(c + 1) * P], ksum[:, c:c + 1], ident[:, :])
            ins.then_inc(m_turned, 1)
            pe.wait_ge(mt_out, C + 1)
            pe.wait_ge(vp_loaded, 32)
            for c in range(C):
                s = slice(c * P, (c + 1) * P)
                ins = accumulate(bank[4][:, s], [(Wv32[:, f, s], MT32[:, f, s]) for f in range(C)],
                                 first=(bvrow[:, s], krow[:, s]))
            ins.then_inc(kv_done, 1)
            pe.wait_ge(kv_out, C)
            for c in range(C):
                ins = nc.tensor.matmul(bank[c][:, :], kvt[:, c, :], Wp32[:, c, :], start=True, stop=True)
            ins.then_inc(kvp_done, 1)
            pe.wait_ge(kv_out, 2 * C)
            pe.wait_ge(kvp_out, C)

            def mix(t, b):
                pe.wait_ge(qz_made, t + 1)
                at_least(pe, mix_added, t - 1)
                accumulate(bank[3 + b][:, :], [(qz[:, b, c * P:(c + 1) * P], KVP[:, c, :]) for c in range(C)],
                           first=(ones3[:, :], mrows[:, :])).then_inc(mix_done, 1)

            def second_pe(t, h, b):
                pe.wait_ge(xt_in[b], 16 * ((T + 1 - b) // 2) + 16 * h + 16)
                at_least(pe, f_used, T + t - 1)
                for c in range(C):
                    s = slice(c * P, (c + 1) * P)
                    pairs = [(qrows[:, s], ones3[:, :])] + [(Wq16[:, p, f, s], xta[:, b, q, f, :]) for f in range(C)
                                                            for p, q in PASSES]
                    for n, (lhs, rhs) in enumerate(pairs):
                        ins = nc.tensor.matmul(bank[b][:, s], lhs, rhs, start=(c == 0 and n == 0),
                                               stop=(n == len(pairs) - 1), skip_group_check=True)
                ins.then_inc(f_done, 1)
                if not (isinstance(t, int) and t == 0):
                    mix(t - 1, 1 - b)
                one = lambda r: step(S2 + SB * t + r, 2 * (SB * b + r), r, 6 + (b + r) % 2, T + h + 1)
                one(0)
                one(1)
                pe.wait_ge(f_used, T + t + 1)
                at_least(pe, rz_made, t)
                for c in range(C):
                    s = slice(c * P, (c + 1) * P)
                    ins = nc.tensor.matmul(bank[2][:, s], kden[:, c, :], kf[:, b, s], start=True, stop=True)
                ins.then_inc(den_done, 1)
                one(2)

            second_tiles(pe, second_pe)
            mix(T - 1, (T - 1) % 2)

            pe.wait_ge(edge_added, S2 + SB * T)
            unordered = pe.value_load(flag[0:1, 0:1], min_val=0, max_val=1)
            with pe.If(unordered > 0):
                with pe.Fori(0, NG) as n:
                    pe.wait_ge(u_picked, n + 1)
                    waited(pe)
                    turn_picked().then_inc(u_turned, 1)
                    with pe.Fori(0, T) as d:
                        s = T * n + d
                        pe.wait_ge(u_gathered, 32 * s + 32)
                        pe.wait_ge(u_onehot, 2 * s + 2)
                        waited(pe)
                        accumulate(bank[6][:, :], [(oneh[:, 0, i, p, :], rows[:, i, q, :]) for i in range(2)
                                                   for p, q in PASSES]).then_inc(u_stepped, 1)

            pe.wait_ge(edges_done, 1)
            pe.wait_ge(graw_loaded, 16)
            for f in range(C):
                for o in range(C):
                    ins = nc.tensor.transpose(bank[2 + f][:, o * P:(o + 1) * P], graw[:, o, f * P:(f + 1) * P], ident[:, :])
            ins.then_inc(graw_turned, 1)
            pe.wait_ge(small_loaded, 16 * 14)
            pe.wait_ge(ln_coefs, 1)
            nc.tensor.matmul(bank[6][:, :], lncoef[:, :], lnrows[:, :], start=True, stop=True).then_inc(ln_done, 1)
            nc.tensor.matmul(bank[7][:, :], lncoef[:, :], lbrows[:, :], start=True, stop=True).then_inc(ln_done, 1)
            pe.wait_ge(ln_out, 2)
            for c in range(C):
                ins = nc.tensor.transpose(bank[6][:, c * NE:(c + 1) * NE], g2raw[:, c * P:(c + 1) * P], ident[0:NE, 0:NE])
            ins.then_inc(g2_turned, 1)
            pe.wait_ge(high_made, 3 + C)
            pe.wait_ge(low_made, 3 + C)

            pe.wait_ge(g2_out, 1)

            def tail_tick(g, j):
                if exists(g, j):
                    turn_rows(tail, g, j, zh, zl)
                if gate_exists(g, j):
                    q, m = gate_at(g, j)
                    par = ((j - Q4 - 1 - m) // Q4) % 2
                    last = isinstance(q, int) and q == NQ - 1
                    if m == 0:
                        pe.wait_ge(tail.high_out, T if last else Q4 * q + Q4)
                        pe.wait_ge(tail.low_out, T if last else Q4 * q + Q4)
                    at_least(pe, gf_out, C * (q - 1) + m + 1)
                    s = slice(m * P, (m + 1) * P)
                    n = LAST if last else D
                    if last:
                        pairs = [(G16[:, a, f, s], ztg[:, par, 0, b_, f, 0:LAST]) for f in range(C) for a, b_ in PASSES]
                    else:
                        pairs = [(G16[:, a, f, s], ztg[:, par, :, b_, f, :]) for f in range(C) for a, b_ in PASSES]
                    accumulate(bank[2 + m][:, 0:n], pairs).then_inc(gf_done, 1)

            row_ticks(pe, tail_tick, Q4 * NQ + 5)

            pe.wait_ge(gate_in, C)
            accumulate(bank[6][:, 0:NE], [(geye[:, c, :], g2T[:, c, :]) for c in range(C)] + [(ones[0:1, :], gbr[:, :])]
                       ).then_inc(gate_done, 1)
            accumulate(bank[6][0:NE, NE:NE + 1], [(g2T[:, c, :], gcol[:, c:c + 1]) for c in range(C)]
                       + [(gbr[:, :], ones[0:1, 0:1])]).then_inc(gate_done, 1)
            pe.wait_ge(gate_out, NE)
            accumulate(bank[7][0:1, :], [(gT[:, :], tvb2[:, :]), (ones[0:1, 0:1], b2r[:, :])]).then_inc(b2_done, 1)
            pe.wait_ge(tv1_loaded, 16 * NE)
            pe.wait_ge(gf_out, C * NQ)
            for f in range(C):
                for o in range(FC):
                    s = slice(f * P, (f + 1) * P)
                    at = (f % 2) * F + o * P
                    ins = accumulate(bank[2 + f // 2][:, at:at + P], [(W1raw[:, o, s], ident[:, :])]
                                     + [(tvW1[:, e, o, s], geye[:, e, :]) for e in range(NE)])
            ins.then_inc(w1_done, 1)
            pe.wait_ge(tv2_loaded, 16 * NE)
            for o in range(FC):
                for c in range(C):
                    s = slice(o * P, (o + 1) * P)
                    ins = accumulate(bank[4 + o][:, c * P:(c + 1) * P], [(W2raw[:, c, s], ident[:, :])]
                                     + [(tvW2[:, e, c, s], geye[:, e, :]) for e in range(NE)])
            ins.then_inc(w2_done, 1)
            pe.wait_ge(high_made, 3 + C + C)
            pe.wait_ge(low_made, 3 + C + C)

            def hidden(q, par, n):
                for o in range(FC):
                    at_least(pe, h_out, FC * (q - 1) + o + 1)
                    s = slice(o * P, (o + 1) * P)
                    if n == P:
                        pairs = [(W1m[:, a, f, s], xd[:, par, 0, b_, f, :]) for f in range(C) for a, b_ in PASSES]
                    else:
                        pairs = [(W1m[:, a, f, s], xd[:, par, :, b_, f, :]) for f in range(C) for a, b_ in PASSES]
                    accumulate(bank[2 + o][:, 0:n], pairs).then_inc(h_done, 1)

            pe.wait_ge(zd_in[0], 16)
            hidden(0, 0, Q4 * P)
            pe.wait_ge(w2_out, FC)
            pe.wait_ge(bias_spread, 16 * 12)

            def out_tick(g, j):
                quad = quad_at(g, j)
                if j % Q4 == 0 and not (isinstance(quad, int) and quad + 1 >= NQ):
                    pe.wait_ge(zd_in[(j // Q4 + 1) % 2], 16 * (g + 1 + j // Q4))
                    hidden(quad + 1, (j // Q4 + 1) % 2, P if isinstance(quad, int) and quad + 1 == NQ - 1 else Q4 * P)
                if exists(g, j):
                    t, b = tile_at(g, j), j % 2
                    pe.wait_ge(h_out, FC * (quad + 1))
                    at_least(pe, res_made, t - 1)
                    s = slice((j % Q4) * P, (j % Q4 + 1) * P)
                    accumulate(bank[4 + b][:, :], [(hT[:, j // Q4, o, s], W2m[:, o, :]) for o in range(FC)],
                               first=(ones3[:, :], b2rows[:, :])).then_inc(o_done, 1)

            row_ticks(pe, out_tick, T)


_NAMES = ["x", "src", "dst", "edge_weight", "L0_gnn_weight", "L0_gnn_bias", "L0_mix_Wq", "L0_mix_bq", "L0_mix_Wk",
          "L0_mix_bk", "L0_mix_Wv", "L0_mix_bv", "L0_mix_Wp", "L0_mix_bp", "L0_ffn_gfc1_w", "L0_ffn_gfc1_b",
          "L0_ffn_gfc2_w", "L0_ffn_gfc2_b", "L0_ffn_W1", "L0_ffn_b1", "L0_ffn_W2", "L0_ffn_b2", "L0_ffn_ln_g",
          "L0_ffn_ln_b", "L0_ffn_tv_W1", "L0_ffn_tv_b1", "L0_ffn_tv_W2", "L0_ffn_tv_b2", "L0_ffn_tv_ln_g",
          "L0_ffn_tv_ln_b"]


def kernel(**inputs):
    import numpy as np
    from concourse import bacc
    from concourse.bass_utils import run_bass_kernel_spmd

    nc = bacc.Bacc("TRN2", target_bir_lowering=False, num_devices=1)
    arrays, args = {}, []
    for name in _NAMES:
        a = np.ascontiguousarray(inputs[name])
        arrays["in_" + name] = a
        args.append(nc.dram_tensor("in_" + name, a.shape, mybir.dt.from_np(a.dtype), kind="ExternalInput").ap())
    out = nc.dram_tensor("out", (N, D), F32, kind="ExternalOutput").ap()
    build(nc, *args, out)
    result = run_bass_kernel_spmd(nc, [arrays], core_ids=[0])
    return result.results[0]["out"]
```

```python
from contextlib import ExitStack

import concourse.bass as bass
from concourse import mybir

F32 = mybir.dt.float32
F16 = mybir.dt.float16
BF16 = mybir.dt.bfloat16
I32 = mybir.dt.int32
ALU = mybir.AluOpType
ACT = mybir.ActivationFunctionType
AX_X = mybir.AxisListType.X
RMAX = bass.bass_isa.ReduceOp.max
RADD = bass.bass_isa.ReduceOp.add

P = 128
N, D = 6250, 512
E = 100000
C = D // P
T = -(-N // P)
LAST = N - (T - 1) * P
H = 8
HD = D // H
F = 256
FC = F // P
NE = 8
EG = 2 * P
NG = -(-E // EG)
GFULL = E // EG
SA = -(-(NG + T - 1) // T)
SC = -(-SA * T // P)
RING = 6
SLOTS = 2 * RING
OHS = 6
AHEAD = 4
STEP_BANKS = (6, 7, 4)
U_HOT = 4
BLOCKS = -(-NG * T // P)
DR, DW = 125, E // 125
OUTSIDE = float(1 << 20)
QS = float(1 << 14)
XS = 1024.0
EPS = 1e-5
LN_MERGE = 0.03
Q4 = 4
U = 2 * Q4
NQ = -(-T // Q4)
EXPONENT = 0x7F800000
PASSES = ((0, 0), (0, 1), (1, 0))


def at_least(eng, sem, n):
    if not isinstance(n, int) or n > 0:
        eng.wait_ge(sem, n)


def size_of(shape, dt):
    n = mybir.dt.size(dt)
    for s in shape[1:]:
        n *= s
    return -(-n // 32) * 32


def build(nc, x, src, dst, edge_weight, gnn_w, gnn_b, Wq, bq, Wk, bk, Wv, bv, Wp, bp,
          gfc1_w, gfc1_b, gfc2_w, gfc2_b, W1, b1, W2, b2, ln_g, ln_b,
          tv_W1, tv_b1, tv_W2, tv_b2, tv_ln_g, tv_ln_b, out):
    packed = nc.dram_tensor("packed", (NG, 3 * EG), I32, kind="Internal").ap()
    y_rows = nc.dram_tensor("y_rows", (T * P, 2 * D), F16, kind="Internal").ap()
    xt_rows = nc.dram_tensor("xt_rows", (T * P, 2 * D), F16, kind="Internal").ap()
    zt_rows = nc.dram_tensor("zt_rows", (T * P, 2 * D), F16, kind="Internal").ap()

    def row_tile(ap, t):
        return ap.rearrange("(t p) d -> t p d", p=P)[bass.ds(t, 1)].rearrange("a p d -> (a p) d")

    with ExitStack() as ctx:
        ctx.enter_context(nc.allow_non_contiguous_dma(reason="small columns: group starts, biases"))
        base, top = -(-nc.sbuf_base // 32) * 32, nc.sbuf_usable_end
        cursor = [base]

        def put(name, shape, dt):
            at = cursor[0]
            cursor[0] += size_of(shape, dt)
            assert cursor[0] <= top, (name, cursor[0], top)
            return nc.alloc_sbuf_tensor_at(name, shape, dt, offset=at)

        def over(at, *specs):
            made = []
            for name, shape, dt in specs:
                made.append(nc.alloc_sbuf_tensor_at(name, shape, dt, offset=at))
                at += size_of(shape, dt)
                assert at <= top, (name, at, top)
            return made if len(made) > 1 else made[0]

        def region(size):
            cursor[0] += size
            return cursor[0] - size

        sem = lambda name: ctx.enter_context(nc.semaphore(name))

        acc = put("acc", [P, T, D], F32)
        ident = put("ident", [P, P], F32)
        ident16 = put("ident16", [P, P], F16)
        iota16 = put("iota16", [P, P], F16)
        ones = put("ones", [P, P], F32)
        ones3 = put("ones3", [3, P], BF16)
        headmask = put("headmask", [P, P], F32)
        rs = put("rs", [P, T + Q4 - 1], F32)
        nb = put("nb", [P, T + Q4 - 1], F32)
        var4 = put("var4", [P, 2, Q4, 2], F32)
        st6 = put("st6", [P, Q4, 6], F32)
        sd4 = put("sd4", [P, Q4], F32)
        rsr = put("rsr", [P, 2, Q4], F32)
        nbr = put("nbr", [P, 2, Q4], F32)
        epsc = put("epsc", [P, 1], F32)
        minus1 = put("minus1", [P, 1], F32)
        mx = put("mx", [P, 8], F32)
        mxa = put("mxa", [P, 8], F32)
        pw = put("pw", [P, 8], I32)
        sc = put("sc", [P, 8], I32)
        inv = put("inv", [P, 8], I32)
        cols = put("cols", [P, 8], F32)
        den = put("den", [P, H], F32)
        rden = put("rden", [P, H], F32)
        stepi = put("stepi", [P, SC], I32)
        stepf = put("stepf", [P, SC], F32)
        cnt = put("cnt", [P, SC], F32)
        gidx = put("gidx", [P, SC], I32)
        ntile = put("ntile", [P, SC], F32)
        negd = put("negd", [P, SC], F32)
        late = put("late", [P, SC], F32)
        viol = put("viol", [P, 1], F32)
        uns = put("uns", [P, 1], F32)
        srt = put("srt", [P, 1], F32)
        flag = put("flag", [1, 1], I32)
        tileof = put("tileof", [1, SC * P], I32)
        krows = put("krows", [3, D], BF16)
        qrows = put("qrows", [3, D], BF16)
        mrow = put("mrow", [1, D], F32)
        kinv = put("kinv", [P, C], F32)
        bvrow = put("bvrow", [1, D], F32)
        rA, rB, rQ, rV, rP = (region(4 * C * D) for _ in range(5))
        rTab, rIdx, rG = region(SC * P * 16), region(SC * P * 8), region(SLOTS * 4 * D)
        rW = cursor[0]
        Wg16 = over(rA, ("Wg16", [P, 2, C, D], F16))
        Wk16 = over(rB, ("Wk16", [P, 2, C, D], F16))
        Wq16 = over(rQ, ("Wq16", [P, 2, C, D], F16))
        Wv32 = over(rV, ("Wv32", [P, C, D], F32))
        Wp32 = over(rP, ("Wp32", [P, C, D], F32))
        M32 = over(rA, ("M32", [P, C, D], F32))
        MT32 = over(rB, ("MT32", [P, C, D], F32))
        KVP = over(rA, ("KVP", [P, C, D], F32))
        KVP16 = over(rV, ("KVP16", [P, 2, C, D], F16))
        qk, qs, qhl, kvt = over(
            rB, ("qk", [P, D], F32), ("qs", [P, D], F32), ("qhl", [P, 2, D], F16), ("kvt", [P, C, P], F32))
        qT = over(rP, ("qT", [P, 2, 2, C, P], F16))
        tab = over(rTab, ("tab", [P, SC * P, 2, 2], F32))
        idx = over(rIdx, ("idx", [P, SC * P, 2], I32))
        rows = over(rG, ("rows", [P, SLOTS, 2, D], F16))
        stage = over(rG, ("stage", [P, 3, C, D], F32))
        pk, srcf, rel, ok = over(
            rV, ("pk", [P, 3, EG], I32), ("srcf", [P, EG], F32), ("rel", [P, EG], F32), ("ok", [P, EG], F32))
        startb, pad = over(rP, ("startb", [P, NG], F32), ("pad", [1, 3, EG], I32))
        dsts, ews, junk = over(rTab, ("dsts", [P, DW + 1], I32), ("ews", [P, DW], F32), ("junk", [P, NG], F32))
        srow, srowf, irow, bf, b16, brow = over(
            rW, ("srow", [1, NG], I32),
            ("srowf", [1, NG], F32), ("irow", [1, NG], I32), ("bf", [1, D], F32), ("b16", [1, 2, 3, D], BF16),
            ("brow", [1, 4, D], F32))
        xh, xl, xtb, yb, kh, kl, fill = over(
            rG, ("xh", [P, 4, D], F16), ("xl", [P, 4, D], F16), ("xtb", [P, 2, 2, C, P], F16),
            ("yb", [P, 2, 2, D], F16), ("kh", [P, 2, D], F16), ("kl", [P, 2, D], F16), ("fill", [P, 4 * D], F16))
        xnb = over(rW, ("xnb", [P, 2, D], F32))
        xta, kf, ksacc, mb, ksb, hotw, idxc, tabc, wh16, wlo = over(
            rW, ("xta", [P, 2, 2, C, P], F16), ("kf", [P, 2, D], F32), ("ksacc", [P, D], F32), ("mb", [P, D], F32),
            ("ksb", [P, D], F32), ("hotw", [P, OHS, 2, 2, P], F16), ("idxc", [P, 2, 2 * SA], I32),
            ("tabc", [P, 2, 2 * SA, 2], F32), ("wh16", [P, 2, 2 * SA], F16), ("wlo", [P, 2, 2 * SA], F32))
        oneh = over(rW + 3 * 4 * D, ("oneh", [P, OHS, 2, P], F16))
        graw = over(rA, ("graw", [P, C, D], F32))
        tvW1 = over(rA, ("tvW1", [P, NE, FC, D], F32))
        xd, hT, zq, zr = over(
            rA, ("xd", [P, 2, Q4, 2, C, P], F16), ("hT", [P, 2, FC, D], F32), ("zq", [P, 2, D], F32),
            ("zr", [P, 2, D], F32))
        G16, ztg = over(rP, ("G16", [P, 2, C, D], F16), ("ztg", [P, 2, Q4, 2, C, P], F16))
        tvW2 = over(rP, ("tvW2", [P, NE, C, F], F32))
        res, ob = over(rP, ("res", [P, U, D], F32), ("ob", [P, 2, D], F32))
        rN = rP + 4 * NE * C * F
        zn, zh, zl = over(rN, ("zn", [P, 2, D], F32), ("zh", [P, 2, D], F16), ("zl", [P, 2, D], F16))
        W1m, W2m = over(rN, ("W1m", [P, 2, C, F], F16), ("W2m", [P, FC, D], F32))
        (W1raw, W2raw, lnrows, lbrows, g2raw, lngb, lnbb, lncoef, gjunk, gsum, gsq, gcol, gbias, g2T,
         gall, gT, gbr, b1c, tvb1, b1m, tvb2, geye) = over(
            rN + 16 * D, ("W1raw", [P, FC, D], F32), ("W2raw", [P, C, F], F32),
            ("lnrows", [NE + 1, D], F32), ("lbrows", [NE + 1, D], F32), ("g2raw", [NE, D], F32),
            ("lngb", [P, D], F32), ("lnbb", [P, D], F32), ("lncoef", [NE + 1, P], F32), ("gjunk", [P, D], F16),
            ("gsum", [P, C, NQ], F32), ("gsq", [P, C], F32), ("gcol", [P, C], F32), ("gbias", [P, C], F32),
            ("g2T", [P, C, NE], F32), ("gall", [P, NE], F32), ("gT", [NE, 1], F32),
            ("gbr", [1, NE], F32), ("b1c", [P, FC], F32), ("tvb1", [P, FC, NE], F32),
            ("b1m", [P, FC], F32), ("tvb2", [NE, D], F32), ("geye", [P, NE, P], F32))
        b2f, b216 = over(rN + 16 * D + 8 * F * 4 + 0, ("b2f", [1, D], F32), ("b216", [1, 3, D], BF16))
        b2rows, b2r = krows, bvrow

        bank = [ctx.enter_context(nc.psum_tensor(f"bank{i}", [P, D], F32)) for i in range(8)]

        pool_set = sem("pool_set")
        consts_made = sem("consts_made")
        edges_loaded, start_loaded, bias_loaded = sem("edges_loaded"), sem("start_loaded"), sem("bias_loaded")
        w_loaded = [sem(f"w_loaded{k}") for k in range(3)]
        edges_packed, vp_loaded = sem("edges_packed"), sem("vp_loaded")
        x_loaded = [sem(f"x_loaded{j}") for j in range(Q4)]
        maxes_made, maxes_all = sem("maxes_made"), sem("maxes_all")
        scales_made, high_made, low_made = sem("scales_made"), sem("high_made"), sem("low_made")
        chain = sem("chain")
        start_made, start_spread = sem("start_made"), sem("start_spread")
        groups_made, tiles_turned = sem("groups_made"), sem("tiles_turned")
        bias_split, bias_spread = sem("bias_split"), sem("bias_spread")
        pk_ready, picked, turned, tabled = sem("pk_ready"), sem("picked"), sem("turned"), sem("tabled")

        class RowLoop:

            def __init__(self, name):
                self.vars_made = sem(name + "_vars_made")
                self.std_made = sem(name + "_std_made")
                self.scale_made = sem(name + "_scale_made")
                self.high = sem(name + "_high")
                self.low = sem(name + "_low")
                self.turned = sem(name + "_turned")
                self.turned_out = sem(name + "_turned_out")
                self.turned_kept = [sem(f"{name}_turned_kept{b}") for b in range(2)]

                self.six = sem(name + "_six")
                self.rec = sem(name + "_rec")

        head, tail = RowLoop("head"), RowLoop("tail")
        y_made, y_high, y_low = sem("y_made"), sem("y_high"), sem("y_low")
        y_kept = [sem(f"y_kept{b}") for b in range(2)]
        copied, indexed, parted = sem("copied"), sem("indexed"), sem("parted")
        gathered = [sem(f"gathered{q}") for q in range(SLOTS)]
        onehot, weighted, stepped, edge_added = (sem(n) for n in ("onehot", "weighted", "stepped", "edge_added"))
        xt_in = [sem(f"xt_in{b}") for b in range(2)]
        f_done, f_min, f_exp, f_used, m_done = (sem(n) for n in ("f_done", "f_min", "f_exp", "f_used", "m_done"))
        k_high, k_low, k_summed = sem("k_high"), sem("k_low"), sem("k_summed")
        ks_done, m_out, m_turned, mt_out = (sem(n) for n in ("ks_done", "m_out", "m_turned", "mt_out"))
        kv_done, kv_out, kvp_done, kvp_out, kvp_low, kmax_turned, kmax_row, kmax_spread = (sem(n) for n in (
            "kv_done", "kv_out", "kvp_done", "kvp_out", "kvp_low", "kmax_turned", "kmax_row", "kmax_spread"))
        q_summed, q_scaled, q_high, q_low, q_turned, q_out, mix_done, mix_added = (sem(n) for n in (
            "q_summed", "q_scaled", "q_high", "q_low", "q_turned", "q_out", "mix_done", "mix_added"))
        graw_loaded = sem("graw_loaded")
        u_chain, u_group, u_pk, u_picked, u_turned, u_index, u_gathered, u_onehot, u_stepped, u_added = (
            sem(n) for n in ("u_chain", "u_group", "u_pk", "u_picked", "u_turned", "u_index", "u_gathered",
                             "u_onehot", "u_stepped", "u_added"))
        edges_done, u_start = sem("edges_done"), sem("u_start")
        small_loaded, tv1_loaded, tv2_loaded = sem("small_loaded"), sem("tv1_loaded"), sem("tv2_loaded")
        ln_coefs, g2_turned, g2_out, gate_in = sem("ln_coefs"), sem("g2_turned"), sem("g2_out"), sem("gate_in")
        graw_turned = sem("graw_turned")
        ln_done, ln_out = sem("ln_done"), sem("ln_out")
        gf_done, gf_out = sem("gf_done"), sem("gf_out")
        gate_done, gate_out, b2_done = sem("gate_done"), sem("gate_out"), sem("b2_done")
        w1_done, w2_done, w2_out = sem("w1_done"), sem("w2_done"), sem("w2_out")
        zd_in = [sem(f"zd_in{b}") for b in range(2)]
        h_done, h_out, o_done, zq_made, res_made, six_made, two_made, r_std, r_rec, r_scale = (sem(n) for n in (
            "h_done", "h_out", "o_done", "zq_made", "res_made", "six_made", "two_made", "r_std", "r_rec", "r_scale"))
        zr_made, gained, based, ob_made = sem("zr_made"), sem("gained"), sem("based"), sem("ob_made")
        out_kept = [sem(f"out_kept{b}") for b in range(2)]

        block = ctx.enter_context(nc.Block())
        flat = lambda ap, t: ap[:, bass.ds(t, 1), :].rearrange("p a d -> p (a d)")

        def back(g, j, n):
            return g + (j - n) // U, (j - n) % U

        def tile_at(g, j):
            return U * g + j

        def half_at(g, j):
            return U // 2 * g + j // 2

        def quad_at(g, j):
            return 2 * g + j // Q4

        def row_ticks(eng, tick, last):
            for j in range(U):
                tick(0, j)
            with eng.Fori(1, T // U - 1) as g:
                for j in range(U):
                    tick(g, j)
            for t in range((T // U - 1) * U, last):
                tick(t // U, t % U)

        def exists(g, j):
            return not isinstance(g, int) or 0 <= tile_at(g, j) < T

        def edge_tiles(eng, tile):
            tile(0, 0, 0)
            tile(1, 0, 1)
            with eng.Fori(1, T // 2) as h:
                tile(2 * h, h, 0)
                tile(2 * h + 1, h, 1)
            tile(T - 1, T // 2, (T - 1) % 2)

        def place(h, b, r):
            turn = 2 * SA // RING
            return (SA * b + r) % RING, turn * h + (SA * b + r) // RING + 1

        def step_bank(b, r):
            return bank[STEP_BANKS[(SA * b + r) % len(STEP_BANKS)]]

        def head_kept(eng):
            for b in range(2):
                n = 16 * ((T + 1 - b) // 2)
                eng.wait_ge(head.turned_kept[b], n)
                eng.wait_ge(y_kept[b], n)

        def gate_at(g, j):
            m = (j - 1) % Q4
            return 2 * g + (j - Q4 - 1 - m) // Q4, m

        def gate_exists(g, j):
            return not isinstance(g, int) or 0 <= gate_at(g, j)[0] < NQ

        def free_group(eng, g, j):
            at_least(eng, tail.turned_kept[j % 2], 16 * (half_at(g, j) - Q4 + 2))
            if j % Q4 == 0:
                at_least(eng, gf_done, C * (quad_at(g, j) - 1))

        def waited(eng):
            eng.nop(nofuse=True)

        def turned16(b):
            return bank[b][:, :].bitcast(F16).rearrange("p (a c m) -> p a c m", a=2, c=C)

        scf, invf = sc[:, :].bitcast(F32), inv[:, :].bitcast(F32)
        by_half = lambda ap: ap.rearrange("p (j s) -> p j s", j=2)

        @block.sync
        def _(sp):
            flat_dst = dst.rearrange("(a n) -> a n", a=1)
            by_row = dst.rearrange("(p w) -> p w", w=DW)
            sp.dma_start(dsts[0:DR, 0:DW], by_row).then_inc(edges_loaded, 16)
            sp.dma_start(dsts[0:DR - 1, DW:DW + 1], by_row[1:DR, 0:1]).then_inc(edges_loaded, 16)
            sp.dma_start(dsts[DR - 1:DR, DW:DW + 1], flat_dst[:, E - 1:E]).then_inc(edges_loaded, 16)
            sp.dma_start(ews[0:DR, :], edge_weight.rearrange("(p w) -> p w", w=DW)).then_inc(edges_loaded, 16)
            for k, w in enumerate((gnn_w, Wk, Wq)):
                sp.dma_start(stage[:, k], w.rearrange("(c p) n -> p c n", p=P)).then_inc(w_loaded[k], 16)
            sp.dma_start(srow[:, :], flat_dst[:, 0:E:EG]).then_inc(start_loaded, 16)
            for r, b in enumerate((bk, bq, bp, gnn_b)):
                sp.dma_start(brow[:, r, :], b.rearrange("(a n) -> a n", a=1)).then_inc(bias_loaded, 16)
            sp.dma_start(bvrow[:, :], bv.rearrange("(a n) -> a n", a=1)).then_inc(bias_loaded, 16)

            def load_x(g, j):
                t = Q4 * g + j
                at_least(sp, x_loaded[j], 16 * g)
                sp.dma_start(flat(acc, t), row_tile(x[0:(T - 1) * P, :], t)).then_inc(x_loaded[j], 16)

            for j in range(Q4):
                load_x(0, j)
            with sp.Fori(1, (T - 1) // Q4) as g:
                for j in range(Q4):
                    load_x(g, j)
            sp.wait_ge(consts_made, 1)
            sp.dma_start(acc[0:LAST, T - 1, :], x[(T - 1) * P:N, :]).then_inc(x_loaded[0], 16)

            sp.wait_ge(bias_split, 2)
            for r, dest in enumerate((krows, qrows)):
                for part in range(3):
                    sp.dma_start(dest[part:part + 1, :], b16[:, r, part, :]).then_inc(bias_spread, 16)
            sp.wait_ge(tabled, SC)
            sp.dma_start(Wv32[:, :, :], Wv.rearrange("(c p) n -> p c n", p=P)).then_inc(vp_loaded, 16)
            sp.dma_start(Wp32[:, :, :], Wp.rearrange("(c p) n -> p c n", p=P)).then_inc(vp_loaded, 16)

            def head_stores(g, j):
                g1, j1 = back(g, j, 1)
                if exists(g1, j1):
                    t, b1 = tile_at(g1, j1), j1 % 2
                    sp.wait_ge(head.turned_out, t + 1)
                    sp.dma_start(row_tile(xt_rows, t), xtb[:, b1].rearrange("p a c m -> p (a c m)")
                                 ).then_inc(head.turned_kept[b1], 16)
                g2, j2 = back(g, j, 2)
                if exists(g2, j2):
                    t, b = tile_at(g2, j2), j2 % 2
                    sp.wait_ge(y_low, t + 1)
                    sp.dma_start(row_tile(y_rows, t), yb[:, b].rearrange("p a d -> p (a d)")
                                 ).then_inc(y_kept[b], 16)

            row_ticks(sp, head_stores, T + 2)
            head_kept(sp)
            sp.wait_ge(head.turned, T)

            def turned_loads(t, h, b):
                at_least(sp, f_done, T + t - 1)
                sp.dma_start(xta[:, b].rearrange("p a c m -> p (a c m)"), row_tile(xt_rows, t)
                             ).then_inc(xt_in[b], 16)

            edge_tiles(sp, turned_loads)
            sp.wait_ge(kvp_low, C)
            sp.dma_start(graw[:, :, :], gfc1_w.rearrange("(c p) n -> p c n", p=P)).then_inc(graw_loaded, 16)

            sp.wait_ge(edges_done, 1)
            one = lambda ap: ap.rearrange("(a n) -> a n", a=1)
            for dest, source in (
                    (lnrows[0:1, :], one(ln_g)), (lnrows[1:NE + 1, :], tv_ln_g),
                    (lbrows[0:1, :], one(ln_b)), (lbrows[1:NE + 1, :], tv_ln_b),
                    (g2raw[:, :], gfc2_w), (gbr[:, :], one(gfc2_b)), (gbias[:, :], gfc1_b.rearrange("(c p) -> p c", p=P)),
                    (tvb2[:, :], tv_b2), (b2r[:, :], one(b2)), (b1c[:, :], b1.rearrange("(c p) -> p c", p=P)),
                    (W1raw[:, :, :], W1.rearrange("(c p) d -> p c d", p=P)),
                    (W2raw[:, :, :], W2.rearrange("(c p) f -> p c f", p=P))):
                sp.dma_start(dest, source).then_inc(small_loaded, 16)
            for c in range(FC):
                sp.dma_start(tvb1[:, c, :], tv_b1[:, c * P:(c + 1) * P].rearrange("e p -> p e")
                             ).then_inc(small_loaded, 16)
            sp.wait_ge(graw_turned, 1)
            sp.wait_ge(maxes_made, 2)
            for e in range(NE):
                sp.dma_start(tvW1[:, e], tv_W1[e].rearrange("(c p) d -> p c d", p=P)).then_inc(tv1_loaded, 16)

            def tail_stores(g, j):
                g1, j1 = back(g, j, 1)
                if exists(g1, j1):
                    t, b1 = tile_at(g1, j1), j1 % 2
                    sp.wait_ge(tail.turned_out, t + 1)
                    at_least(sp, tail.turned_kept[b1], 16 * half_at(g1, j1))
                    sp.dma_start(row_tile(zt_rows, t), ztg[:, j1 // Q4, j1 % Q4].rearrange("p a c m -> p (a c m)")
                                 ).then_inc(tail.turned_kept[b1], 16)

            row_ticks(sp, tail_stores, T + 1)
            for b in range(2):
                sp.wait_ge(tail.turned_kept[b], 16 * ((T + 1 - b) // 2))
            sp.wait_ge(gf_done, C * NQ)
            for e in range(NE):
                sp.dma_start(tvW2[:, e], tv_W2[e].rearrange("(c p) f -> p c f", p=P)).then_inc(tv2_loaded, 16)
            sp.wait_ge(w1_done, 1)

            def load_zd(q, b, n):
                sp.dma_start(xd[:, b, 0:n].rearrange("p t a c m -> p t (a c m)"),
                             zt_rows.rearrange("(t p) d -> p t d", p=P)[:, bass.ds(Q4 * q, n), :]
                             ).then_inc(zd_in[b], 16)

            load_zd(0, 0, Q4)
            load_zd(1, 1, Q4)
            sp.wait_ge(bias_split, 3)
            for part in range(3):
                sp.dma_start(b2rows[part:part + 1, :], b216[:, part, :]).then_inc(bias_spread, 16)

            def out_stores(g, j):
                q = quad_at(g, j)
                if j % Q4 == 0 and not (isinstance(q, int) and q + 2 >= NQ):
                    sp.wait_ge(h_done, FC * (q + 1))
                    load_zd(q + 2, j // Q4, 1 if isinstance(q, int) and q + 2 == NQ - 1 else Q4)
                g4, j4 = back(g, j, Q4)
                if exists(g4, j4):
                    t, b = tile_at(g4, j4), j4 % 2
                    sp.wait_ge(ob_made, t + 1)
                    if isinstance(t, int) and t == T - 1:
                        sp.dma_start(out[t * P:N, :], ob[0:LAST, b, :]).then_inc(out_kept[b], 16)
                    else:
                        sp.dma_start(row_tile(out[0:(T - 1) * P, :], t), ob[:, b, :]).then_inc(out_kept[b], 16)

            row_ticks(sp, out_stores, T + Q4)
            for b in range(2):
                sp.wait_ge(out_kept[b], 16 * ((T + 1 - b) // 2))

        @block.scalar
        def _(act):
            for i, a in enumerate((src, dst, edge_weight.bitcast(I32))):
                act.dma_start(packed[0:GFULL, i * EG:(i + 1) * EG],
                              a[0:GFULL * EG].rearrange("(g e) -> g e", e=EG)).then_inc(edges_packed, 16)
                act.dma_start(packed[GFULL:NG, i * EG:i * EG + E - GFULL * EG],
                              a[GFULL * EG:E].rearrange("(g e) -> g e", g=1)).then_inc(edges_packed, 16)
            act.wait_ge(consts_made, 1)
            act.dma_start(packed[GFULL:NG, :].rearrange("g (i e) -> g i e", i=3)[:, :, E - GFULL * EG:EG],
                          pad[:, :, 0:NG * EG - E]).then_inc(edges_packed, 16)
            for k, w16 in enumerate((Wg16, Wk16, Wq16)):
                act.wait_ge(scales_made, 1)
                nc.scalar.activation(w16[:, 0], stage[:, k], ACT.Copy, scale=scf[:, k:k + 1]).then_inc(high_made, 1)

            def deviations(loop, quad, par, n):
                act.wait_ge(loop.vars_made, quad + 1)
                at_least(act, loop.rec, 2 * quad)
                nc.scalar.activation(sd4[:, 0:n], var4[:, par, 0:n, 1], ACT.Sqrt, bias=epsc[:, :]
                                     ).then_inc(loop.std_made, 1)

            def normalise(loop, g, j, dest, high, ring):
                t, b = tile_at(g, j), j % 2
                act.wait_ge(loop.scale_made, quad_at(g, j) + 1)
                at_least(act, loop.low, t - 1)
                if loop is head:
                    at_least(act, m_done, t - ring + 1)
                else:
                    at_least(act, tail.turned, t - ring + 1)
                waited(act)
                for to in (dest[:, b, :], high[:, j % ring, :]):
                    nc.scalar.activation(to, flat(acc, t), ACT.Identity, scale=rs[:, bass.ds(t, 1)],
                                         bias=nb[:, bass.ds(t, 1)]).then_inc(loop.high, 1)
                quad = quad_at(g, j)
                if j % Q4 == 1 and not (isinstance(quad, int) and quad + 1 >= NQ):
                    n = 1 if isinstance(quad, int) and quad + 1 == NQ - 1 else Q4
                    deviations(loop, quad + 1, (j // Q4 + 1) % 2, n)

            def head_tick(g, j):
                g2, j2 = back(g, j, 2)
                t2, b2_ = tile_at(g2, j2), j2 % 2
                if exists(g2, j2):
                    act.wait_ge(y_made, t2 + 1)
                    at_least(act, y_kept[b2_], 16 * half_at(g2, j2))
                    nc.scalar.activation(yb[:, b2_, 0, :], bank[4][:, :], ACT.Copy, scale=cols[:, 0:1]
                                         ).then_inc(y_high, 1)
                if exists(g, j):
                    normalise(head, g, j, xnb, xh, 4)
                if exists(g2, j2):
                    act.wait_ge(f_min, t2 + 1)
                    nc.scalar.activation(mb[:, :], mb[:, :], ACT.Exp, bias=minus1[:, :]).then_inc(f_exp, 1)
                    act.wait_ge(f_used, t2 + 1)
                    at_least(act, m_done, t2 - 1)
                    nc.scalar.activation(kh[:, b2_, :], kf[:, b2_, :], ACT.Copy, scale=scf[:, 5:6]).then_inc(k_high, 1)

            deviations(head, 0, 0, Q4)
            row_ticks(act, head_tick, T + 2)

            def copy_columns(t, b):
                at_least(act, weighted, SA * (t - 1))
                at_least(act, parted, t - 1)
                waited(act)
                nc.scalar.copy(tabc[:, b, :, :], tab[:, bass.ds(SA * t, SA)].rearrange("p s j k -> p (s j) k")
                               ).then_inc(copied, 1)
                act.wait_ge(copied, 2 * t + 1)
                nc.scalar.copy(wh16[:, b, :], tabc[:, b, :, 1]).then_inc(copied, 1)

            def weigh(t, b, r):
                s, at = SA * t + r, (SA * b + r) % OHS
                b = (b + r // SA) % 2
                act.wait_ge(onehot, s + 1)
                at_least(act, stepped, s - OHS + 1)
                for i in range(2):
                    e = 2 * (r % SA) + i
                    for part, w in enumerate((tabc[:, b, e, 1:2], wlo[:, b, e:e + 1])):
                        ins = nc.scalar.activation(hotw[:, at, i, part, :], oneh[:, at, i, :], ACT.Copy, scale=w)
                ins.then_inc(weighted, 1)

            act.wait_ge(tabled, SC)
            copy_columns(0, 0)
            act.wait_ge(m_done, T)
            for c in (1, 3):
                nc.scalar.activation(M32[:, c, :], bank[c][:, :], ACT.Copy, scale=cols[:, 6:7]).then_inc(m_out, 1)
            act.wait_ge(m_turned, 1)
            for c in (1, 3):
                nc.scalar.copy(MT32[:, c, :], bank[c][:, :]).then_inc(mt_out, 1)

            def edge_act(t, h, b):
                first, last = isinstance(t, int) and t == 0, isinstance(t, int) and t == T - 1
                if first:
                    act.wait_ge(ks_done, 1)
                    for r in range(AHEAD):
                        weigh(t, b, r)
                    act.wait_ge(kvp_done, 1)
                    act.wait_ge(kv_out, C + 1)
                    for c in (1, 3):
                        nc.scalar.activation(KVP[:, c, :], bank[c][:, :], ACT.Copy, scale=kinv[:, c:c + 1]
                                             ).then_inc(kvp_out, 1)
                    for r in range(AHEAD, AHEAD + 2):
                        weigh(t, b, r)
                if not last:
                    copy_columns(t + 1, 1 - b)
                act.wait_ge(f_min, T + t + 1)
                nc.scalar.activation(mb[:, :], mb[:, :], ACT.Exp, bias=minus1[:, :]).then_inc(f_exp, 1)
                for r in range(AHEAD + 2 if first else AHEAD, AHEAD + (4 if first else 3)):
                    weigh(t, b, r)
                act.wait_ge(q_scaled, t + 1)
                at_least(act, q_turned, t)
                nc.scalar.activation(qhl[:, 0, :], qs[:, :], ACT.Copy, scale=QS).then_inc(q_high, 1)
                for r in range(AHEAD + (4 if first else 3), SA if last else SA + 2):
                    weigh(t, b, r)
                act.wait_ge(q_turned, t + 1)
                at_least(act, mix_done, t - 1)
                nc.scalar.copy(qT[:, b], turned16(1)).then_inc(q_out, 1)
                if not last:
                    for r in range(SA + 2, SA + AHEAD):
                        weigh(t, b, r)

            edge_tiles(act, edge_act)

            act.wait_ge(edges_done, 1)
            act.wait_ge(scales_made, 2)
            act.wait_ge(graw_turned, 1)
            for f in range(C):
                nc.scalar.activation(G16[:, 0, f, :], bank[2 + f][:, :], ACT.Copy, scale=scf[:, 0:1]
                                     ).then_inc(high_made, 1)

            def tail_tick(g, j):
                if exists(g, j):
                    normalise(tail, g, j, zn, zh, 2)
                g1, j1 = back(g, j, 1)
                if gate_exists(g1, j1):
                    q, m = gate_at(g1, j1)
                    act.wait_ge(gf_done, C * q + m + 1)
                    at_least(act, gf_out, C * q + m)
                    waited(act)
                    n = LAST if isinstance(q, int) and q == NQ - 1 else D
                    nc.scalar.activation(gjunk[:, 0:n], bank[2 + m][:, 0:n], ACT.Relu, scale=cols[:, 0:1],
                                         bias=gbias[:, m:m + 1], accum_out=gsum[:, m, bass.ds(q, 1)]
                                         ).then_inc(gf_out, 1)

            act.wait_ge(small_loaded, 16 * 14)
            deviations(tail, 0, 0, Q4)
            row_ticks(act, tail_tick, Q4 * NQ + 6)
            act.wait_ge(scales_made, 3)
            for f in range(C):
                nc.scalar.activation(W1m[:, 0, f, :], bank[2 + f // 2][:, (f % 2) * F:(f % 2 + 1) * F], ACT.Copy,
                                     scale=scf[:, 1:2]).then_inc(high_made, 1)

            def hidden(q, par, n):
                for o in range(FC):
                    act.wait_ge(h_done, FC * q + o + 1)
                    if not (isinstance(q, int) and q < 2):
                        act.wait_ge(o_done, Q4 * (q - 1))
                    nc.scalar.activation(hT[:, par, o, 0:n], bank[2 + o][:, 0:n], ACT.Relu, scale=cols[:, 1:2],
                                         bias=b1m[:, o:o + 1]).then_inc(h_out, 1)

            def out_tick(g, j):
                quad = quad_at(g, j)
                if exists(g, j):
                    t, b = tile_at(g, j), j % 2
                    at_least(act, res_made, t - 1)
                    waited(act)
                    nc.scalar.activation(zq[:, b, :], flat(acc, t), ACT.Identity, scale=rs[:, bass.ds(t, 1)],
                                         bias=nb[:, bass.ds(t, 1)]).then_inc(zq_made, 1)
                if j % Q4 == 0 and not (isinstance(quad, int) and quad == 0):
                    n = 1 if isinstance(quad, int) and quad == NQ else Q4
                    act.wait_ge(two_made, quad)
                    at_least(act, r_rec, quad - 1)
                    nc.scalar.activation(sd4[:, 0:n], var4[:, (j // Q4 + 1) % 2, 0:n, 1], ACT.Sqrt, bias=epsc[:, :]
                                         ).then_inc(r_std, 1)
                if j % Q4 == 1 and not (isinstance(quad, int) and quad + 1 >= NQ):
                    hidden(quad + 1, (j // Q4 + 1) % 2, P if isinstance(quad, int) and quad + 1 == NQ - 1 else Q4 * P)
                g4, j4 = back(g, j, Q4)
                if exists(g4, j4):
                    t, b = tile_at(g4, j4), j4 % 2
                    act.wait_ge(r_scale, quad_at(g4, j4) + 1)
                    at_least(act, ob_made, t - 1)
                    nc.scalar.activation(zr[:, b, :], res[:, j4, :], ACT.Identity, scale=rsr[:, j4 // Q4, j4 % Q4:j4 % Q4 + 1],
                                         bias=nbr[:, j4 // Q4, j4 % Q4:j4 % Q4 + 1]).then_inc(zr_made, 1)

            act.wait_ge(bias_split, 3)
            hidden(0, 0, Q4 * P)
            row_ticks(act, out_tick, T + Q4)

        @block.gpsimd
        def _(pool):
            pool.memset(ident[:, :], 0.0).then_inc(pool_set, 1)
            pool.memset(ident16[:, :], 0.0).then_inc(pool_set, 1)
            pool.memset(ones[:, :], 1.0).then_inc(pool_set, 1)
            pool.memset(ones3[:, :], 1.0).then_inc(pool_set, 1)
            pool.memset(headmask[:, :], 0.0).then_inc(pool_set, 1)
            pool.memset(epsc[:, :], EPS).then_inc(pool_set, 1)
            pool.memset(minus1[:, :], -1.0).then_inc(pool_set, 1)
            pool.memset(acc[:, T - 1, :], 0.0).then_inc(pool_set, 1)
            pool.memset(pad[:, 0, :], 0).then_inc(pool_set, 1)
            pool.memset(pad[:, 1, :], int(OUTSIDE)).then_inc(pool_set, 1)
            pool.memset(pad[:, 2, :], 0).then_inc(pool_set, 1)
            pool.iota(stepi[:, :], pattern=[[P, SC]], base=0, channel_multiplier=1).then_inc(pool_set, 1)
            pool.iota(iota16[:, :], pattern=[[1, P]], base=0, channel_multiplier=0,
                      allow_small_or_imprecise_dtypes=True).then_inc(pool_set, 1)
            pool.iota(irow[:, :], pattern=[[1, NG]], base=0, channel_multiplier=0).then_inc(pool_set, 1)
            pool.wait_ge(pool_set, 14)
            for m in (ident, ident16):
                pool.affine_select(out=m[:, :], in_=m[:, :], compare_op=ALU.not_equal, fill=1.0, base=0,
                                   pattern=[[-1, P]], channel_multiplier=1).then_inc(pool_set, 1)
            pool.wait_ge(pool_set, 16)
            for b in range(2):
                pool.memset(headmask[b * HD:(b + 1) * HD, b * HD:(b + 1) * HD], 1.0).then_inc(pool_set, 1)
            pool.wait_ge(pool_set, 18)
            pool.nop(nofuse=True).then_inc(consts_made, 1)

            pool.wait_ge(maxes_made, 1)
            pool.partition_all_reduce(mxa[:, 0:6], mx[:, 0:6], P, RMAX).then_inc(maxes_all, 1)
            pool.partition_all_reduce(uns[:, :], viol[:, :], P, RADD).then_inc(maxes_all, 1)

            pool.wait_ge(groups_made, 1)
            pool.wait_ge(edges_packed, 16 * 7)
            for n in range(SC):
                at_least(pool, turned, n)
                at_least(pool, picked, n)
                pool.indirect_dma_start(out=pk[:, :, :].rearrange("p i e -> p (i e)"), out_offset=None, in_=packed,
                                        in_offset=bass.IndirectOffsetOnAxis(ap=gidx[:, n:n + 1], axis=0)
                                        ).then_inc(pk_ready, 16)

            pool.wait_ge(bias_spread, 16 * 6)
            pool.memset(ksacc[:, :], 0.0).then_inc(pool_set, 1)
            pool.wait_ge(pool_set, 19)

            def sum_k(g, j):
                g2, j2 = back(g, j, 2)
                if exists(g2, j2):
                    t, b = tile_at(g2, j2), j2 % 2
                    n = LAST if isinstance(t, int) and t == T - 1 else P
                    pool.wait_ge(f_used, t + 1)
                    at_least(pool, k_summed, t)
                    waited(pool)
                    pool.tensor_tensor(ksacc[0:n, :], ksacc[0:n, :], kf[0:n, b, :], ALU.add).then_inc(k_summed, 1)

            row_ticks(pool, sum_k, T + 2)

            pool.wait_ge(high_made, 3)
            pool.wait_ge(low_made, 3)
            pool.memset(fill[:, :], 0.0).then_inc(pool_set, 1)
            pool.wait_ge(pool_set, 20)
            head_kept(pool)
            pool.wait_ge(m_done, T)
            limit = pool.to_reg(T * P - 1)

            def gather(slot, column):
                pool.indirect_dma_start(out=rows[:, slot].rearrange("p a d -> p (a d)"), out_offset=None, in_=y_rows,
                                        in_offset=bass.IndirectOffsetOnAxis(ap=column, axis=0),
                                        bounds_check=limit, oob_is_err=False).then_inc(gathered[slot], 16)

            def edge_gathers(t, h, b):
                pool.tensor_copy(idxc[:, b, :], idx[:, bass.ds(SA * t, SA), :].rearrange("p s j -> p (s j)")
                                 ).then_inc(indexed, 1)
                pool.wait_ge(indexed, t + 1)
                for r in range(SA):
                    at_least(pool, stepped, SA * t + r - RING + 1)
                    waited(pool)
                    slot = 2 * place(h, b, r)[0]
                    for i in range(2):
                        gather(slot + i, idxc[:, b, 2 * r + i:2 * r + i + 1])

            pool.wait_ge(tabled, SC)
            edge_tiles(pool, edge_gathers)

            pool.wait_ge(edge_added, SA * T)
            unordered = pool.value_load(flag[0:1, 0:1], min_val=0, max_val=1)
            with pool.If(unordered > 0):
                with pool.Fori(0, NG) as n:
                    pool.wait_ge(u_group, n + 1)
                    waited(pool)
                    pool.indirect_dma_start(out=pk[:, :, :].rearrange("p i e -> p (i e)"), out_offset=None, in_=packed,
                                            in_offset=bass.IndirectOffsetOnAxis(ap=gidx[:, 0:1], axis=0)
                                            ).then_inc(u_pk, 16)
                    pool.wait_ge(u_index, n + 1)
                    waited(pool)
                    for i in range(2):
                        pool.indirect_dma_start(
                            out=rows[:, i].rearrange("p a d -> p (a d)"), out_offset=None, in_=y_rows,
                            in_offset=bass.IndirectOffsetOnAxis(ap=idxc[:, 0, i:i + 1], axis=0),
                            bounds_check=limit, oob_is_err=False).then_inc(u_gathered, 16)

            pool.wait_ge(maxes_made, 2)
            pool.partition_all_reduce(mxa[:, 0:1], mx[:, 0:1], P, RMAX).then_inc(maxes_all, 1)
            pool.wait_ge(maxes_made, 3)
            pool.partition_all_reduce(mxa[:, 1:2], mx[:, 1:2], P, RMAX).then_inc(maxes_all, 1)

            def out_tick(g, j):
                if exists(g, j):
                    t = tile_at(g, j)
                    pool.wait_ge(zq_made, t + 1)
                    waited(pool)
                    pool.tensor_tensor(flat(acc, t), flat(acc, t), lnbb[:, :], ALU.add).then_inc(based, 1)
                g4, j4 = back(g, j, Q4)
                if exists(g4, j4):
                    t, b = tile_at(g4, j4), j4 % 2
                    pool.wait_ge(gained, t + 1)
                    pool.wait_ge(based, t + 1)
                    at_least(pool, out_kept[b], 16 * half_at(g4, j4))
                    waited(pool)
                    pool.tensor_tensor(ob[:, b, :], zr[:, b, :], flat(acc, t), ALU.add).then_inc(ob_made, 1)

            row_ticks(pool, out_tick, T + Q4)

        @block.vector
        def _(dve):
            links = [0]

            def link(ins):
                links[0] += 1
                ins.then_inc(chain, 1)
                dve.wait_ge(chain, links[0])

            def powers(first, n, link):
                s = slice(first, first + n)
                link(nc.vector.tensor_scalar(mxa[:, s], mxa[:, s], 1e-30, None, ALU.max))
                link(nc.vector.tensor_scalar(pw[:, s], mxa[:, s].bitcast(I32), EXPONENT, None, ALU.bitwise_and))
                link(nc.vector.tensor_scalar(sc[:, s], pw[:, s], -1.0, float(268 << 23), ALU.mult, ALU.add))
                link(nc.vector.tensor_scalar(inv[:, s], sc[:, s], -1.0, float(254 << 23), ALU.mult, ALU.add))

            def pick(gate, negtile, link, ready, count, path=True):
                dve.wait_ge(ready, count)
                link(nc.vector.tensor_scalar(rel[:, :], pk[:, 1, :], negtile, None, ALU.add))
                link(nc.vector.tensor_scalar(ok[:, :], rel[:, :], 0.0, gate, ALU.is_ge, ALU.mult))
                link(nc.vector.scalar_tensor_tensor(out=ok[:, :], in0=rel[:, :], scalar=float(P), in1=ok[:, :],
                                                    op0=ALU.is_lt, op1=ALU.mult))
                link(nc.vector.tensor_scalar(ok[:, :], ok[:, :], -OUTSIDE, OUTSIDE, ALU.mult, ALU.add))
                if path:
                    link(nc.vector.tensor_tensor(srcf[:, :], pk[:, 0, :], ok[:, :], ALU.add))
                else:
                    link(nc.vector.tensor_copy(srcf[:, :], pk[:, 0, :]))
                link(nc.vector.tensor_tensor(rel[:, :], rel[:, :], ok[:, :], ALU.add))

            def tabulate(s, link):
                span = slice(s, s + P)
                link(nc.vector.tensor_copy(idx[:, span, :].rearrange("p s j -> p j s"), by_half(bank[4][:, 0:EG])))
                link(nc.vector.tensor_copy(tab[:, span, :, 0].rearrange("p s j -> p j s"), by_half(bank[4][:, EG:2 * EG])))
                link(nc.vector.tensor_scalar(tab[:, span, :, 1].rearrange("p s j -> p j s"), by_half(bank[5][:, 0:EG]),
                                             scf[:, 3:4], None, ALU.mult))

            link(nc.vector.memset(mx[:, :], 0.0))
            link(nc.vector.memset(viol[:, :], 0.0))
            for k in range(3):
                dve.wait_ge(w_loaded[k], 16)
                link(nc.vector.tensor_reduce(mx[:, k:k + 1], stage[:, k].rearrange("p c n -> p (c n)"), AX_X, ALU.max,
                                             apply_absolute_value=True))
            dve.wait_ge(bias_loaded, 16 * 5)
            link(nc.vector.tensor_reduce(mx[0:1, 5:6], brow[:, 0, :], AX_X, ALU.max, apply_absolute_value=True))
            dve.wait_ge(edges_loaded, 64)
            link(nc.vector.tensor_reduce(mx[0:DR, 3:4], ews[0:DR, :], AX_X, ALU.max, apply_absolute_value=True))
            link(nc.vector.tensor_tensor(ews[0:DR, :], dsts[0:DR, 1:DW + 1], dsts[0:DR, 0:DW], ALU.is_lt))
            nc.vector.tensor_reduce(viol[0:DR, :], ews[0:DR, :], AX_X, ALU.add).then_inc(maxes_made, 1)

            dve.wait_ge(start_loaded, 16)
            dve.wait_ge(consts_made, 1)
            link(nc.vector.tensor_scalar(srow[:, :], srow[:, :], 7, None, ALU.logical_shift_right))
            link(nc.vector.tensor_copy(srowf[:, :], srow[:, :]))
            link(nc.vector.memset(srowf[:, 0:1], 0.0))
            nc.vector.tensor_tensor(srowf[:, :], srowf[:, :], irow[:, :], ALU.add).then_inc(start_made, 1)

            dve.wait_ge(maxes_all, 2)
            link(nc.vector.tensor_scalar(mxa[:, 4:5], mxa[:, 0:1], float(D), None, ALU.mult))
            link(nc.vector.tensor_scalar(mxa[:, 5:6], mxa[:, 5:6], 1.0, None, ALU.add))
            link(nc.vector.scalar_tensor_tensor(out=mxa[:, 5:6], in0=mxa[:, 1:2], scalar=float(D), in1=mxa[:, 5:6],
                                                op0=ALU.mult, op1=ALU.add))
            powers(0, 6, link)
            scale = 1.0 / XS
            link(nc.vector.tensor_scalar(cols[:, 0:1], invf[:, 0:1], scf[:, 4:5], scale, ALU.mult, ALU.mult))
            link(nc.vector.tensor_scalar(cols[:, 1:3], invf[:, 1:3], scale, None, ALU.mult))
            link(nc.vector.tensor_tensor(cols[:, 3:4], invf[:, 3:4], invf[:, 4:5], ALU.mult))
            link(nc.vector.tensor_scalar(cols[:, 4:6], scf[:, 1:3], XS, None, ALU.mult))
            link(nc.vector.tensor_scalar(cols[:, 6:7], invf[:, 5:6], scale, None, ALU.mult))
            link(nc.vector.tensor_scalar(uns[:, :], uns[:, :], 1.0, None, ALU.min))
            link(nc.vector.tensor_scalar(srt[:, :], uns[:, :], -1.0, 1.0, ALU.mult, ALU.add))
            link(nc.vector.tensor_copy(flag[:, :], uns[0:1, :]))
            nc.vector.tensor_copy(stepf[:, :], stepi[:, :]).then_inc(scales_made, 1)

            dve.wait_ge(start_spread, 1)
            link(nc.vector.tensor_copy(startb[:, :], bank[4][:, 0:NG]))
            dve.wait_ge(scales_made, 1)
            for c in range(SC):
                link(nc.vector.tensor_scalar(junk[:, :], startb[:, :], stepf[:, c:c + 1], None, ALU.is_le, ALU.add,
                                             accum_out=cnt[:, c:c + 1]))
            link(nc.vector.tensor_tensor(ntile[:, :], stepf[:, :], cnt[:, :], ALU.subtract))
            link(nc.vector.tensor_scalar(ntile[:, :], ntile[:, :], 1.0, None, ALU.add))
            link(nc.vector.tensor_scalar(late[:, :], ntile[:, :], float(T - 1), -OUTSIDE, ALU.is_gt, ALU.mult))
            link(nc.vector.scalar_tensor_tensor(out=negd[:, :], in0=ntile[:, :], scalar=-float(P), in1=late[:, :],
                                                op0=ALU.mult, op1=ALU.add))
            link(nc.vector.tensor_scalar(ntile[:, :], ntile[:, :], float(T - 1), 0.0, ALU.min, ALU.max))
            nc.vector.tensor_scalar(gidx[:, :], cnt[:, :], -1.0, None, ALU.add).then_inc(groups_made, 1)
            dve.wait_ge(tiles_turned, 1)
            link(nc.vector.tensor_copy(tileof[:, :], bank[5][0:1, :]))

            for k, w16 in enumerate((Wg16, Wk16, Wq16)):
                dve.wait_ge(high_made, k + 1)
                nc.vector.scalar_tensor_tensor(out=w16[:, 1], in0=stage[:, k], scalar=scf[:, k:k + 1], in1=w16[:, 0],
                                               op0=ALU.mult, op1=ALU.subtract).then_inc(low_made, 1)

            def split(row, dest, link):
                link(nc.vector.tensor_copy(dest[:, 0, :], row[:, :]))
                link(nc.vector.tensor_tensor(row[:, :], row[:, :], dest[:, 0, :], ALU.subtract))
                link(nc.vector.tensor_copy(dest[:, 1, :], row[:, :]))
                link(nc.vector.tensor_tensor(row[:, :], row[:, :], dest[:, 1, :], ALU.subtract))
                return nc.vector.tensor_copy(dest[:, 2, :], row[:, :])

            for r in range(2):
                link(nc.vector.tensor_scalar(bf[:, :], brow[:, r, :], 1.0, cols[0:1, 4 + r:5 + r], ALU.add, ALU.mult))
                split(bf, b16[:, r], link).then_inc(bias_split, 1)
                dve.wait_ge(bias_split, r + 1)
            link(nc.vector.tensor_tensor(mrow[:, :], brow[:, 2, :], brow[:, 3, :], ALU.add))
            link(nc.vector.tensor_scalar(mrow[:, :], mrow[:, :], 1.0 / H, None, ALU.mult))

            for n in range(SC):
                pick(srt[:, 0:1], negd[:, n:n + 1], link, pk_ready, 16 * (n + 1))
                dve.nop(nofuse=True).then_inc(picked, 1)
                dve.wait_ge(turned, n + 1)
                tabulate(n * P, link)
                dve.nop(nofuse=True).then_inc(tabled, 1)

            def statistics(loop, quad, par, n):
                at_least(dve, loop.vars_made, quad)
                for i in range(n):
                    if loop is head:
                        dve.wait_ge(x_loaded[i], 16 * (quad + 1))
                    waited(dve)
                    nc.vector.bn_stats(st6[:, i, :], flat(acc, Q4 * quad + i)).then_inc(loop.six, 1)
                dve.wait_ge(loop.six, Q4 * quad + n)
                waited(dve)
                for i in range(n):
                    ins = nc.vector.bn_aggr(var4[:, par, i, :], st6[:, i, :])
                ins.then_inc(loop.vars_made, 1)

            def scales(loop, quad, par, n):
                s = bass.ds(Q4 * quad, n)
                dve.wait_ge(loop.std_made, quad + 1)
                nc.vector.reciprocal(rs[:, s], sd4[:, 0:n]).then_inc(loop.rec, 1)
                dve.wait_ge(loop.rec, 2 * quad + 1)
                nc.vector.tensor_scalar(rs[:, s], rs[:, s], XS, None, ALU.mult).then_inc(loop.rec, 1)
                dve.wait_ge(loop.rec, 2 * quad + 2)
                nc.vector.scalar_tensor_tensor(out=nb[:, s], in0=var4[:, par, 0:n, 0], scalar=-1.0, in1=rs[:, s],
                                               op0=ALU.mult, op1=ALU.mult).then_inc(loop.scale_made, 1)

            def group_work(loop, g, j, what, at):
                quad = quad_at(g, j)
                if j % Q4 == at and not (isinstance(quad, int) and quad + 1 >= NQ):
                    what(loop, quad + 1, (j // Q4 + 1) % 2, 1 if isinstance(quad, int) and quad + 1 == NQ - 1 else Q4)

            def low_parts(loop, g, j, full, high, dest, ring):
                t = tile_at(g, j)
                dve.wait_ge(loop.high, 2 * t + 2)
                if loop is head:
                    at_least(dve, m_done, t - ring + 1)
                else:
                    at_least(dve, tail.turned, t - ring + 1)
                nc.vector.tensor_tensor(dest[:, j % ring, :], full[:, j % 2, :], high[:, j % ring, :], ALU.subtract
                                        ).then_inc(loop.low, 1)

            def head_tick(g, j):
                group_work(head, g, j, statistics, 0)
                g2, j2 = back(g, j, 2)
                t2, b2_ = tile_at(g2, j2), j2 % 2
                if exists(g2, j2):
                    dve.wait_ge(y_high, t2 + 1)
                    at_least(dve, y_kept[b2_], 16 * half_at(g2, j2))
                    nc.vector.scalar_tensor_tensor(out=yb[:, b2_, 1, :], in0=bank[4][:, :], scalar=cols[:, 0:1],
                                                   in1=yb[:, b2_, 0, :], op0=ALU.mult, op1=ALU.subtract
                                                   ).then_inc(y_low, 1)
                    dve.wait_ge(f_done, t2 + 1)
                    at_least(dve, f_used, t2)
                    nc.vector.tensor_scalar(mb[:, :], bank[5][:, :], cols[:, 1:2], 1.0, ALU.mult, ALU.min).then_inc(f_min, 1)
                if exists(g, j):
                    low_parts(head, g, j, xnb, xh, xl, 4)
                if exists(g2, j2):
                    dve.wait_ge(f_exp, t2 + 1)
                    at_least(dve, k_high, t2 - 1)
                    at_least(dve, k_low, t2 - 1)
                    at_least(dve, k_summed, t2 - 1)
                    nc.vector.scalar_tensor_tensor(out=kf[:, b2_, :], in0=bank[5][:, :], scalar=cols[:, 1:2], in1=mb[:, :],
                                                   op0=ALU.mult, op1=ALU.max).then_inc(f_used, 1)
                g1, j1 = back(g, j, 1)
                if exists(g1, j1):
                    t, b = tile_at(g1, j1), j1 % 2
                    dve.wait_ge(head.turned, t + 1)
                    at_least(dve, f_done, t - 1)
                    at_least(dve, head.turned_kept[b], 16 * half_at(g1, j1))
                    nc.vector.tensor_copy(xtb[:, b], turned16(6 + b)).then_inc(head.turned_out, 1)
                if exists(g2, j2):
                    dve.wait_ge(k_high, t2 + 1)
                    at_least(dve, m_done, t2 - 1)
                    nc.vector.scalar_tensor_tensor(out=kl[:, b2_, :], in0=kf[:, b2_, :], scalar=scf[:, 5:6],
                                                   in1=kh[:, b2_, :], op0=ALU.mult, op1=ALU.subtract).then_inc(k_low, 1)
                group_work(head, g, j, scales, 2)

            statistics(head, 0, 0, Q4)
            dve.wait_ge(bias_spread, 16 * 6)
            scales(head, 0, 0, Q4)
            row_ticks(dve, head_tick, T + 2)

            def low_weights(t, b):
                dve.wait_ge(copied, 2 * t + 2)
                nc.vector.tensor_tensor(wlo[:, b, :], tabc[:, b, :, 1], wh16[:, b, :], ALU.subtract).then_inc(parted, 1)

            def hot(t, b, r):
                s, at = SA * t + r, (SA * b + r) % OHS
                b = (b + r // SA) % 2
                at_least(dve, weighted, s - OHS + 1)
                for i in range(2):
                    e = 2 * (r % SA) + i
                    ins = nc.vector.tensor_scalar(oneh[:, at, i, :], iota16[:, :], tabc[:, b, e, 0:1], None, ALU.is_equal)
                ins.then_inc(onehot, 1)

            def add_step(t, b, r):
                s = SA * t + r
                tile = dve.value_load(tileof[0:1, bass.ds(s, 1)], min_val=0, max_val=T - 1)
                dve.wait_ge(stepped, s + 1)
                at_least(dve, edge_added, s)
                at_least(dve, mix_added, t)
                waited(dve)
                nc.vector.scalar_tensor_tensor(out=flat(acc, tile), in0=step_bank(b, r)[:, :],
                                               scalar=cols[:, 3:4], in1=flat(acc, tile), op0=ALU.mult, op1=ALU.add
                                               ).then_inc(edge_added, 1)

            def add_mix(t, b):
                dve.wait_ge(mix_done, t + 1)
                dve.wait_ge(edge_added, SA * (t + 1))
                waited(dve)
                nc.vector.scalar_tensor_tensor(out=flat(acc, t), in0=bank[2 + b][:, :], scalar=cols[:, 7:8],
                                               in1=flat(acc, t), op0=ALU.mult, op1=ALU.add).then_inc(mix_added, 1)

            by_head = lambda ap: ap.rearrange("p (h d) -> p h d", h=H)

            def q_least(t):
                dve.wait_ge(f_done, T + t + 1)
                dve.wait_ge(f_used, T + t)
                nc.vector.tensor_scalar(mb[:, :], bank[0][:, :], cols[:, 2:3], 1.0, ALU.mult, ALU.min).then_inc(f_min, 1)

            def q_whole(t):
                dve.wait_ge(f_exp, T + t + 1)
                if isinstance(t, int) and t == 0:
                    dve.wait_ge(k_summed, T)
                nc.vector.scalar_tensor_tensor(out=kf[:, 0, :], in0=bank[0][:, :], scalar=cols[:, 2:3], in1=mb[:, :],
                                               op0=ALU.mult, op1=ALU.max).then_inc(f_used, 1)

            def q_times_sum(t):
                dve.wait_ge(f_used, T + t + 1)
                at_least(dve, q_scaled, t)
                nc.vector.tensor_tensor(qk[:, :], kf[:, 0, :], ksb[:, :], ALU.mult).then_inc(q_summed, 1)

            def q_sums(t):
                dve.wait_ge(q_summed, 3 * t + 1)
                nc.vector.tensor_reduce(den[:, :], by_head(qk[:, :]), AX_X, ALU.add).then_inc(q_summed, 1)

            def q_inverse(t):
                dve.wait_ge(q_summed, 3 * t + 2)
                nc.vector.reciprocal(rden[:, :], den[:, :]).then_inc(q_summed, 1)

            def q_share(t):
                dve.wait_ge(q_summed, 3 * t + 3)
                at_least(dve, q_low, t)
                nc.vector.tensor_tensor(by_head(qs[:, :]), by_head(qk[:, :]),
                                        rden[:, :].rearrange("p (h d) -> p h d", d=1).broadcast_to([P, H, HD]), ALU.mult
                                        ).then_inc(q_scaled, 1)

            def q_lower(t):
                dve.wait_ge(q_high, t + 1)
                at_least(dve, q_turned, t)
                nc.vector.scalar_tensor_tensor(out=qhl[:, 1, :], in0=qs[:, :], scalar=QS, in1=qhl[:, 0, :],
                                               op0=ALU.mult, op1=ALU.subtract).then_inc(q_low, 1)

            def kv_parts():
                dve.wait_ge(kvp_done, 1)
                for c in (0, 2):
                    nc.vector.tensor_scalar(KVP[:, c, :], bank[c][:, :], kinv[:, c:c + 1], None, ALU.mult
                                            ).then_inc(kvp_out, 1)
                dve.wait_ge(kvp_out, C)
                nc.vector.tensor_reduce(mx[:, 6:7], KVP[:, :, :].rearrange("p c n -> p (c n)"), AX_X, ALU.max,
                                        apply_absolute_value=True).then_inc(kmax_row, 1)
                dve.wait_ge(kmax_turned, 1)
                nc.vector.tensor_reduce(mx[0:1, 7:8], bank[5][0:1, 0:P], AX_X, ALU.max).then_inc(kmax_row, 1)
                dve.wait_ge(kmax_spread, 1)
                link(nc.vector.tensor_copy(mxa[:, 6:7], bank[5][:, P:P + 1]))
                powers(6, 1, link)
                link(nc.vector.tensor_scalar(cols[:, 7:8], invf[:, 6:7], 1.0 / QS, None, ALU.mult))
                for c in range(C):
                    link(nc.vector.tensor_scalar(KVP16[:, 0, c, :], KVP[:, c, :], scf[:, 6:7], None, ALU.mult))
                    nc.vector.scalar_tensor_tensor(out=KVP16[:, 1, c, :], in0=KVP[:, c, :], scalar=scf[:, 6:7],
                                                   in1=KVP16[:, 0, c, :], op0=ALU.mult, op1=ALU.subtract
                                                   ).then_inc(kvp_low, 1)

            dve.wait_ge(ks_done, 1)
            link(nc.vector.tensor_copy(ksb[:, :], bank[4][:, :]))
            link(nc.vector.tensor_scalar(kinv[:, :], bank[5][:, 0:C], 1e-30, None, ALU.max))
            nc.vector.reciprocal(kinv[:, :], kinv[:, :]).then_inc(kv_out, 1)
            dve.wait_ge(m_done, T)
            for c in (0, 2):
                nc.vector.tensor_scalar(M32[:, c, :], bank[c][:, :], cols[:, 6:7], None, ALU.mult).then_inc(m_out, 1)
            dve.wait_ge(m_turned, 1)
            for c in (0, 2):
                nc.vector.tensor_copy(MT32[:, c, :], bank[c][:, :]).then_inc(mt_out, 1)
            low_weights(0, 0)
            dve.wait_ge(k_low, T)
            for r in range(AHEAD):
                hot(0, 0, r)
            dve.wait_ge(kv_done, 1)
            for c in range(C):
                nc.vector.tensor_tensor(kvt[:, c, :], bank[4][:, c * P:(c + 1) * P], headmask[:, :], ALU.mult
                                        ).then_inc(kv_out, 1)

            def edge_dve(t, h, b):
                last = isinstance(t, int) and t == T - 1
                add, ahead = lambda r: add_step(t, b, r), lambda r: hot(t, b, r + AHEAD)
                if isinstance(t, int) and t == 0:
                    add(0)
                    add(1)
                    ahead(0)
                    ahead(1)
                    kv_parts()
                    q_least(t)
                    add(2)
                    q_whole(t)
                    ahead(2)
                    q_times_sum(t)
                    add(3)
                    q_sums(t)
                    ahead(3)
                    q_inverse(t)
                    q_share(t)
                    ahead(4)
                    add(4)
                    q_lower(t)
                else:
                    add_mix(t - 1, 1 - b)
                    q_least(t)
                    ahead(0)
                    add(0)
                    q_whole(t)
                    ahead(1)
                    q_times_sum(t)
                    add(1)
                    q_sums(t)
                    ahead(2)
                    q_inverse(t)
                    add(2)
                    q_share(t)
                    ahead(3)
                    add(3)
                    q_lower(t)
                    ahead(4)
                    add(4)
                if not last:
                    low_weights(t + 1, 1 - b)
                for r in range(5, SA):
                    if not last:
                        ahead(r)
                    add(r)

            edge_tiles(dve, edge_dve)
            add_mix(T - 1, (T - 1) % 2)
            dve.wait_ge(mix_added, T)

            unordered = dve.value_load(flag[0:1, 0:1], min_val=0, max_val=1)
            with dve.If(unordered > 0):
                K = 11

                def linked(n):
                    k = [0]

                    def one(ins):
                        k[0] += 1
                        ins.then_inc(u_chain, 1)
                        dve.wait_ge(u_chain, K * n + k[0])
                    return one, k

                nc.vector.tensor_scalar(negd[:, 0:1], stepf[:, 0:1], -float(P), None, ALU.mult).then_inc(u_start, 1)
                nc.vector.memset(cnt[:, 0:1], 0.0).then_inc(u_start, 1)
                dve.wait_ge(u_start, 2)
                with dve.Fori(0, NG) as n:
                    one, k = linked(n)
                    one(nc.vector.tensor_copy(gidx[:, 0:1], cnt[:, 0:1]))
                    one(nc.vector.tensor_scalar(cnt[:, 0:1], cnt[:, 0:1], 1.0, None, ALU.add))
                    dve.nop(nofuse=True).then_inc(u_group, 1)
                    pick(1.0, negd[:, 0:1], one, u_pk, 16 * n + 16, path=False)
                    dve.nop(nofuse=True).then_inc(u_picked, 1)
                    dve.wait_ge(u_turned, n + 1)
                    tabulate(0, one)
                    assert k[0] == K
                    nc.vector.tensor_copy(idxc[:, 0, 0:2], idx[:, 0, :]).then_inc(u_index, 1)
                    with dve.Fori(0, T) as d:
                        s = T * n + d
                        waited(dve)
                        nc.vector.tensor_copy(tabc[:, 0, 0:2, :], tab[:, bass.ds(d, 1)].rearrange("p s j k -> p (s j) k")
                                              ).then_inc(u_onehot, 1)
                        dve.wait_ge(u_onehot, U_HOT * s + 1)
                        nc.vector.tensor_copy(wh16[:, 0, 0:2], tabc[:, 0, 0:2, 1]).then_inc(u_onehot, 1)
                        dve.wait_ge(u_onehot, U_HOT * s + 2)
                        nc.vector.tensor_tensor(wlo[:, 0, 0:2], tabc[:, 0, 0:2, 1], wh16[:, 0, 0:2], ALU.subtract
                                                ).then_inc(u_onehot, 1)
                        dve.wait_ge(u_onehot, U_HOT * s + 3)
                        for i in range(2):
                            for part, w in enumerate((tabc[:, 0, i, 1:2], wlo[:, 0, i:i + 1])):
                                ins = nc.vector.tensor_scalar(hotw[:, 0, i, part, :], iota16[:, :], tabc[:, 0, i, 0:1],
                                                              w, ALU.is_equal, ALU.mult)
                        ins.then_inc(u_onehot, 1)
                        dve.wait_ge(u_stepped, s + 1)
                        waited(dve)
                        nc.vector.scalar_tensor_tensor(out=flat(acc, d), in0=bank[6][:, :], scalar=cols[:, 3:4],
                                                       in1=flat(acc, d), op0=ALU.mult, op1=ALU.add).then_inc(u_added, 1)
                        dve.wait_ge(u_added, s + 1)
                        waited(dve)
            dve.nop(nofuse=True).then_inc(edges_done, 1)

            dve.wait_ge(graw_loaded, 16)
            nc.vector.tensor_reduce(mx[:, 0:1], graw[:, :, :].rearrange("p c n -> p (c n)"), AX_X, ALU.max,
                                    apply_absolute_value=True).then_inc(maxes_made, 1)
            statistics(tail, 0, 0, Q4)
            link(nc.vector.memset(lncoef[:, :], LN_MERGE))
            nc.vector.memset(lncoef[0:1, :], 1.0 - LN_MERGE * NE).then_inc(ln_coefs, 1)
            dve.wait_ge(maxes_all, 3)
            powers(0, 1, link)
            nc.vector.tensor_scalar(cols[:, 0:1], invf[:, 0:1], 1.0 / XS, None, ALU.mult).then_inc(scales_made, 1)
            scales(tail, 0, 0, Q4)
            for f in range(C):
                dve.wait_ge(high_made, 3 + f + 1)
                nc.vector.scalar_tensor_tensor(out=G16[:, 1, f, :], in0=bank[2 + f][:, :], scalar=scf[:, 0:1],
                                               in1=G16[:, 0, f, :], op0=ALU.mult, op1=ALU.subtract).then_inc(low_made, 1)
            dve.wait_ge(ln_done, 2)
            nc.vector.tensor_copy(lngb[:, :], bank[6][:, :]).then_inc(ln_out, 1)
            nc.vector.tensor_copy(lnbb[:, :], bank[7][:, :]).then_inc(ln_out, 1)
            dve.wait_ge(g2_turned, 1)
            nc.vector.tensor_copy(g2T[:, :, :].rearrange("p c e -> p (c e)"), bank[6][:, 0:C * NE]).then_inc(g2_out, 1)

            def tail_tick(g, j):
                group_work(tail, g, j, statistics, 0)
                if exists(g, j):
                    low_parts(tail, g, j, zn, zh, zl, 2)
                g1, j1 = back(g, j, 1)
                if exists(g1, j1):
                    t, b = tile_at(g1, j1), j1 % 2
                    dve.wait_ge(tail.turned, t + 1)
                    free_group(dve, g1, j1)
                    nc.vector.tensor_copy(ztg[:, j1 // Q4, j1 % Q4], turned16(b)).then_inc(tail.turned_out, 1)
                group_work(tail, g, j, scales, 2)

            row_ticks(dve, tail_tick, T + 1)

            dve.wait_ge(gf_out, C * NQ)
            link(nc.vector.tensor_reduce(gsq[:, :], gsum[:, :, :], AX_X, ALU.add))
            link(nc.vector.tensor_scalar(gcol[:, :], gsq[:, :], 1.0 / N, None, ALU.mult))
            for c in range(C):
                nc.vector.tensor_scalar(geye[:, c, :], ones[:, :], gcol[:, c:c + 1], None, ALU.mult).then_inc(gate_in, 1)
            dve.wait_ge(gate_done, 2)
            link(nc.vector.tensor_copy(gall[:, :], bank[6][:, 0:NE]))
            link(nc.vector.tensor_copy(gT[:, :], bank[6][0:NE, NE:NE + 1]))
            for e in range(NE):
                nc.vector.tensor_scalar(geye[:, e, :], ident[:, :], gall[:, e:e + 1], None, ALU.mult).then_inc(gate_out, 1)
            for o in range(FC):
                link(nc.vector.tensor_tensor(tvb1[:, o, :], tvb1[:, o, :], gall[:, :], ALU.mult))
            link(nc.vector.tensor_reduce(b1m[:, :], tvb1[:, :, :], AX_X, ALU.add))
            link(nc.vector.tensor_tensor(b1m[:, :], b1m[:, :], b1c[:, :], ALU.add))
            dve.wait_ge(b2_done, 1)
            link(nc.vector.tensor_copy(b2f[:, :], bank[7][0:1, :]))
            split(b2f, b216, link).then_inc(bias_split, 1)
            dve.wait_ge(w1_done, 1)
            link(nc.vector.tensor_reduce(mx[:, 1:2], bank[2][:, :], AX_X, ALU.max, apply_absolute_value=True))
            link(nc.vector.tensor_reduce(mx[:, 2:3], bank[3][:, :], AX_X, ALU.max, apply_absolute_value=True))
            nc.vector.tensor_tensor(mx[:, 1:2], mx[:, 1:2], mx[:, 2:3], ALU.max).then_inc(maxes_made, 1)
            dve.wait_ge(maxes_all, 4)
            powers(1, 1, link)
            nc.vector.tensor_scalar(cols[:, 1:2], invf[:, 1:2], 1.0 / XS, None, ALU.mult).then_inc(scales_made, 1)
            dve.wait_ge(scales_made, 3)
            for f in range(C):
                dve.wait_ge(high_made, 3 + C + f // 2 * 2 + 2)
                nc.vector.scalar_tensor_tensor(out=W1m[:, 1, f, :], in0=bank[2 + f // 2][:, (f % 2) * F:(f % 2 + 1) * F],
                                               scalar=scf[:, 1:2], in1=W1m[:, 0, f, :], op0=ALU.mult, op1=ALU.subtract
                                               ).then_inc(low_made, 1)
            dve.wait_ge(w2_done, 1)
            for o in range(FC):
                nc.vector.tensor_copy(W2m[:, o, :], bank[4 + o][:, :]).then_inc(w2_out, 1)

            def out_tick(g, j):
                quad = quad_at(g, j)
                if exists(g, j):
                    t, b = tile_at(g, j), j % 2
                    dve.wait_ge(zq_made, t + 1)
                    dve.wait_ge(o_done, t + 1)
                    at_least(dve, zr_made, t - U + 1)
                    nc.vector.scalar_tensor_tensor(out=res[:, j, :], in0=zq[:, b, :], scalar=1.0 / XS,
                                                   in1=bank[4 + b][:, :], op0=ALU.mult, op1=ALU.add).then_inc(res_made, 1)
                    dve.wait_ge(res_made, t + 1)
                    if not (isinstance(quad, int) and quad == 0):
                        dve.wait_ge(two_made, quad)
                    nc.vector.bn_stats(st6[:, j % Q4, :], res[:, j, :]).then_inc(six_made, 1)
                if j % Q4 == 0 and not (isinstance(quad, int) and quad == 0):
                    n, par = 1 if isinstance(quad, int) and quad == NQ else Q4, (j // Q4 + 1) % 2
                    dve.wait_ge(r_std, quad)
                    nc.vector.reciprocal(rsr[:, par, 0:n], sd4[:, 0:n]).then_inc(r_rec, 1)
                    dve.wait_ge(r_rec, quad)
                    nc.vector.scalar_tensor_tensor(out=nbr[:, par, 0:n], in0=var4[:, par, 0:n, 0], scalar=-1.0,
                                                   in1=rsr[:, par, 0:n], op0=ALU.mult, op1=ALU.mult).then_inc(r_scale, 1)
                last = isinstance(quad, int) and quad == NQ - 1
                if exists(g, j) and (j % Q4 == Q4 - 1 or last):
                    n = 1 if last else Q4
                    dve.wait_ge(six_made, Q4 * quad + n)
                    waited(dve)
                    for i in range(n):
                        ins = nc.vector.bn_aggr(var4[:, j // Q4, i, :], st6[:, i, :])
                    ins.then_inc(two_made, 1)
                g4, j4 = back(g, j, Q4)
                if exists(g4, j4):
                    t, b = tile_at(g4, j4), j4 % 2
                    dve.wait_ge(zr_made, t + 1)
                    nc.vector.tensor_tensor(zr[:, b, :], zr[:, b, :], lngb[:, :], ALU.mult).then_inc(gained, 1)

            row_ticks(dve, out_tick, T + Q4)

        @block.tensor
        def _(pe):
            def accumulate(dest, pairs, first=None, only=True):
                pairs = ([first] if first else []) + pairs
                for n, (lhs, rhs) in enumerate(pairs):
                    ins = nc.tensor.matmul(dest, lhs, rhs, start=(n == 0 and only), stop=(n == len(pairs) - 1),
                                           skip_group_check=not only)
                return ins

            pe.wait_ge(consts_made, 1)
            pe.wait_ge(start_made, 1)
            nc.tensor.matmul(bank[4][:, 0:NG], ones[0:1, :], srowf[:, :], start=True, stop=True).then_inc(start_spread, 1)
            pe.wait_ge(groups_made, 1)
            for c in range(SC):
                ins = nc.tensor.matmul(bank[5][0:1, c * P:(c + 1) * P], ntile[:, c:c + 1], ident[:, :],
                                       start=True, stop=True)
            ins.then_inc(tiles_turned, 1)

            def turn_picked():
                for i in range(2):
                    nc.tensor.transpose(bank[4][:, i * P:(i + 1) * P], srcf[:, i * P:(i + 1) * P], ident[:, :])
                    nc.tensor.transpose(bank[4][:, (2 + i) * P:(3 + i) * P], rel[:, i * P:(i + 1) * P], ident[:, :])
                    ins = nc.tensor.transpose(bank[5][:, i * P:(i + 1) * P],
                                              pk[:, 2, i * P:(i + 1) * P].bitcast(F32), ident[:, :])
                return ins

            for n in range(SC):
                pe.wait_ge(picked, n + 1)
                turn_picked().then_inc(turned, 1)

            def turn_rows(loop, g, j, high, low, ring, base):
                t, b = tile_at(g, j), j % 2
                pe.wait_ge(loop.low, t + 1)
                at_least(pe, loop.turned_out, t - 1)
                for part, rows_ in enumerate((high, low)):
                    for c in range(C):
                        ins = nc.tensor.transpose(turned16(base + b)[:, part, c, :], rows_[:, j % ring, c * P:(c + 1) * P],
                                                  ident16[:, :])
                ins.then_inc(loop.turned, 1)

            def head_tick(g, j):
                if exists(g, j):
                    turn_rows(head, g, j, xh, xl, 4, 6)
                g1, j1 = back(g, j, 1)
                if exists(g1, j1):
                    t, b = tile_at(g1, j1), j1 % 2
                    if isinstance(t, int) and t == 0:
                        pe.wait_ge(low_made, 3)
                        pe.wait_ge(bias_spread, 16 * 6)
                    pe.wait_ge(head.turned_out, t + 1)
                    at_least(pe, y_low, t)
                    accumulate(bank[4][:, :], [(xtb[:, b, p, c, :], Wg16[:, q, c, :]) for c in range(C)
                                               for p, q in PASSES]).then_inc(y_made, 1)
                    at_least(pe, f_used, t)
                    accumulate(bank[5][:, :], [(xtb[:, b, p, c, :], Wk16[:, q, c, :]) for c in range(C)
                                               for p, q in PASSES], first=(ones3[:, :], krows[:, :])).then_inc(f_done, 1)
                g2, j2 = back(g, j, 2)
                if exists(g2, j2):
                    t, b = tile_at(g2, j2), j2 % 2
                    pe.wait_ge(k_low, t + 1)
                    for c in range(C):
                        s = slice(c * P, (c + 1) * P)
                        for n, (p, q) in enumerate(PASSES):
                            ins = nc.tensor.matmul(bank[c][:, :], (kh, kl)[p][:, b, s], (xh, xl)[q][:, j2 % 4, :],
                                                   start=isinstance(t, int) and t == 0 and n == 0,
                                                   stop=isinstance(t, int) and t == T - 1 and n == 2,
                                                   skip_group_check=True)
                    ins.then_inc(m_done, 1)

            row_ticks(pe, head_tick, T + 2)

            pe.wait_ge(k_summed, T)
            pe.wait_ge(y_low, T)
            pe.wait_ge(f_used, T)
            nc.tensor.matmul(bank[4][:, :], ones[:, :], ksacc[:, :], start=True, stop=True)
            for c in range(C):
                ins = nc.tensor.matmul(bank[5][:, c:c + 1], ksacc[:, c * P:(c + 1) * P], ones[:, 0:1], start=True, stop=True)
            ins.then_inc(ks_done, 1)
            pe.wait_ge(m_out, C)
            for f in range(C):
                for c in range(C):
                    ins = nc.tensor.transpose(bank[f][:, c * P:(c + 1) * P], M32[:, c, f * P:(f + 1) * P], ident[:, :])
            ins.then_inc(m_turned, 1)
            pe.wait_ge(mt_out, C)
            pe.wait_ge(vp_loaded, 32)
            pe.wait_ge(kv_out, 1)
            for c in range(C):
                s = slice(c * P, (c + 1) * P)
                ins = accumulate(bank[4][:, s], [(Wv32[:, f, s], MT32[:, f, s]) for f in range(C)],
                                 first=(bvrow[:, s], ksb[0:1, s]))
            ins.then_inc(kv_done, 1)

            def step(t, h, b, r):
                s = SA * t + r
                at, use = place(h, b, r)
                pe.wait_ge(weighted, s + 1)
                at_least(pe, edge_added, s - len(STEP_BANKS) + 1)
                for i in range(2):
                    pe.wait_ge(gathered[2 * at + i], 16 * use)
                accumulate(step_bank(b, r)[:, :],
                           [(hotw[:, (SA * b + r) % OHS, i, p, :], rows[:, 2 * at + i, q, :]) for i in range(2) for p, q in PASSES]
                           ).then_inc(stepped, 1)

            def edge_pe(t, h, b):
                start = isinstance(t, int) and t == 0
                if start:
                    step(t, h, b, 0)
                    step(t, h, b, 1)
                    pe.wait_ge(kv_out, C + 1)
                    for c in range(C):
                        ins = accumulate(bank[c][:, :], [(kvt[:, c, :], Wp32[:, c, :])],
                                         first=(ksb[0:1, c * P:(c + 1) * P], mrow[:, :]))
                    ins.then_inc(kvp_done, 1)
                    step(t, h, b, 2)
                    pe.wait_ge(kmax_row, 1)
                    nc.tensor.transpose(bank[5][0:1, 0:P], mx[:, 6:7], ident[:, :]).then_inc(kmax_turned, 1)
                    pe.wait_ge(kmax_row, 2)
                    nc.tensor.matmul(bank[5][:, P:P + 1], ones[0:1, :], mx[0:1, 7:8], start=True, stop=True
                                     ).then_inc(kmax_spread, 1)
                pe.wait_ge(xt_in[b], 16 * h + 16)
                pe.wait_ge(f_used, T + t)
                accumulate(bank[0][:, :], [(xta[:, b, p, c, :], Wq16[:, q, c, :]) for c in range(C) for p, q in PASSES],
                           first=(ones3[:, :], qrows[:, :])).then_inc(f_done, 1)
                for r in range(3 if start else 0, 6):
                    step(t, h, b, r)
                pe.wait_ge(q_low, t + 1)
                at_least(pe, q_out, t)
                for part in range(2):
                    for c in range(C):
                        ins = nc.tensor.transpose(turned16(1)[:, part, c, :], qhl[:, part, c * P:(c + 1) * P], ident16[:, :])
                ins.then_inc(q_turned, 1)
                for r in range(6, SA):
                    step(t, h, b, r)
                pe.wait_ge(q_out, t + 1)
                at_least(pe, mix_added, t - 1)
                if start:
                    pe.wait_ge(kvp_low, C)
                accumulate(bank[2 + b][:, :], [(qT[:, b, p, c, :], KVP16[:, q, c, :]) for c in range(C)
                                               for p, q in PASSES]).then_inc(mix_done, 1)

            edge_tiles(pe, edge_pe)
            pe.wait_ge(edge_added, SA * T)
            unordered = pe.value_load(flag[0:1, 0:1], min_val=0, max_val=1)
            with pe.If(unordered > 0):
                with pe.Fori(0, NG) as n:
                    pe.wait_ge(u_picked, n + 1)
                    waited(pe)
                    turn_picked().then_inc(u_turned, 1)
                    pe.wait_ge(u_gathered, 32 * n + 32)
                    waited(pe)
                    with pe.Fori(0, T) as d:
                        s = T * n + d
                        pe.wait_ge(u_onehot, U_HOT * s + U_HOT)
                        waited(pe)
                        accumulate(bank[6][:, :], [(hotw[:, 0, i, p, :], rows[:, i, q, :]) for i in range(2)
                                                   for p, q in PASSES]).then_inc(u_stepped, 1)

            pe.wait_ge(edges_done, 1)
            pe.wait_ge(graw_loaded, 16)
            for f in range(C):
                for o in range(C):
                    ins = nc.tensor.transpose(bank[2 + f][:, o * P:(o + 1) * P], graw[:, o, f * P:(f + 1) * P], ident[:, :])
            ins.then_inc(graw_turned, 1)
            pe.wait_ge(small_loaded, 16 * 14)
            pe.wait_ge(ln_coefs, 1)
            nc.tensor.matmul(bank[6][:, :], lncoef[:, :], lnrows[:, :], start=True, stop=True).then_inc(ln_done, 1)
            nc.tensor.matmul(bank[7][:, :], lncoef[:, :], lbrows[:, :], start=True, stop=True).then_inc(ln_done, 1)
            pe.wait_ge(ln_out, 2)
            for c in range(C):
                ins = nc.tensor.transpose(bank[6][:, c * NE:(c + 1) * NE], g2raw[:, c * P:(c + 1) * P], ident[0:NE, 0:NE])
            ins.then_inc(g2_turned, 1)
            pe.wait_ge(high_made, 3 + C)
            pe.wait_ge(low_made, 3 + C)

            pe.wait_ge(g2_out, 1)

            def tail_tick(g, j):
                if exists(g, j):
                    turn_rows(tail, g, j, zh, zl, 2, 0)
                if gate_exists(g, j):
                    q, m = gate_at(g, j)
                    par = ((j - Q4 - 1 - m) // Q4) % 2
                    last = isinstance(q, int) and q == NQ - 1
                    if m == 0:
                        pe.wait_ge(tail.turned_out, T if last else Q4 * q + Q4)
                    at_least(pe, gf_out, C * (q - 1) + m + 1)
                    s = slice(m * P, (m + 1) * P)
                    n = LAST if last else D
                    if last:
                        pairs = [(G16[:, a, f, s], ztg[:, par, 0, b_, f, 0:LAST]) for f in range(C) for a, b_ in PASSES]
                    else:
                        pairs = [(G16[:, a, f, s], ztg[:, par, :, b_, f, :]) for f in range(C) for a, b_ in PASSES]
                    accumulate(bank[2 + m][:, 0:n], pairs).then_inc(gf_done, 1)

            row_ticks(pe, tail_tick, Q4 * NQ + 5)

            pe.wait_ge(gate_in, C)
            accumulate(bank[6][:, 0:NE], [(geye[:, c, :], g2T[:, c, :]) for c in range(C)] + [(ones[0:1, :], gbr[:, :])]
                       ).then_inc(gate_done, 1)
            accumulate(bank[6][0:NE, NE:NE + 1], [(g2T[:, c, :], gcol[:, c:c + 1]) for c in range(C)]
                       + [(gbr[:, :], ones[0:1, 0:1])]).then_inc(gate_done, 1)
            pe.wait_ge(gate_out, NE)
            accumulate(bank[7][0:1, :], [(gT[:, :], tvb2[:, :]), (ones[0:1, 0:1], b2r[:, :])]).then_inc(b2_done, 1)
            pe.wait_ge(tv1_loaded, 16 * NE)
            pe.wait_ge(gf_out, C * NQ)
            for f in range(C):
                for o in range(FC):
                    s = slice(f * P, (f + 1) * P)
                    at = (f % 2) * F + o * P
                    ins = accumulate(bank[2 + f // 2][:, at:at + P], [(W1raw[:, o, s], ident[:, :])]
                                     + [(tvW1[:, e, o, s], geye[:, e, :]) for e in range(NE)])
            ins.then_inc(w1_done, 1)
            pe.wait_ge(tv2_loaded, 16 * NE)
            for o in range(FC):
                for c in range(C):
                    s = slice(o * P, (o + 1) * P)
                    ins = accumulate(bank[4 + o][:, c * P:(c + 1) * P], [(W2raw[:, c, s], ident[:, :])]
                                     + [(tvW2[:, e, c, s], geye[:, e, :]) for e in range(NE)])
            ins.then_inc(w2_done, 1)
            pe.wait_ge(high_made, 3 + C + C)
            pe.wait_ge(low_made, 3 + C + C)

            def hidden(q, par, n):
                for o in range(FC):
                    at_least(pe, h_out, FC * (q - 1) + o + 1)
                    s = slice(o * P, (o + 1) * P)
                    if n == P:
                        pairs = [(W1m[:, a, f, s], xd[:, par, 0, b_, f, :]) for f in range(C) for a, b_ in PASSES]
                    else:
                        pairs = [(W1m[:, a, f, s], xd[:, par, :, b_, f, :]) for f in range(C) for a, b_ in PASSES]
                    accumulate(bank[2 + o][:, 0:n], pairs).then_inc(h_done, 1)

            pe.wait_ge(zd_in[0], 16)
            hidden(0, 0, Q4 * P)
            pe.wait_ge(w2_out, FC)
            pe.wait_ge(bias_spread, 16 * 9)

            def out_tick(g, j):
                quad = quad_at(g, j)
                if j % Q4 == 0 and not (isinstance(quad, int) and quad + 1 >= NQ):
                    pe.wait_ge(zd_in[(j // Q4 + 1) % 2], 16 * (g + 1 + j // Q4))
                    hidden(quad + 1, (j // Q4 + 1) % 2, P if isinstance(quad, int) and quad + 1 == NQ - 1 else Q4 * P)
                if exists(g, j):
                    t, b = tile_at(g, j), j % 2
                    pe.wait_ge(h_out, FC * (quad + 1))
                    at_least(pe, res_made, t - 1)
                    s = slice((j % Q4) * P, (j % Q4 + 1) * P)
                    accumulate(bank[4 + b][:, :], [(hT[:, j // Q4, o, s], W2m[:, o, :]) for o in range(FC)],
                               first=(ones3[:, :], b2rows[:, :])).then_inc(o_done, 1)

            row_ticks(pe, out_tick, T)


_NAMES = ["x", "src", "dst", "edge_weight", "L0_gnn_weight", "L0_gnn_bias", "L0_mix_Wq", "L0_mix_bq", "L0_mix_Wk",
          "L0_mix_bk", "L0_mix_Wv", "L0_mix_bv", "L0_mix_Wp", "L0_mix_bp", "L0_ffn_gfc1_w", "L0_ffn_gfc1_b",
          "L0_ffn_gfc2_w", "L0_ffn_gfc2_b", "L0_ffn_W1", "L0_ffn_b1", "L0_ffn_W2", "L0_ffn_b2", "L0_ffn_ln_g",
          "L0_ffn_ln_b", "L0_ffn_tv_W1", "L0_ffn_tv_b1", "L0_ffn_tv_W2", "L0_ffn_tv_b2", "L0_ffn_tv_ln_g",
          "L0_ffn_tv_ln_b"]


def kernel(**inputs):
    import numpy as np
    from concourse import bacc
    from concourse.bass_utils import run_bass_kernel_spmd

    nc = bacc.Bacc("TRN2", target_bir_lowering=False, num_devices=1)
    arrays, args = {}, []
    for name in _NAMES:
        a = np.ascontiguousarray(inputs[name])
        arrays["in_" + name] = a
        args.append(nc.dram_tensor("in_" + name, a.shape, mybir.dt.from_np(a.dtype), kind="ExternalInput").ap())
    out = nc.dram_tensor("out", (N, D), F32, kind="ExternalOutput").ap()
    build(nc, *args, out)
    result = run_bass_kernel_spmd(nc, [arrays], core_ids=[0])
    return result.results[0]["out"]
```

```python
from contextlib import ExitStack

import concourse.bass as bass
from concourse import mybir

F32 = mybir.dt.float32
F16 = mybir.dt.float16
BF16 = mybir.dt.bfloat16
I32 = mybir.dt.int32
ALU = mybir.AluOpType
ACT = mybir.ActivationFunctionType
AX_X = mybir.AxisListType.X
RMAX = bass.bass_isa.ReduceOp.max
RADD = bass.bass_isa.ReduceOp.add

P = 128
N, D = 6250, 512
E = 100000
C = D // P
T = -(-N // P)
LAST = N - (T - 1) * P
H = 8
HD = D // H
F = 256
FC = F // P
NE = 8
EG = 2 * P
NG = -(-E // EG)
GFULL = E // EG
SA = -(-(NG + T - 1) // T)
SC = -(-SA * T // P)
RING = 6
SLOTS = 2 * RING
OHS = 6
AHEAD = 4
TABLES_AT = 3
MIX_AT = 3
ADD_MIX_AFTER = 4
STEP_BANKS = (6, 7, 4)
U_HOT = 4
H_HIGH, H_LOW = 3 + 2 * C, 2 + 2 * C
DR, DW = 125, E // 125
OUTSIDE = float(1 << 20)
QS = float(1 << 14)
XS = 1024.0
EPS = 1e-5
LN_MERGE = 0.03
Q4 = 4
U = 2 * Q4
NQ = -(-T // Q4)
EXPONENT = 0x7F800000
PASSES = ((0, 0), (0, 1), (1, 0))


def at_least(eng, sem, n):
    if not isinstance(n, int) or n > 0:
        eng.wait_ge(sem, n)


def size_of(shape, dt):
    n = mybir.dt.size(dt)
    for s in shape[1:]:
        n *= s
    return -(-n // 32) * 32


def build(nc, x, src, dst, edge_weight, gnn_w, gnn_b, Wq, bq, Wk, bk, Wv, bv, Wp, bp,
          gfc1_w, gfc1_b, gfc2_w, gfc2_b, W1, b1, W2, b2, ln_g, ln_b,
          tv_W1, tv_b1, tv_W2, tv_b2, tv_ln_g, tv_ln_b, out):
    packed = nc.dram_tensor("packed", (NG, 3 * EG), I32, kind="Internal").ap()
    y_rows = nc.dram_tensor("y_rows", (T * P, 2 * D), F16, kind="Internal").ap()
    xt_rows = nc.dram_tensor("xt_rows", (T * P, 2 * D), F16, kind="Internal").ap()
    zt_rows = nc.dram_tensor("zt_rows", (T * P, 2 * D), F16, kind="Internal").ap()

    def row_tile(ap, t):
        return ap.rearrange("(t p) d -> t p d", p=P)[bass.ds(t, 1)].rearrange("a p d -> (a p) d")

    with ExitStack() as ctx:
        ctx.enter_context(nc.allow_non_contiguous_dma(reason="small columns: group starts, biases"))
        base, top = -(-nc.sbuf_base // 32) * 32, nc.sbuf_usable_end
        cursor = [base]

        def put(name, shape, dt):
            at = cursor[0]
            cursor[0] += size_of(shape, dt)
            assert cursor[0] <= top, (name, cursor[0], top)
            return nc.alloc_sbuf_tensor_at(name, shape, dt, offset=at)

        def over(at, *specs):
            made = []
            for name, shape, dt in specs:
                made.append(nc.alloc_sbuf_tensor_at(name, shape, dt, offset=at))
                at += size_of(shape, dt)
                assert at <= top, (name, at, top)
            return made if len(made) > 1 else made[0]

        def region(size):
            cursor[0] += size
            return cursor[0] - size

        sem = lambda name: ctx.enter_context(nc.semaphore(name))

        acc = put("acc", [P, T, D], F32)
        ident = put("ident", [P, P], F32)
        ident16 = put("ident16", [P, P], F16)
        iota16 = put("iota16", [P, P], F16)
        ones = put("ones", [P, P], F32)
        ones3 = put("ones3", [3, P], BF16)
        headmask = put("headmask", [P, P], F32)
        rs = put("rs", [P, T + Q4 - 1], F32)
        nb = put("nb", [P, T + Q4 - 1], F32)
        var4 = put("var4", [P, 2, Q4, 2], F32)
        st6 = put("st6", [P, Q4, 6], F32)
        sd4 = put("sd4", [P, Q4], F32)
        rsr = put("rsr", [P, 2, Q4], F32)
        nbr = put("nbr", [P, 2, Q4], F32)
        epsc = put("epsc", [P, 1], F32)
        minus1 = put("minus1", [P, 1], F32)
        mx = put("mx", [P, 8], F32)
        mxa = put("mxa", [P, 8], F32)
        pw = put("pw", [P, 8], I32)
        sc = put("sc", [P, 8], I32)
        inv = put("inv", [P, 8], I32)
        cols = put("cols", [P, 8], F32)
        den = put("den", [P, H], F32)
        rden = put("rden", [P, H], F32)
        stepi = put("stepi", [P, SC], I32)
        stepf = put("stepf", [P, SC], F32)
        cnt = put("cnt", [P, SC], F32)
        gidx = put("gidx", [P, SC], I32)
        ntile = put("ntile", [P, SC], F32)
        negd = put("negd", [P, SC], F32)
        late = put("late", [P, SC], F32)
        viol = put("viol", [P, 1], F32)
        uns = put("uns", [P, 1], F32)
        srt = put("srt", [P, 1], F32)
        flag = put("flag", [1, 1], I32)
        tileof = put("tileof", [1, SC * P], I32)
        krows = put("krows", [3, D], BF16)
        qrows = put("qrows", [3, D], BF16)
        mrow = put("mrow", [1, D], F32)
        kinv = put("kinv", [P, C], F32)
        bvrow = put("bvrow", [1, D], F32)
        rA, rB, rQ, rV, rP = (region(4 * C * D) for _ in range(5))
        rTab, rIdx, rG = region(SC * P * 16), region(SC * P * 8), region(SLOTS * 4 * D)
        rW = cursor[0]
        Wg16 = over(rA, ("Wg16", [P, 2, C, D], F16))
        Wk16 = over(rB, ("Wk16", [P, 2, C, D], F16))
        Wq16 = over(rQ, ("Wq16", [P, 2, C, D], F16))
        Wv32 = over(rV, ("Wv32", [P, C, D], F32))
        Wp32 = over(rP, ("Wp32", [P, C, D], F32))
        M32 = over(rA, ("M32", [P, C, D], F32))
        MT32 = over(rB, ("MT32", [P, C, D], F32))
        KVP = over(rA, ("KVP", [P, C, D], F32))
        KVP16 = over(rV, ("KVP16", [P, 2, C, D], F16))
        qk, qs, qhl, kvt = over(
            rB, ("qk", [P, D], F32), ("qs", [P, D], F32), ("qhl", [P, 2, D], F16), ("kvt", [P, C, P], F32))
        qT = over(rP, ("qT", [P, 2, 2, C, P], F16))
        tab = over(rTab, ("tab", [P, SC * P, 2, 2], F32))
        idx = over(rIdx, ("idx", [P, SC * P, 2], I32))
        rows = over(rG, ("rows", [P, SLOTS, 2, D], F16))
        stage = over(rG, ("stage", [P, 3, C, D], F32))
        pk, srcf, rel, ok = over(
            rV, ("pk", [P, 3, EG], I32), ("srcf", [P, EG], F32), ("rel", [P, EG], F32), ("ok", [P, EG], F32))
        startb, pad, bfq = over(rP, ("startb", [P, NG], F32), ("pad", [1, 3, EG], I32), ("bfq", [1, D], F32))
        dsts, ews, junk = over(rTab, ("dsts", [P, DW + 1], I32), ("ews", [P, DW], F32), ("junk", [P, NG], F32))
        srow, srowf, irow, bf, b16, brow = over(
            rW, ("srow", [1, NG], I32),
            ("srowf", [1, NG], F32), ("irow", [1, NG], I32), ("bf", [1, D], F32), ("b16", [1, 2, 3, D], BF16),
            ("brow", [1, 4, D], F32))
        xh, xl, xtb, yb, kh, kl, fill = over(
            rG, ("xh", [P, 4, D], F16), ("xl", [P, 4, D], F16), ("xtb", [P, 2, 2, C, P], F16),
            ("yb", [P, 2, 2, D], F16), ("kh", [P, 2, D], F16), ("kl", [P, 2, D], F16), ("fill", [P, 4 * D], F16))
        xnb = over(rW, ("xnb", [P, 2, D], F32))
        xta, kf, ksacc, mb, ksb, hotw, idxc, tabc, wh16, wlo = over(
            rW, ("xta", [P, 2, 2, C, P], F16), ("kf", [P, 2, D], F32), ("ksacc", [P, D], F32), ("mb", [P, D], F32),
            ("ksb", [P, D], F32), ("hotw", [P, OHS, 2, 2, P], F16), ("idxc", [P, 2, 2 * SA], I32),
            ("tabc", [P, 2, 2 * SA, 2], F32), ("wh16", [P, 2, 2 * SA], F16), ("wlo", [P, 2, 2 * SA], F32))
        oneh = over(rW + 3 * 4 * D, ("oneh", [P, OHS, 2, P], F16))
        graw = over(rA, ("graw", [P, C, D], F32))
        tvW1 = over(rA, ("tvW1", [P, NE, FC, D], F32))
        xd, hT, zq, zr = over(
            rA, ("xd", [P, 2, Q4, 2, C, P], F16), ("hT", [P, 2, 2, FC, D], F16), ("zq", [P, 2, D], F32),
            ("zr", [P, 2, D], F32))
        G16, ztg = over(rP, ("G16", [P, 2, C, D], F16), ("ztg", [P, 2, Q4, 2, C, P], F16))
        tvW2 = over(rP, ("tvW2", [P, NE, C, F], F32))
        res, ob, h32 = over(rP, ("res", [P, U, D], F32), ("ob", [P, 2, D], F32), ("h32", [P, FC, D], F32))
        rN = rP + 4 * NE * C * F
        zn, zh, zl = over(rN, ("zn", [P, 2, D], F32), ("zh", [P, 2, D], F16), ("zl", [P, 2, D], F16))
        W1m, W2m = over(rN, ("W1m", [P, 2, C, F], F16), ("W2m", [P, 2, FC, D], F16))
        (W1raw, W2raw, lnrows, lbrows, g2raw, lngb, lnbb, lncoef, gjunk, gsum, gsq, gcol, gbias, g2T,
         gall, gT, gbr, b1c, tvb1, b1m, tvb2, geye) = over(
            rN + 16 * D, ("W1raw", [P, FC, D], F32), ("W2raw", [P, C, F], F32),
            ("lnrows", [NE + 1, D], F32), ("lbrows", [NE + 1, D], F32), ("g2raw", [NE, D], F32),
            ("lngb", [P, D], F32), ("lnbb", [P, D], F32), ("lncoef", [NE + 1, P], F32), ("gjunk", [P, D], F16),
            ("gsum", [P, C, NQ], F32), ("gsq", [P, C], F32), ("gcol", [P, C], F32), ("gbias", [P, C], F32),
            ("g2T", [P, C, NE], F32), ("gall", [P, NE], F32), ("gT", [NE, 1], F32),
            ("gbr", [1, NE], F32), ("b1c", [P, FC], F32), ("tvb1", [P, FC, NE], F32),
            ("b1m", [P, FC], F32), ("tvb2", [NE, D], F32), ("geye", [P, NE, P], F32))
        b2f, b216 = over(rN + 16 * D + 8 * F * 4 + 0, ("b2f", [1, D], F32), ("b216", [1, 3, D], BF16))
        b2rows, b2r, scale3 = krows, bvrow, qrows

        bank = [ctx.enter_context(nc.psum_tensor(f"bank{i}", [P, D], F32)) for i in range(8)]

        pool_set = sem("pool_set")
        consts_made = sem("consts_made")
        edges_loaded, start_loaded, bias_loaded = sem("edges_loaded"), sem("start_loaded"), sem("bias_loaded")
        w_loaded = [sem(f"w_loaded{k}") for k in range(3)]
        edges_packed, vp_loaded = sem("edges_packed"), sem("vp_loaded")
        x_loaded = [sem(f"x_loaded{j}") for j in range(Q4)]
        maxes_made, maxes_all = sem("maxes_made"), sem("maxes_all")
        scales_made, high_made, low_made = sem("scales_made"), sem("high_made"), sem("low_made")
        chain = sem("chain")
        start_made, start_spread = sem("start_made"), sem("start_spread")
        groups_made, tiles_turned, tiles_out = sem("groups_made"), sem("tiles_turned"), sem("tiles_out")
        bias_split, bias_spread = sem("bias_split"), sem("bias_spread")
        q_split, q_spread, wq_low = sem("q_split"), sem("q_spread"), sem("wq_low")
        pool_chain = sem("pool_chain")
        pk_ready, picked, turned, tabled = sem("pk_ready"), sem("picked"), sem("turned"), sem("tabled")

        class RowLoop:

            def __init__(self, name):
                self.vars_made = sem(name + "_vars_made")
                self.std_made = sem(name + "_std_made")
                self.scale_made = sem(name + "_scale_made")
                self.high = sem(name + "_high")
                self.low = sem(name + "_low")
                self.turned = sem(name + "_turned")
                self.turned_out = sem(name + "_turned_out")
                self.turned_kept = [sem(f"{name}_turned_kept{b}") for b in range(2)]

                self.six = sem(name + "_six")
                self.rec = sem(name + "_rec")

        head, tail = RowLoop("head"), RowLoop("tail")
        y_made, y_high, y_low = sem("y_made"), sem("y_high"), sem("y_low")
        y_kept = [sem(f"y_kept{b}") for b in range(2)]
        copied, indexed, parted = sem("copied"), sem("indexed"), sem("parted")
        gathered = [sem(f"gathered{q}") for q in range(SLOTS)]
        onehot, weighted, stepped, edge_added = (sem(n) for n in ("onehot", "weighted", "stepped", "edge_added"))
        xt_in = [sem(f"xt_in{b}") for b in range(2)]
        f_done, f_min, f_exp, f_used, m_done = (sem(n) for n in ("f_done", "f_min", "f_exp", "f_used", "m_done"))
        k_high, k_low, k_summed = sem("k_high"), sem("k_low"), sem("k_summed")
        ks_done, m_out, m_turned, mt_out = (sem(n) for n in ("ks_done", "m_out", "m_turned", "mt_out"))
        kv_done, kv_out, kvp_done, kvp_out, kvp_low, kmax_turned, kmax_row, kmax_spread = (sem(n) for n in (
            "kv_done", "kv_out", "kvp_done", "kvp_out", "kvp_low", "kmax_turned", "kmax_row", "kmax_spread"))
        q_summed, q_scaled, q_high, q_low, q_turned, q_out, mix_done, mix_added = (sem(n) for n in (
            "q_summed", "q_scaled", "q_high", "q_low", "q_turned", "q_out", "mix_done", "mix_added"))
        graw_loaded = sem("graw_loaded")
        u_chain, u_group, u_pk, u_picked, u_turned, u_index, u_gathered, u_onehot, u_stepped, u_added = (
            sem(n) for n in ("u_chain", "u_group", "u_pk", "u_picked", "u_turned", "u_index", "u_gathered",
                             "u_onehot", "u_stepped", "u_added"))
        edges_done, u_start = sem("edges_done"), sem("u_start")
        small_loaded, tv1_loaded, tv2_loaded = sem("small_loaded"), sem("tv1_loaded"), sem("tv2_loaded")
        ln_coefs, gate_in = sem("ln_coefs"), sem("gate_in")
        graw_turned = sem("graw_turned")
        ln_done, ln_out = sem("ln_done"), sem("ln_out")
        gf_done, gf_out = sem("gf_done"), sem("gf_out")
        gate_done, gate_out = sem("gate_done"), sem("gate_out")
        w1_done, w2_done, w2_out = sem("w1_done"), sem("w2_done"), sem("w2_out")
        zd_in = [sem(f"zd_in{b}") for b in range(2)]
        h_done, h_out, o_done, zq_made, res_made, six_made, two_made, r_std, r_rec, r_scale = (sem(n) for n in (
            "h_done", "h_out", "o_done", "zq_made", "res_made", "six_made", "two_made", "r_std", "r_rec", "r_scale"))
        zr_made, gained, based, ob_made = sem("zr_made"), sem("gained"), sem("based"), sem("ob_made")
        out_kept = [sem(f"out_kept{b}") for b in range(2)]

        block = ctx.enter_context(nc.Block())
        flat = lambda ap, t: ap[:, bass.ds(t, 1), :].rearrange("p a d -> p (a d)")

        def back(g, j, n):
            return g + (j - n) // U, (j - n) % U

        def tile_at(g, j):
            return U * g + j

        def half_at(g, j):
            return U // 2 * g + j // 2

        def quad_at(g, j):
            return 2 * g + j // Q4

        def row_ticks(eng, tick, last):
            for j in range(U):
                tick(0, j)
            with eng.Fori(1, T // U - 1) as g:
                for j in range(U):
                    tick(g, j)
            for t in range((T // U - 1) * U, last):
                tick(t // U, t % U)

        def exists(g, j):
            return not isinstance(g, int) or 0 <= tile_at(g, j) < T

        def edge_tiles(eng, tile):
            tile(0, 0, 0)
            tile(1, 0, 1)
            with eng.Fori(1, T // 2) as h:
                tile(2 * h, h, 0)
                tile(2 * h + 1, h, 1)
            tile(T - 1, T // 2, (T - 1) % 2)

        def place(h, b, r):
            turn = 2 * SA // RING
            return (SA * b + r) % RING, turn * h + (SA * b + r) // RING + 1

        def step_bank(b, r):
            return bank[STEP_BANKS[(SA * b + r) % len(STEP_BANKS)]]

        def head_kept(eng):
            for b in range(2):
                n = 16 * ((T + 1 - b) // 2)
                eng.wait_ge(head.turned_kept[b], n)
                eng.wait_ge(y_kept[b], n)

        def gate_at(g, j):
            m = (j - 1) % Q4
            return 2 * g + (j - Q4 - 1 - m) // Q4, m

        def gate_exists(g, j):
            return not isinstance(g, int) or 0 <= gate_at(g, j)[0] < NQ

        def free_group(eng, g, j):
            at_least(eng, tail.turned_kept[j % 2], 16 * (half_at(g, j) - Q4 + 2))
            if j % Q4 == 0:
                at_least(eng, gf_done, C * (quad_at(g, j) - 1))

        def waited(eng):
            eng.nop(nofuse=True)

        def turned16(b):
            return bank[b][:, :].bitcast(F16).rearrange("p (a c m) -> p a c m", a=2, c=C)

        def split(eng, row, work, dest, scale, link):
            if scale is not None:
                link(eng.tensor_scalar(work[:, :], row, 1.0, scale, ALU.add, ALU.mult))
            link(eng.tensor_copy(dest[:, 0, :], work[:, :]))
            link(eng.tensor_tensor(work[:, :], work[:, :], dest[:, 0, :], ALU.subtract))
            link(eng.tensor_copy(dest[:, 1, :], work[:, :]))
            link(eng.tensor_tensor(work[:, :], work[:, :], dest[:, 1, :], ALU.subtract))
            return eng.tensor_copy(dest[:, 2, :], work[:, :])

        scf, invf = sc[:, :].bitcast(F32), inv[:, :].bitcast(F32)
        by_half = lambda ap: ap.rearrange("p (j s) -> p j s", j=2)

        @block.sync
        def _(sp):
            flat_dst = dst.rearrange("(a n) -> a n", a=1)
            by_row = dst.rearrange("(p w) -> p w", w=DW)
            sp.dma_start(dsts[0:DR, 0:DW], by_row).then_inc(edges_loaded, 16)
            sp.dma_start(dsts[0:DR - 1, DW:DW + 1], by_row[1:DR, 0:1]).then_inc(edges_loaded, 16)
            sp.dma_start(dsts[DR - 1:DR, DW:DW + 1], flat_dst[:, E - 1:E]).then_inc(edges_loaded, 16)
            sp.dma_start(ews[0:DR, :], edge_weight.rearrange("(p w) -> p w", w=DW)).then_inc(edges_loaded, 16)
            for k, w in enumerate((gnn_w, Wk, Wq)):
                sp.dma_start(stage[:, k], w.rearrange("(c p) n -> p c n", p=P)).then_inc(w_loaded[k], 16)
            sp.dma_start(srow[:, :], flat_dst[:, 0:E:EG]).then_inc(start_loaded, 16)
            for r, b in enumerate((bk, bq, bp, gnn_b)):
                sp.dma_start(brow[:, r, :], b.rearrange("(a n) -> a n", a=1)).then_inc(bias_loaded, 16)
            sp.dma_start(bvrow[:, :], bv.rearrange("(a n) -> a n", a=1)).then_inc(bias_loaded, 16)

            def load_x(g, j):
                t = Q4 * g + j
                at_least(sp, x_loaded[j], 16 * g)
                sp.dma_start(flat(acc, t), row_tile(x[0:(T - 1) * P, :], t)).then_inc(x_loaded[j], 16)

            for j in range(Q4):
                load_x(0, j)
            with sp.Fori(1, (T - 1) // Q4) as g:
                for j in range(Q4):
                    load_x(g, j)
            sp.wait_ge(consts_made, 1)
            sp.dma_start(acc[0:LAST, T - 1, :], x[(T - 1) * P:N, :]).then_inc(x_loaded[0], 16)

            def head_stores(g, j):
                g1, j1 = back(g, j, 1)
                if exists(g1, j1):
                    t, b1 = tile_at(g1, j1), j1 % 2
                    sp.wait_ge(head.turned_out, t + 1)
                    sp.dma_start(row_tile(xt_rows, t), xtb[:, b1].rearrange("p a c m -> p (a c m)")
                                 ).then_inc(head.turned_kept[b1], 16)
                g2, j2 = back(g, j, 2)
                if exists(g2, j2):
                    t, b = tile_at(g2, j2), j2 % 2
                    sp.wait_ge(y_low, t + 1)
                    sp.dma_start(row_tile(y_rows, t), yb[:, b].rearrange("p a d -> p (a d)")
                                 ).then_inc(y_kept[b], 16)

            row_ticks(sp, head_stores, T + 2)
            sp.wait_ge(tabled, SC)
            sp.dma_start(Wv32[:, :, :], Wv.rearrange("(c p) n -> p c n", p=P)).then_inc(vp_loaded, 16)
            sp.dma_start(Wp32[:, :, :], Wp.rearrange("(c p) n -> p c n", p=P)).then_inc(vp_loaded, 16)
            head_kept(sp)
            sp.wait_ge(head.turned, T)

            def turned_loads(t, h, b):
                at_least(sp, f_done, T + t - 1)
                sp.dma_start(xta[:, b].rearrange("p a c m -> p (a c m)"), row_tile(xt_rows, t)
                             ).then_inc(xt_in[b], 16)

            edge_tiles(sp, turned_loads)
            sp.wait_ge(kvp_low, C)
            sp.dma_start(graw[:, :, :], gfc1_w.rearrange("(c p) n -> p c n", p=P)).then_inc(graw_loaded, 16)

            sp.wait_ge(edges_done, 1)
            one = lambda ap: ap.rearrange("(a n) -> a n", a=1)
            for dest, source in (
                    (lnrows[0:1, :], one(ln_g)), (lnrows[1:NE + 1, :], tv_ln_g),
                    (lbrows[0:1, :], one(ln_b)), (lbrows[1:NE + 1, :], tv_ln_b),
                    (g2raw[:, :], gfc2_w), (gbr[:, :], one(gfc2_b)), (gbias[:, :], gfc1_b.rearrange("(c p) -> p c", p=P)),
                    (tvb2[:, :], tv_b2), (b2r[:, :], one(b2)), (b1c[:, :], b1.rearrange("(c p) -> p c", p=P)),
                    (W1raw[:, :, :], W1.rearrange("(c p) d -> p c d", p=P)),
                    (W2raw[:, :, :], W2.rearrange("(c p) f -> p c f", p=P))):
                sp.dma_start(dest, source).then_inc(small_loaded, 16)
            for c in range(FC):
                sp.dma_start(tvb1[:, c, :], tv_b1[:, c * P:(c + 1) * P].rearrange("e p -> p e")
                             ).then_inc(small_loaded, 16)
            sp.wait_ge(graw_turned, 1)
            sp.wait_ge(maxes_made, 2)
            for e in range(NE):
                sp.dma_start(tvW1[:, e], tv_W1[e].rearrange("(c p) d -> p c d", p=P)).then_inc(tv1_loaded, 16)

            def tail_stores(g, j):
                g1, j1 = back(g, j, 1)
                if exists(g1, j1):
                    t, b1 = tile_at(g1, j1), j1 % 2
                    sp.wait_ge(tail.turned_out, t + 1)
                    at_least(sp, tail.turned_kept[b1], 16 * half_at(g1, j1))
                    sp.dma_start(row_tile(zt_rows, t), ztg[:, j1 // Q4, j1 % Q4].rearrange("p a c m -> p (a c m)")
                                 ).then_inc(tail.turned_kept[b1], 16)

            row_ticks(sp, tail_stores, T + 1)
            for b in range(2):
                sp.wait_ge(tail.turned_kept[b], 16 * ((T + 1 - b) // 2))
            sp.wait_ge(gf_done, C * NQ)
            for e in range(NE):
                sp.dma_start(tvW2[:, e], tv_W2[e].rearrange("(c p) f -> p c f", p=P)).then_inc(tv2_loaded, 16)
            sp.wait_ge(gate_out, 2 * NE)

            def load_zd(q, b, n):
                sp.dma_start(xd[:, b, 0:n].rearrange("p t a c m -> p t (a c m)"),
                             zt_rows.rearrange("(t p) d -> p t d", p=P)[:, bass.ds(Q4 * q, n), :]
                             ).then_inc(zd_in[b], 16)

            load_zd(0, 0, Q4)
            load_zd(1, 1, Q4)
            sp.wait_ge(bias_split, 2)
            for part in range(3):
                sp.dma_start(b2rows[part:part + 1, :], b216[:, part, :]).then_inc(bias_spread, 16)

            def out_stores(g, j):
                q = quad_at(g, j)
                if j % Q4 == 0 and not (isinstance(q, int) and q + 2 >= NQ):
                    sp.wait_ge(h_done, FC * (q + 1))
                    load_zd(q + 2, j // Q4, 1 if isinstance(q, int) and q + 2 == NQ - 1 else Q4)
                g4, j4 = back(g, j, Q4)
                if exists(g4, j4):
                    t, b = tile_at(g4, j4), j4 % 2
                    sp.wait_ge(ob_made, t + 1)
                    if isinstance(t, int) and t == T - 1:
                        sp.dma_start(out[t * P:N, :], ob[0:LAST, b, :]).then_inc(out_kept[b], 16)
                    else:
                        sp.dma_start(row_tile(out[0:(T - 1) * P, :], t), ob[:, b, :]).then_inc(out_kept[b], 16)

            row_ticks(sp, out_stores, T + Q4)
            for b in range(2):
                sp.wait_ge(out_kept[b], 16 * ((T + 1 - b) // 2))

        @block.scalar
        def _(act):
            for i, a in enumerate((src, dst, edge_weight.bitcast(I32))):
                act.dma_start(packed[0:GFULL, i * EG:(i + 1) * EG],
                              a[0:GFULL * EG].rearrange("(g e) -> g e", e=EG)).then_inc(edges_packed, 16)
                act.dma_start(packed[GFULL:NG, i * EG:i * EG + E - GFULL * EG],
                              a[GFULL * EG:E].rearrange("(g e) -> g e", g=1)).then_inc(edges_packed, 16)
            act.wait_ge(consts_made, 1)
            act.dma_start(packed[GFULL:NG, :].rearrange("g (i e) -> g i e", i=3)[:, :, E - GFULL * EG:EG],
                          pad[:, :, 0:NG * EG - E]).then_inc(edges_packed, 16)
            for k, w16 in enumerate((Wg16, Wk16, Wq16)):
                act.wait_ge(scales_made, 1)
                nc.scalar.activation(w16[:, 0], stage[:, k], ACT.Copy, scale=scf[:, k:k + 1]).then_inc(high_made, 1)

            def deviations(loop, quad, par, n):
                act.wait_ge(loop.vars_made, quad + 1)
                at_least(act, loop.rec, 2 * quad)
                nc.scalar.activation(sd4[:, 0:n], var4[:, par, 0:n, 1], ACT.Sqrt, bias=epsc[:, :]
                                     ).then_inc(loop.std_made, 1)

            def normalise(loop, g, j, dest, high, ring):
                t, b = tile_at(g, j), j % 2
                act.wait_ge(loop.scale_made, quad_at(g, j) + 1)
                at_least(act, loop.low, t - 1)
                if loop is head:
                    at_least(act, m_done, t - ring + 1)
                else:
                    at_least(act, tail.turned, t - ring + 1)
                waited(act)
                for to in (dest[:, b, :], high[:, j % ring, :]):
                    nc.scalar.activation(to, flat(acc, t), ACT.Identity, scale=rs[:, bass.ds(t, 1)],
                                         bias=nb[:, bass.ds(t, 1)]).then_inc(loop.high, 1)

            def next_deviations(loop, g, j):
                quad = quad_at(g, j)
                if j % Q4 == 2 and not (isinstance(quad, int) and quad + 1 >= NQ):
                    n = 1 if isinstance(quad, int) and quad + 1 == NQ - 1 else Q4
                    deviations(loop, quad + 1, (j // Q4 + 1) % 2, n)

            def head_tick(g, j):
                g2, j2 = back(g, j, 2)
                t2, two_back = tile_at(g2, j2), j2 % 2
                if exists(g2, j2):
                    act.wait_ge(y_made, t2 + 1)
                    at_least(act, y_kept[two_back], 16 * half_at(g2, j2))
                    nc.scalar.activation(yb[:, two_back, 0, :], bank[4][:, :], ACT.Copy, scale=cols[:, 0:1]
                                         ).then_inc(y_high, 1)
                if exists(g, j):
                    normalise(head, g, j, xnb, xh, 4)
                if isinstance(g, int) and g == 0 and j < 2:
                    split_row, spread, dest = ((bias_split, bias_spread, krows), (q_split, q_spread, qrows))[j]
                    act.wait_ge(split_row, 1)
                    for part in range(3):
                        act.dma_start(dest[part:part + 1, :], b16[:, j, part, :]).then_inc(spread, 16)
                if exists(g2, j2):
                    act.wait_ge(f_min, t2 + 1)
                    nc.scalar.activation(mb[:, :], mb[:, :], ACT.Exp, bias=minus1[:, :]).then_inc(f_exp, 1)
                    act.wait_ge(f_used, t2 + 1)
                    at_least(act, m_done, t2 - 1)
                    if isinstance(t2, int) and t2 == 0:
                        act.wait_ge(wq_low, 1)
                    nc.scalar.activation(kh[:, two_back, :], kf[:, two_back, :], ACT.Copy, scale=scf[:, 5:6]).then_inc(k_high, 1)
                next_deviations(head, g, j)

            deviations(head, 0, 0, Q4)
            row_ticks(act, head_tick, T + 2)

            def copy_columns(t, b):
                at_least(act, weighted, SA * (t - 1))
                at_least(act, parted, t - 1)
                waited(act)
                nc.scalar.copy(tabc[:, b, :, :], tab[:, bass.ds(SA * t, SA)].rearrange("p s j k -> p (s j) k")
                               ).then_inc(copied, 1)
                act.wait_ge(copied, 2 * t + 1)
                nc.scalar.copy(wh16[:, b, :], tabc[:, b, :, 1]).then_inc(copied, 1)

            def weigh(t, b, r):
                s, at = SA * t + r, (SA * b + r) % OHS
                b = (b + r // SA) % 2
                act.wait_ge(onehot, s + 1)
                at_least(act, stepped, s - OHS + 1)
                for i in range(2):
                    e = 2 * (r % SA) + i
                    for part, w in enumerate((tabc[:, b, e, 1:2], wlo[:, b, e:e + 1])):
                        ins = nc.scalar.activation(hotw[:, at, i, part, :], oneh[:, at, i, :], ACT.Copy, scale=w)
                ins.then_inc(weighted, 1)

            act.wait_ge(tabled, SC)
            copy_columns(0, 0)
            act.wait_ge(m_done, T)
            for c in (1, 3):
                nc.scalar.activation(M32[:, c, :], bank[c][:, :], ACT.Copy, scale=cols[:, 6:7]).then_inc(m_out, 1)
            act.wait_ge(m_turned, 1)
            for c in (1, 3):
                nc.scalar.copy(MT32[:, c, :], bank[c][:, :]).then_inc(mt_out, 1)

            def edge_exp(t):
                act.wait_ge(f_min, T + t + 1)
                nc.scalar.activation(mb[:, :], mb[:, :], ACT.Exp, bias=minus1[:, :]).then_inc(f_exp, 1)

            def weigh_all(t, b, first, last):
                for r in range(first, last):
                    weigh(t, b, r)

            def edge_act(t, h, b):
                last = isinstance(t, int) and t == T - 1
                if isinstance(t, int) and t == 0:
                    act.wait_ge(ks_done, 1)
                    weigh_all(t, b, 0, 6)
                    act.wait_ge(kvp_done, 1)
                    act.wait_ge(kv_out, C + 1)
                    for c in (1, 3):
                        nc.scalar.activation(KVP[:, c, :], bank[c][:, :], ACT.Copy, scale=kinv[:, c:c + 1]
                                             ).then_inc(kvp_out, 1)
                    weigh(t, b, 6)
                    copy_columns(1, 1)
                    edge_exp(t)
                    weigh_all(t, b, 7, 9)
                else:
                    if not last:
                        copy_columns(t + 1, 1 - b)
                    edge_exp(t)
                    weigh_all(t, b, AHEAD, AHEAD + 3)
                act.wait_ge(q_scaled, t + 1)
                at_least(act, q_turned, t)
                nc.scalar.activation(qhl[:, 0, :], qs[:, :], ACT.Copy, scale=QS).then_inc(q_high, 1)
                weigh_all(t, b, SA if isinstance(t, int) and t == 0 else AHEAD + 3, SA if last else SA + 2)
                act.wait_ge(q_turned, t + 1)
                at_least(act, mix_done, t - 1)
                nc.scalar.copy(qT[:, b], turned16(1)).then_inc(q_out, 1)
                if not last:
                    weigh_all(t, b, SA + 2, SA + AHEAD)

            edge_tiles(act, edge_act)

            def gate_weights():
                act.wait_ge(scales_made, 2)
                act.wait_ge(graw_turned, 1)
                for f in range(C):
                    nc.scalar.activation(G16[:, 0, f, :], bank[2 + f][:, :], ACT.Copy, scale=scf[:, 0:1]
                                         ).then_inc(high_made, 1)

            def tail_tick(g, j):
                if exists(g, j):
                    normalise(tail, g, j, zn, zh, 2)
                next_deviations(tail, g, j)
                if isinstance(g, int) and g == 0 and j == 1:
                    gate_weights()
                g1, j1 = back(g, j, 1)
                if gate_exists(g1, j1):
                    q, m = gate_at(g1, j1)
                    if isinstance(q, int) and q == 0 and m == 0:
                        act.wait_ge(small_loaded, 16 * 14)
                    act.wait_ge(gf_done, C * q + m + 1)
                    at_least(act, gf_out, C * q + m)
                    waited(act)
                    n = LAST if isinstance(q, int) and q == NQ - 1 else D
                    nc.scalar.activation(gjunk[:, 0:n], bank[2 + m][:, 0:n], ACT.Relu, scale=cols[:, 0:1],
                                         bias=gbias[:, m:m + 1], accum_out=gsum[:, m, bass.ds(q, 1)]
                                         ).then_inc(gf_out, 1)

            act.wait_ge(edges_done, 1)
            deviations(tail, 0, 0, Q4)
            row_ticks(act, tail_tick, Q4 * NQ + 6)
            act.wait_ge(scales_made, 3)
            for f in range(C):
                nc.scalar.activation(W1m[:, 0, f, :], bank[2 + f // 2][:, (f % 2) * F:(f % 2 + 1) * F], ACT.Copy,
                                     scale=scf[:, 1:2]).then_inc(high_made, 1)

            def hidden(q, par, n, chunks=range(FC)):
                for o in chunks:
                    act.wait_ge(h_done, FC * q + o + 1)
                    if not (isinstance(q, int) and q < 2):
                        act.wait_ge(o_done, Q4 * (q - 1))
                    at_least(act, low_made, H_LOW + FC * (q - 1) + o + 1)
                    nc.scalar.activation(h32[:, o, 0:n], bank[2 + o][:, 0:n], ACT.Relu, scale=cols[:, 1:2],
                                         bias=b1m[:, o:o + 1]).then_inc(high_made, 1)
                    act.wait_ge(high_made, H_HIGH + FC * q + o + 1)
                    nc.scalar.activation(hT[:, par, 0, o, 0:n], h32[:, o, 0:n], ACT.Copy, scale=scf[:, 2:3]
                                         ).then_inc(h_out, 1)

            def next_input(g, j):
                t, b = tile_at(g, j), j % 2
                at_least(act, res_made, t - 1)
                waited(act)
                nc.scalar.activation(zq[:, b, :], flat(acc, t), ACT.Identity, scale=rs[:, bass.ds(t, 1)],
                                     bias=nb[:, bass.ds(t, 1)]).then_inc(zq_made, 1)

            def out_tick(g, j):
                quad = quad_at(g, j)
                gn, jn = back(g, j, -1)
                if exists(gn, jn):
                    next_input(gn, jn)
                if j % Q4 == 0 and not (isinstance(quad, int) and quad == 0):
                    n = 1 if isinstance(quad, int) and quad == NQ else Q4
                    act.wait_ge(two_made, quad)
                    at_least(act, r_rec, quad - 1)
                    nc.scalar.activation(sd4[:, 0:n], var4[:, (j // Q4 + 1) % 2, 0:n, 1], ACT.Sqrt, bias=epsc[:, :]
                                         ).then_inc(r_std, 1)
                g4, j4 = back(g, j, Q4)
                if exists(g4, j4):
                    t, b = tile_at(g4, j4), j4 % 2
                    act.wait_ge(r_scale, quad_at(g4, j4) + 1)
                    at_least(act, ob_made, t - 1)
                    nc.scalar.activation(zr[:, b, :], res[:, j4, :], ACT.Identity, scale=rsr[:, j4 // Q4, j4 % Q4:j4 % Q4 + 1],
                                         bias=nbr[:, j4 // Q4, j4 % Q4:j4 % Q4 + 1]).then_inc(zr_made, 1)
                if j % Q4 < FC and not (isinstance(quad, int) and quad + 1 >= NQ):
                    hidden(quad + 1, (j // Q4 + 1) % 2, P if isinstance(quad, int) and quad + 1 == NQ - 1 else Q4 * P,
                           [j % Q4])

            act.wait_ge(w2_out, FC)
            hidden(0, 0, Q4 * P)
            next_input(0, 0)
            row_ticks(act, out_tick, T + Q4)

        @block.gpsimd
        def _(pool):
            pool.memset(ident[:, :], 0.0).then_inc(pool_set, 1)
            pool.memset(ident16[:, :], 0.0).then_inc(pool_set, 1)
            pool.memset(ones[:, :], 1.0).then_inc(pool_set, 1)
            pool.memset(ones3[:, :], 1.0).then_inc(pool_set, 1)
            pool.memset(headmask[:, :], 0.0).then_inc(pool_set, 1)
            pool.memset(epsc[:, :], EPS).then_inc(pool_set, 1)
            pool.memset(minus1[:, :], -1.0).then_inc(pool_set, 1)
            pool.memset(acc[:, T - 1, :], 0.0).then_inc(pool_set, 1)
            pool.memset(pad[:, 0, :], 0).then_inc(pool_set, 1)
            pool.memset(pad[:, 1, :], int(OUTSIDE)).then_inc(pool_set, 1)
            pool.memset(pad[:, 2, :], 0).then_inc(pool_set, 1)
            pool.iota(stepi[:, :], pattern=[[P, SC]], base=0, channel_multiplier=1).then_inc(pool_set, 1)
            pool.iota(iota16[:, :], pattern=[[1, P]], base=0, channel_multiplier=0,
                      allow_small_or_imprecise_dtypes=True).then_inc(pool_set, 1)
            pool.iota(irow[:, :], pattern=[[1, NG]], base=0, channel_multiplier=0).then_inc(pool_set, 1)
            pool.wait_ge(pool_set, 14)
            for m in (ident, ident16):
                pool.affine_select(out=m[:, :], in_=m[:, :], compare_op=ALU.not_equal, fill=1.0, base=0,
                                   pattern=[[-1, P]], channel_multiplier=1).then_inc(pool_set, 1)
            pool.wait_ge(pool_set, 16)
            for b in range(2):
                pool.memset(headmask[b * HD:(b + 1) * HD, b * HD:(b + 1) * HD], 1.0).then_inc(pool_set, 1)
            pool.wait_ge(pool_set, 18)
            pool.nop(nofuse=True).then_inc(consts_made, 1)

            pool.wait_ge(maxes_made, 1)
            pool.partition_all_reduce(mxa[:, 0:6], mx[:, 0:6], P, RMAX).then_inc(maxes_all, 1)
            pool.partition_all_reduce(uns[:, :], viol[:, :], P, RADD).then_inc(maxes_all, 1)

            def pool_link(ins):
                pool_links[0] += 1
                ins.then_inc(pool_chain, 1)
                pool.wait_ge(pool_chain, pool_links[0])

            pool_links = [0]
            pool.wait_ge(bias_loaded, 16 * 5)
            pool.wait_ge(scales_made, 1)
            split(nc.gpsimd, brow[:, 1, :], bfq, b16[:, 1], cols[0:1, 5:6], pool_link).then_inc(q_split, 1)
            pool_link(pool.tensor_tensor(mrow[:, :], brow[:, 2, :], brow[:, 3, :], ALU.add))
            pool_link(pool.tensor_scalar(mrow[:, :], mrow[:, :], 1.0 / H, None, ALU.mult))


            def load_groups(n):
                at_least(pool, turned, n)
                at_least(pool, picked, n)
                pool.indirect_dma_start(out=pk[:, :, :].rearrange("p i e -> p (i e)"), out_offset=None, in_=packed,
                                        in_offset=bass.IndirectOffsetOnAxis(ap=gidx[:, n:n + 1], axis=0)
                                        ).then_inc(pk_ready, 16)

            pool.wait_ge(bias_spread, 16 * 3)
            pool.wait_ge(q_spread, 16 * 3)
            pool.memset(ksacc[:, :], 0.0).then_inc(pool_set, 1)
            pool.wait_ge(pool_set, 19)

            pool.wait_ge(groups_made, 1)
            pool.wait_ge(edges_packed, 16 * 7)
            load_groups(0)

            def sum_k(g, j):
                g2, j2 = back(g, j, 2)
                if exists(g2, j2):
                    t, b = tile_at(g2, j2), j2 % 2
                    n = LAST if isinstance(t, int) and t == T - 1 else P
                    pool.wait_ge(f_used, t + 1)
                    at_least(pool, k_summed, t)
                    waited(pool)
                    pool.tensor_tensor(ksacc[0:n, :], ksacc[0:n, :], kf[0:n, b, :], ALU.add).then_inc(k_summed, 1)
                if isinstance(g, int) and g == 0 and 1 <= j + 1 - TABLES_AT < SC:
                    load_groups(j + 1 - TABLES_AT)

            row_ticks(pool, sum_k, T + 2)

            pool.wait_ge(high_made, 3)
            pool.wait_ge(low_made, 2)
            pool.memset(fill[:, :], 0.0).then_inc(pool_set, 1)
            pool.wait_ge(pool_set, 20)
            head_kept(pool)
            pool.wait_ge(m_done, T)
            limit = pool.to_reg(T * P - 1)

            def gather(slot, column):
                pool.indirect_dma_start(out=rows[:, slot].rearrange("p a d -> p (a d)"), out_offset=None, in_=y_rows,
                                        in_offset=bass.IndirectOffsetOnAxis(ap=column, axis=0),
                                        bounds_check=limit, oob_is_err=False).then_inc(gathered[slot], 16)

            def edge_gathers(t, h, b):
                pool.tensor_copy(idxc[:, b, :], idx[:, bass.ds(SA * t, SA), :].rearrange("p s j -> p (s j)")
                                 ).then_inc(indexed, 1)
                pool.wait_ge(indexed, t + 1)
                for r in range(SA):
                    at_least(pool, stepped, SA * t + r - RING + 1)
                    waited(pool)
                    slot = 2 * place(h, b, r)[0]
                    for i in range(2):
                        gather(slot + i, idxc[:, b, 2 * r + i:2 * r + i + 1])

            pool.wait_ge(tabled, SC)
            edge_tiles(pool, edge_gathers)

            pool.wait_ge(edge_added, SA * T)
            unordered = pool.value_load(flag[0:1, 0:1], min_val=0, max_val=1)
            with pool.If(unordered > 0):
                with pool.Fori(0, NG) as n:
                    pool.wait_ge(u_group, n + 1)
                    waited(pool)
                    pool.indirect_dma_start(out=pk[:, :, :].rearrange("p i e -> p (i e)"), out_offset=None, in_=packed,
                                            in_offset=bass.IndirectOffsetOnAxis(ap=gidx[:, 0:1], axis=0)
                                            ).then_inc(u_pk, 16)
                    pool.wait_ge(u_index, n + 1)
                    waited(pool)
                    for i in range(2):
                        pool.indirect_dma_start(
                            out=rows[:, i].rearrange("p a d -> p (a d)"), out_offset=None, in_=y_rows,
                            in_offset=bass.IndirectOffsetOnAxis(ap=idxc[:, 0, i:i + 1], axis=0),
                            bounds_check=limit, oob_is_err=False).then_inc(u_gathered, 16)

            pool.wait_ge(maxes_made, 2)
            pool.partition_all_reduce(mxa[:, 0:1], mx[:, 0:1], P, RMAX).then_inc(maxes_all, 1)
            pool.wait_ge(maxes_made, 3)
            pool.partition_all_reduce(mxa[:, 1:2], mx[:, 1:2], P, RMAX).then_inc(maxes_all, 1)
            pool.wait_ge(maxes_made, 4)
            pool.partition_all_reduce(mxa[:, 2:4], mx[:, 2:4], P, RMAX).then_inc(maxes_all, 1)

            def out_tick(g, j):
                if exists(g, j):
                    t = tile_at(g, j)
                    pool.wait_ge(zq_made, t + 1)
                    waited(pool)
                    pool.tensor_tensor(flat(acc, t), flat(acc, t), lnbb[:, :], ALU.add).then_inc(based, 1)
                g4, j4 = back(g, j, Q4)
                if exists(g4, j4):
                    t, b = tile_at(g4, j4), j4 % 2
                    pool.wait_ge(gained, t + 1)
                    pool.wait_ge(based, t + 1)
                    at_least(pool, out_kept[b], 16 * half_at(g4, j4))
                    waited(pool)
                    pool.tensor_tensor(ob[:, b, :], zr[:, b, :], flat(acc, t), ALU.add).then_inc(ob_made, 1)

            row_ticks(pool, out_tick, T + Q4)

        @block.vector
        def _(dve):
            links = [0]

            def link(ins):
                links[0] += 1
                ins.then_inc(chain, 1)
                dve.wait_ge(chain, links[0])

            def powers(first, n, link):
                s = slice(first, first + n)
                link(nc.vector.tensor_scalar(mxa[:, s], mxa[:, s], 1e-30, None, ALU.max))
                link(nc.vector.tensor_scalar(pw[:, s], mxa[:, s].bitcast(I32), EXPONENT, None, ALU.bitwise_and))
                link(nc.vector.tensor_scalar(sc[:, s], pw[:, s], -1.0, float(268 << 23), ALU.mult, ALU.add))
                link(nc.vector.tensor_scalar(inv[:, s], sc[:, s], -1.0, float(254 << 23), ALU.mult, ALU.add))

            def pick(gate, negtile, link, ready, count, path=True):
                dve.wait_ge(ready, count)
                link(nc.vector.tensor_scalar(rel[:, :], pk[:, 1, :], negtile, None, ALU.add))
                link(nc.vector.tensor_scalar(ok[:, :], rel[:, :], 0.0, gate, ALU.is_ge, ALU.mult))
                link(nc.vector.scalar_tensor_tensor(out=ok[:, :], in0=rel[:, :], scalar=float(P), in1=ok[:, :],
                                                    op0=ALU.is_lt, op1=ALU.mult))
                link(nc.vector.tensor_scalar(ok[:, :], ok[:, :], -OUTSIDE, OUTSIDE, ALU.mult, ALU.add))
                if path:
                    link(nc.vector.tensor_tensor(srcf[:, :], pk[:, 0, :], ok[:, :], ALU.add))
                else:
                    link(nc.vector.tensor_copy(srcf[:, :], pk[:, 0, :]))
                link(nc.vector.tensor_tensor(rel[:, :], rel[:, :], ok[:, :], ALU.add))

            def tabulate(s, link):
                span = slice(s, s + P)
                link(nc.vector.tensor_copy(idx[:, span, :].rearrange("p s j -> p j s"), by_half(bank[4][:, 0:EG])))
                link(nc.vector.tensor_copy(tab[:, span, :, 0].rearrange("p s j -> p j s"), by_half(bank[4][:, EG:2 * EG])))
                link(nc.vector.tensor_scalar(tab[:, span, :, 1].rearrange("p s j -> p j s"), by_half(bank[5][:, 0:EG]),
                                             scf[:, 3:4], None, ALU.mult))

            link(nc.vector.memset(mx[:, :], 0.0))
            link(nc.vector.memset(viol[:, :], 0.0))
            for k in range(3):
                dve.wait_ge(w_loaded[k], 16)
                link(nc.vector.tensor_reduce(mx[:, k:k + 1], stage[:, k].rearrange("p c n -> p (c n)"), AX_X, ALU.max,
                                             apply_absolute_value=True))
            dve.wait_ge(bias_loaded, 16 * 5)
            link(nc.vector.tensor_reduce(mx[0:1, 5:6], brow[:, 0, :], AX_X, ALU.max, apply_absolute_value=True))
            dve.wait_ge(edges_loaded, 64)
            link(nc.vector.tensor_reduce(mx[0:DR, 3:4], ews[0:DR, :], AX_X, ALU.max, apply_absolute_value=True))
            link(nc.vector.tensor_tensor(ews[0:DR, :], dsts[0:DR, 1:DW + 1], dsts[0:DR, 0:DW], ALU.is_lt))
            nc.vector.tensor_reduce(viol[0:DR, :], ews[0:DR, :], AX_X, ALU.add).then_inc(maxes_made, 1)

            dve.wait_ge(start_loaded, 16)
            dve.wait_ge(consts_made, 1)
            link(nc.vector.tensor_scalar(srow[:, :], srow[:, :], 7, None, ALU.logical_shift_right))
            link(nc.vector.tensor_copy(srowf[:, :], srow[:, :]))
            link(nc.vector.memset(srowf[:, 0:1], 0.0))
            nc.vector.tensor_tensor(srowf[:, :], srowf[:, :], irow[:, :], ALU.add).then_inc(start_made, 1)

            dve.wait_ge(maxes_all, 2)
            link(nc.vector.tensor_scalar(mxa[:, 4:5], mxa[:, 0:1], float(D), None, ALU.mult))
            link(nc.vector.tensor_scalar(mxa[:, 5:6], mxa[:, 5:6], 1.0, None, ALU.add))
            link(nc.vector.scalar_tensor_tensor(out=mxa[:, 5:6], in0=mxa[:, 1:2], scalar=float(D), in1=mxa[:, 5:6],
                                                op0=ALU.mult, op1=ALU.add))
            powers(0, 6, link)
            scale = 1.0 / XS
            link(nc.vector.tensor_scalar(cols[:, 0:1], invf[:, 0:1], scf[:, 4:5], scale, ALU.mult, ALU.mult))
            link(nc.vector.tensor_scalar(cols[:, 1:3], invf[:, 1:3], scale, None, ALU.mult))
            link(nc.vector.tensor_tensor(cols[:, 3:4], invf[:, 3:4], invf[:, 4:5], ALU.mult))
            link(nc.vector.tensor_scalar(cols[:, 4:6], scf[:, 1:3], XS, None, ALU.mult))
            link(nc.vector.tensor_scalar(cols[:, 6:7], invf[:, 5:6], scale, None, ALU.mult))
            link(nc.vector.tensor_scalar(uns[:, :], uns[:, :], 1.0, None, ALU.min))
            link(nc.vector.tensor_scalar(srt[:, :], uns[:, :], -1.0, 1.0, ALU.mult, ALU.add))
            link(nc.vector.tensor_copy(flag[:, :], uns[0:1, :]))
            nc.vector.tensor_copy(stepf[:, :], stepi[:, :]).then_inc(scales_made, 1)

            dve.wait_ge(start_spread, 1)
            link(nc.vector.tensor_copy(startb[:, :], bank[4][:, 0:NG]))
            for k, w16 in enumerate((Wg16, Wk16)):
                dve.wait_ge(high_made, k + 1)
                nc.vector.scalar_tensor_tensor(out=w16[:, 1], in0=stage[:, k], scalar=scf[:, k:k + 1], in1=w16[:, 0],
                                               op0=ALU.mult, op1=ALU.subtract).then_inc(low_made, 1)

            split(nc.vector, brow[:, 0, :], bf, b16[:, 0], cols[0:1, 4:5], link).then_inc(bias_split, 1)

            def find_groups():
                dve.wait_ge(scales_made, 1)
                for c in range(SC):
                    link(nc.vector.tensor_scalar(junk[:, :], startb[:, :], stepf[:, c:c + 1], None, ALU.is_le, ALU.add,
                                                 accum_out=cnt[:, c:c + 1]))
                link(nc.vector.tensor_tensor(ntile[:, :], stepf[:, :], cnt[:, :], ALU.subtract))
                link(nc.vector.tensor_scalar(ntile[:, :], ntile[:, :], 1.0, None, ALU.add))
                link(nc.vector.tensor_scalar(late[:, :], ntile[:, :], float(T - 1), -OUTSIDE, ALU.is_gt, ALU.mult))
                link(nc.vector.scalar_tensor_tensor(out=negd[:, :], in0=ntile[:, :], scalar=-float(P), in1=late[:, :],
                                                    op0=ALU.mult, op1=ALU.add))
                link(nc.vector.tensor_scalar(ntile[:, :], ntile[:, :], float(T - 1), 0.0, ALU.min, ALU.max))
                nc.vector.tensor_scalar(gidx[:, :], cnt[:, :], -1.0, None, ALU.add).then_inc(groups_made, 1)

            def find_tiles():
                dve.wait_ge(tiles_turned, 1)
                link(nc.vector.tensor_copy(tileof[:, :], bank[5][0:1, :]))
                dve.nop(nofuse=True).then_inc(tiles_out, 1)

            def pick_steps(n):
                pick(srt[:, 0:1], negd[:, n:n + 1], link, pk_ready, 16 * (n + 1))
                dve.nop(nofuse=True).then_inc(picked, 1)

            def tabulate_steps(n):
                dve.wait_ge(turned, n + 1)
                tabulate(n * P, link)
                dve.nop(nofuse=True).then_inc(tabled, 1)

            def statistics(loop, quad, par, n, part=None):
                half = Q4 // 2
                at_least(dve, loop.vars_made, quad)
                for i in range(0 if part != 1 else half, n if part != 0 else min(n, half)):
                    if loop is head:
                        dve.wait_ge(x_loaded[i], 16 * (quad + 1))
                    waited(dve)
                    nc.vector.bn_stats(st6[:, i, :], flat(acc, Q4 * quad + i)).then_inc(loop.six, 1)
                if part == 0:
                    return
                dve.wait_ge(loop.six, Q4 * quad + n)
                waited(dve)
                for i in range(n):
                    ins = nc.vector.bn_aggr(var4[:, par, i, :], st6[:, i, :])
                ins.then_inc(loop.vars_made, 1)

            first_half = lambda *a: statistics(*a, part=0)
            second_half = lambda *a: statistics(*a, part=1)

            def scales(loop, quad, par, n):
                s = bass.ds(Q4 * quad, n)
                dve.wait_ge(loop.std_made, quad + 1)
                nc.vector.reciprocal(rs[:, s], sd4[:, 0:n]).then_inc(loop.rec, 1)
                dve.wait_ge(loop.rec, 2 * quad + 1)
                nc.vector.tensor_scalar(rs[:, s], rs[:, s], XS, None, ALU.mult).then_inc(loop.rec, 1)
                dve.wait_ge(loop.rec, 2 * quad + 2)
                nc.vector.scalar_tensor_tensor(out=nb[:, s], in0=var4[:, par, 0:n, 0], scalar=-1.0, in1=rs[:, s],
                                               op0=ALU.mult, op1=ALU.mult).then_inc(loop.scale_made, 1)

            def group_work(loop, g, j, what, at):
                quad = quad_at(g, j)
                if j % Q4 == at and not (isinstance(quad, int) and quad + 1 >= NQ):
                    what(loop, quad + 1, (j // Q4 + 1) % 2, 1 if isinstance(quad, int) and quad + 1 == NQ - 1 else Q4)

            def low_parts(loop, g, j, full, high, dest, ring):
                t = tile_at(g, j)
                dve.wait_ge(loop.high, 2 * t + 2)
                if loop is head:
                    at_least(dve, m_done, t - ring + 1)
                else:
                    at_least(dve, tail.turned, t - ring + 1)
                nc.vector.tensor_tensor(dest[:, j % ring, :], full[:, j % 2, :], high[:, j % ring, :], ALU.subtract
                                        ).then_inc(loop.low, 1)

            def head_tick(g, j):
                group_work(head, g, j, first_half, 0)
                group_work(head, g, j, second_half, 1)
                g2, j2 = back(g, j, 2)
                t2, two_back = tile_at(g2, j2), j2 % 2
                if exists(g2, j2):
                    dve.wait_ge(y_high, t2 + 1)
                    at_least(dve, y_kept[two_back], 16 * half_at(g2, j2))
                    nc.vector.scalar_tensor_tensor(out=yb[:, two_back, 1, :], in0=bank[4][:, :], scalar=cols[:, 0:1],
                                                   in1=yb[:, two_back, 0, :], op0=ALU.mult, op1=ALU.subtract
                                                   ).then_inc(y_low, 1)
                    dve.wait_ge(f_done, t2 + 1)
                    at_least(dve, f_used, t2)
                    if isinstance(t2, int) and t2 == 0:
                        dve.wait_ge(q_spread, 16 * 3)
                    nc.vector.tensor_scalar(mb[:, :], bank[5][:, :], cols[:, 1:2], 1.0, ALU.mult, ALU.min).then_inc(f_min, 1)
                if exists(g, j):
                    low_parts(head, g, j, xnb, xh, xl, 4)
                if exists(g2, j2):
                    dve.wait_ge(f_exp, t2 + 1)
                    at_least(dve, k_high, t2 - 1)
                    at_least(dve, k_low, t2 - 1)
                    at_least(dve, k_summed, t2 - 1)
                    nc.vector.scalar_tensor_tensor(out=kf[:, two_back, :], in0=bank[5][:, :], scalar=cols[:, 1:2], in1=mb[:, :],
                                                   op0=ALU.mult, op1=ALU.max).then_inc(f_used, 1)
                first = isinstance(g, int) and g == 0
                if first and j == 0:
                    dve.wait_ge(high_made, 3)
                    nc.vector.scalar_tensor_tensor(out=Wq16[:, 1], in0=stage[:, 2], scalar=scf[:, 2:3], in1=Wq16[:, 0],
                                                   op0=ALU.mult, op1=ALU.subtract).then_inc(wq_low, 1)
                if first and j == 1:
                    find_groups()
                if first and j == TABLES_AT - 1:
                    find_tiles()
                if first and 0 <= j - TABLES_AT < SC:
                    tabulate_steps(j - TABLES_AT)
                g1, j1 = back(g, j, 1)
                if exists(g1, j1):
                    t, b = tile_at(g1, j1), j1 % 2
                    dve.wait_ge(head.turned, t + 1)
                    at_least(dve, f_done, t - 1)
                    at_least(dve, head.turned_kept[b], 16 * half_at(g1, j1))
                    nc.vector.tensor_copy(xtb[:, b], turned16(6 + b)).then_inc(head.turned_out, 1)
                if exists(g2, j2):
                    dve.wait_ge(k_high, t2 + 1)
                    at_least(dve, m_done, t2 - 1)
                    nc.vector.scalar_tensor_tensor(out=kl[:, two_back, :], in0=kf[:, two_back, :], scalar=scf[:, 5:6],
                                                   in1=kh[:, two_back, :], op0=ALU.mult, op1=ALU.subtract).then_inc(k_low, 1)
                group_work(head, g, j, scales, 3)
                if first and 0 <= j + 1 - TABLES_AT < SC:
                    pick_steps(j + 1 - TABLES_AT)

            statistics(head, 0, 0, Q4)
            scales(head, 0, 0, Q4)
            row_ticks(dve, head_tick, T + 2)

            def low_weights(t, b):
                dve.wait_ge(copied, 2 * t + 2)
                nc.vector.tensor_tensor(wlo[:, b, :], tabc[:, b, :, 1], wh16[:, b, :], ALU.subtract).then_inc(parted, 1)

            def hot(t, b, r):
                s, at = SA * t + r, (SA * b + r) % OHS
                b = (b + r // SA) % 2
                at_least(dve, weighted, s - OHS + 1)
                for i in range(2):
                    e = 2 * (r % SA) + i
                    ins = nc.vector.tensor_scalar(oneh[:, at, i, :], iota16[:, :], tabc[:, b, e, 0:1], None, ALU.is_equal)
                ins.then_inc(onehot, 1)

            def add_step(t, b, r):
                s = SA * t + r
                tile = dve.value_load(tileof[0:1, bass.ds(s, 1)], min_val=0, max_val=T - 1)
                dve.wait_ge(stepped, s + 1)
                at_least(dve, edge_added, s)
                at_least(dve, mix_added, t if r > ADD_MIX_AFTER else t - 1)
                waited(dve)
                nc.vector.scalar_tensor_tensor(out=flat(acc, tile), in0=step_bank(b, r)[:, :],
                                               scalar=cols[:, 3:4], in1=flat(acc, tile), op0=ALU.mult, op1=ALU.add
                                               ).then_inc(edge_added, 1)

            def add_mix(t, b, added):
                dve.wait_ge(mix_done, t + 1)
                dve.wait_ge(edge_added, added)
                waited(dve)
                nc.vector.scalar_tensor_tensor(out=flat(acc, t), in0=bank[2 + b][:, :], scalar=cols[:, 7:8],
                                               in1=flat(acc, t), op0=ALU.mult, op1=ALU.add).then_inc(mix_added, 1)

            by_head = lambda ap: ap.rearrange("p (h d) -> p h d", h=H)

            def q_least(t):
                dve.wait_ge(f_done, T + t + 1)
                dve.wait_ge(f_used, T + t)
                nc.vector.tensor_scalar(mb[:, :], bank[0][:, :], cols[:, 2:3], 1.0, ALU.mult, ALU.min).then_inc(f_min, 1)

            def q_whole(t):
                dve.wait_ge(f_exp, T + t + 1)
                if isinstance(t, int) and t == 0:
                    dve.wait_ge(k_summed, T)
                nc.vector.scalar_tensor_tensor(out=kf[:, 0, :], in0=bank[0][:, :], scalar=cols[:, 2:3], in1=mb[:, :],
                                               op0=ALU.mult, op1=ALU.max).then_inc(f_used, 1)

            def q_times_sum(t):
                dve.wait_ge(f_used, T + t + 1)
                at_least(dve, q_scaled, t)
                nc.vector.tensor_tensor(qk[:, :], kf[:, 0, :], ksb[:, :], ALU.mult).then_inc(q_summed, 1)

            def q_sums(t):
                dve.wait_ge(q_summed, 3 * t + 1)
                nc.vector.tensor_reduce(den[:, :], by_head(qk[:, :]), AX_X, ALU.add).then_inc(q_summed, 1)

            def q_inverse(t):
                dve.wait_ge(q_summed, 3 * t + 2)
                nc.vector.reciprocal(rden[:, :], den[:, :]).then_inc(q_summed, 1)

            def q_share(t):
                dve.wait_ge(q_summed, 3 * t + 3)
                at_least(dve, q_low, t)
                nc.vector.tensor_tensor(by_head(qs[:, :]), by_head(qk[:, :]),
                                        rden[:, :].rearrange("p (h d) -> p h d", d=1).broadcast_to([P, H, HD]), ALU.mult
                                        ).then_inc(q_scaled, 1)

            def q_lower(t):
                dve.wait_ge(q_high, t + 1)
                at_least(dve, q_turned, t)
                nc.vector.scalar_tensor_tensor(out=qhl[:, 1, :], in0=qs[:, :], scalar=QS, in1=qhl[:, 0, :],
                                               op0=ALU.mult, op1=ALU.subtract).then_inc(q_low, 1)

            def kv_rows():
                dve.wait_ge(kvp_done, 1)
                for c in (0, 2):
                    nc.vector.tensor_scalar(KVP[:, c, :], bank[c][:, :], kinv[:, c:c + 1], None, ALU.mult
                                            ).then_inc(kvp_out, 1)
                dve.wait_ge(kvp_out, C)
                nc.vector.tensor_reduce(mx[:, 6:7], KVP[:, :, :].rearrange("p c n -> p (c n)"), AX_X, ALU.max,
                                        apply_absolute_value=True).then_inc(kmax_row, 1)

            def kv_largest():
                dve.wait_ge(kmax_turned, 1)
                nc.vector.tensor_reduce(mx[0:1, 7:8], bank[5][0:1, 0:P], AX_X, ALU.max).then_inc(kmax_row, 1)

            def kv_parts():
                dve.wait_ge(kmax_spread, 1)
                link(nc.vector.tensor_copy(mxa[:, 6:7], bank[5][:, P:P + 1]))
                powers(6, 1, link)
                link(nc.vector.tensor_scalar(cols[:, 7:8], invf[:, 6:7], 1.0 / QS, None, ALU.mult))
                for c in range(C):
                    link(nc.vector.tensor_scalar(KVP16[:, 0, c, :], KVP[:, c, :], scf[:, 6:7], None, ALU.mult))
                    nc.vector.scalar_tensor_tensor(out=KVP16[:, 1, c, :], in0=KVP[:, c, :], scalar=scf[:, 6:7],
                                                   in1=KVP16[:, 0, c, :], op0=ALU.mult, op1=ALU.subtract
                                                   ).then_inc(kvp_low, 1)

            dve.wait_ge(ks_done, 1)
            link(nc.vector.tensor_copy(ksb[:, :], bank[4][:, :]))
            link(nc.vector.tensor_scalar(kinv[:, :], bank[5][:, 0:C], 1e-30, None, ALU.max))
            nc.vector.reciprocal(kinv[:, :], kinv[:, :]).then_inc(kv_out, 1)
            dve.wait_ge(m_done, T)
            for c in (0, 2):
                nc.vector.tensor_scalar(M32[:, c, :], bank[c][:, :], cols[:, 6:7], None, ALU.mult).then_inc(m_out, 1)
            dve.wait_ge(m_turned, 1)
            for c in (0, 2):
                nc.vector.tensor_copy(MT32[:, c, :], bank[c][:, :]).then_inc(mt_out, 1)
            low_weights(0, 0)
            dve.wait_ge(k_low, T)
            for r in range(AHEAD):
                hot(0, 0, r)
            add_step(0, 0, 0)
            dve.wait_ge(kv_done, 1)
            for c in range(C):
                nc.vector.tensor_tensor(kvt[:, c, :], bank[4][:, c * P:(c + 1) * P], headmask[:, :], ALU.mult
                                        ).then_inc(kv_out, 1)

            def edge_dve(t, h, b):
                last = isinstance(t, int) and t == T - 1
                add, ahead = lambda r: add_step(t, b, r), lambda r: hot(t, b, r + AHEAD)
                if isinstance(t, int) and t == 0:
                    ahead(0)
                    add(1)
                    ahead(1)
                    add(2)
                    add(3)
                    kv_rows()
                    ahead(2)
                    add(4)
                    kv_largest()
                    q_least(t)
                    add(5)
                    ahead(3)
                    q_whole(t)
                    ahead(4)
                    q_times_sum(t)
                    add(6)
                    q_sums(t)
                    q_inverse(t)
                    q_share(t)
                    add(7)
                    q_lower(t)
                else:
                    q_least(t)
                    ahead(0)
                    add(0)
                    q_whole(t)
                    ahead(1)
                    q_times_sum(t)
                    add(1)
                    q_sums(t)
                    ahead(2)
                    q_inverse(t)
                    add(2)
                    q_share(t)
                    ahead(3)
                    add(3)
                    q_lower(t)
                    ahead(4)
                    add(4)
                    add_mix(t - 1, 1 - b, SA * t + ADD_MIX_AFTER + 1)
                if not last:
                    low_weights(t + 1, 1 - b)
                for r in range(5, SA):
                    if not last:
                        ahead(r)
                    if not (isinstance(t, int) and t == 0 and r < SA - 1):
                        add(r)
                if isinstance(t, int) and t == 0:
                    kv_parts()

            edge_tiles(dve, edge_dve)
            add_mix(T - 1, (T - 1) % 2, SA * T)
            dve.wait_ge(mix_added, T)

            unordered = dve.value_load(flag[0:1, 0:1], min_val=0, max_val=1)
            with dve.If(unordered > 0):
                K = 11

                def linked(n):
                    k = [0]

                    def one(ins):
                        k[0] += 1
                        ins.then_inc(u_chain, 1)
                        dve.wait_ge(u_chain, K * n + k[0])
                    return one, k

                nc.vector.tensor_scalar(negd[:, 0:1], stepf[:, 0:1], -float(P), None, ALU.mult).then_inc(u_start, 1)
                nc.vector.memset(cnt[:, 0:1], 0.0).then_inc(u_start, 1)
                dve.wait_ge(u_start, 2)
                with dve.Fori(0, NG) as n:
                    one, k = linked(n)
                    one(nc.vector.tensor_copy(gidx[:, 0:1], cnt[:, 0:1]))
                    one(nc.vector.tensor_scalar(cnt[:, 0:1], cnt[:, 0:1], 1.0, None, ALU.add))
                    dve.nop(nofuse=True).then_inc(u_group, 1)
                    pick(1.0, negd[:, 0:1], one, u_pk, 16 * n + 16, path=False)
                    dve.nop(nofuse=True).then_inc(u_picked, 1)
                    dve.wait_ge(u_turned, n + 1)
                    tabulate(0, one)
                    assert k[0] == K
                    nc.vector.tensor_copy(idxc[:, 0, 0:2], idx[:, 0, :]).then_inc(u_index, 1)
                    with dve.Fori(0, T) as d:
                        s = T * n + d
                        waited(dve)
                        nc.vector.tensor_copy(tabc[:, 0, 0:2, :], tab[:, bass.ds(d, 1)].rearrange("p s j k -> p (s j) k")
                                              ).then_inc(u_onehot, 1)
                        dve.wait_ge(u_onehot, U_HOT * s + 1)
                        nc.vector.tensor_copy(wh16[:, 0, 0:2], tabc[:, 0, 0:2, 1]).then_inc(u_onehot, 1)
                        dve.wait_ge(u_onehot, U_HOT * s + 2)
                        nc.vector.tensor_tensor(wlo[:, 0, 0:2], tabc[:, 0, 0:2, 1], wh16[:, 0, 0:2], ALU.subtract
                                                ).then_inc(u_onehot, 1)
                        dve.wait_ge(u_onehot, U_HOT * s + 3)
                        for i in range(2):
                            for part, w in enumerate((tabc[:, 0, i, 1:2], wlo[:, 0, i:i + 1])):
                                ins = nc.vector.tensor_scalar(hotw[:, 0, i, part, :], iota16[:, :], tabc[:, 0, i, 0:1],
                                                              w, ALU.is_equal, ALU.mult)
                        ins.then_inc(u_onehot, 1)
                        dve.wait_ge(u_stepped, s + 1)
                        waited(dve)
                        nc.vector.scalar_tensor_tensor(out=flat(acc, d), in0=bank[6][:, :], scalar=cols[:, 3:4],
                                                       in1=flat(acc, d), op0=ALU.mult, op1=ALU.add).then_inc(u_added, 1)
                        dve.wait_ge(u_added, s + 1)
                        waited(dve)
            dve.nop(nofuse=True).then_inc(edges_done, 1)

            statistics(tail, 0, 0, Q4)
            dve.wait_ge(graw_loaded, 16)
            nc.vector.tensor_reduce(mx[:, 0:1], graw[:, :, :].rearrange("p c n -> p (c n)"), AX_X, ALU.max,
                                    apply_absolute_value=True).then_inc(maxes_made, 1)
            scales(tail, 0, 0, Q4)

            def gate_scale():
                link(nc.vector.memset(lncoef[:, :], LN_MERGE))
                nc.vector.memset(lncoef[0:1, :], 1.0 - LN_MERGE * NE).then_inc(ln_coefs, 1)
                dve.wait_ge(maxes_all, 3)
                powers(0, 1, link)
                nc.vector.tensor_scalar(cols[:, 0:1], invf[:, 0:1], 1.0 / XS, None, ALU.mult).then_inc(scales_made, 1)

            def gate_weights():
                for f in range(C):
                    dve.wait_ge(high_made, 3 + f + 1)
                    nc.vector.scalar_tensor_tensor(out=G16[:, 1, f, :], in0=bank[2 + f][:, :], scalar=scf[:, 0:1],
                                                   in1=G16[:, 0, f, :], op0=ALU.mult, op1=ALU.subtract
                                                   ).then_inc(low_made, 1)

            def last_norm():
                dve.wait_ge(ln_done, 2)
                nc.vector.tensor_copy(lngb[:, :], bank[6][:, :]).then_inc(ln_out, 1)
                nc.vector.tensor_copy(lnbb[:, :], bank[7][:, :]).then_inc(ln_out, 1)

            def gate_seconds():
                dve.wait_ge(ln_done, 3)
                nc.vector.tensor_copy(g2T[:, :, :].rearrange("p c e -> p (c e)"), bank[6][:, 0:C * NE]).then_inc(ln_out, 1)

            def tail_tick(g, j):
                if exists(g, j):
                    low_parts(tail, g, j, zn, zh, zl, 2)
                if isinstance(g, int) and g == 0 and j in (0, 2, 5, 7):
                    {0: gate_scale, 2: gate_weights, 5: last_norm, 7: gate_seconds}[j]()
                g1, j1 = back(g, j, 1)
                if exists(g1, j1):
                    t, b = tile_at(g1, j1), j1 % 2
                    dve.wait_ge(tail.turned, t + 1)
                    free_group(dve, g1, j1)
                    nc.vector.tensor_copy(ztg[:, j1 // Q4, j1 % Q4], turned16(b)).then_inc(tail.turned_out, 1)
                group_work(tail, g, j, first_half, 0)
                group_work(tail, g, j, second_half, 1)
                group_work(tail, g, j, scales, 3)

            row_ticks(dve, tail_tick, T + 1)

            dve.wait_ge(gf_out, C * NQ)
            link(nc.vector.tensor_reduce(gsq[:, :], gsum[:, :, :], AX_X, ALU.add))
            link(nc.vector.tensor_scalar(gcol[:, :], gsq[:, :], 1.0 / N, None, ALU.mult))
            for c in range(C):
                nc.vector.tensor_scalar(geye[:, c, :], ones[:, :], gcol[:, c:c + 1], None, ALU.mult).then_inc(gate_in, 1)
            dve.wait_ge(gate_done, 2)
            link(nc.vector.tensor_copy(gall[:, :], bank[6][:, 0:NE]))
            link(nc.vector.tensor_copy(gT[:, :], bank[6][0:NE, NE:NE + 1]))
            for e in range(NE):
                nc.vector.tensor_scalar(geye[:, e, :], ident[:, :], gall[:, e:e + 1], None, ALU.mult).then_inc(gate_out, 1)
            dve.wait_ge(small_loaded, 16 * 14)
            dve.wait_ge(tv1_loaded, 16 * NE)
            for e in range(NE):
                nc.vector.scalar_tensor_tensor(out=W1raw[:, :, :], in0=tvW1[:, e], scalar=gall[:, e:e + 1],
                                               in1=W1raw[:, :, :], op0=ALU.mult, op1=ALU.add).then_inc(gate_out, 1)
                dve.wait_ge(gate_out, NE + e + 1)
            for o in range(FC):
                link(nc.vector.tensor_tensor(tvb1[:, o, :], tvb1[:, o, :], gall[:, :], ALU.mult))
            link(nc.vector.tensor_reduce(b1m[:, :], tvb1[:, :, :], AX_X, ALU.add))
            link(nc.vector.tensor_tensor(b1m[:, :], b1m[:, :], b1c[:, :], ALU.add))
            dve.wait_ge(gate_done, 3)
            link(nc.vector.tensor_copy(b2f[:, :], bank[7][0:1, :]))
            split(nc.vector, None, b2f, b216, None, link).then_inc(bias_split, 1)
            dve.wait_ge(w1_done, 1)
            link(nc.vector.tensor_reduce(mx[:, 1:2], bank[2][:, :], AX_X, ALU.max, apply_absolute_value=True))
            link(nc.vector.tensor_reduce(mx[:, 2:3], bank[3][:, :], AX_X, ALU.max, apply_absolute_value=True))
            nc.vector.tensor_tensor(mx[:, 1:2], mx[:, 1:2], mx[:, 2:3], ALU.max).then_inc(maxes_made, 1)
            dve.wait_ge(maxes_all, 4)
            powers(1, 1, link)
            nc.vector.tensor_scalar(cols[:, 1:2], invf[:, 1:2], 1.0 / XS, None, ALU.mult).then_inc(scales_made, 1)
            dve.wait_ge(scales_made, 3)
            for f in range(C):
                dve.wait_ge(high_made, 3 + C + f // 2 * 2 + 2)
                nc.vector.scalar_tensor_tensor(out=W1m[:, 1, f, :], in0=bank[2 + f // 2][:, (f % 2) * F:(f % 2 + 1) * F],
                                               scalar=scf[:, 1:2], in1=W1m[:, 0, f, :], op0=ALU.mult, op1=ALU.subtract
                                               ).then_inc(low_made, 1)
            for ap in (rs, nb):
                link(nc.vector.tensor_scalar(ap[:, 0:T], ap[:, 0:T], 1.0 / XS, None, ALU.mult))
            link(nc.vector.tensor_reduce(mx[:, 2:3], b1m[:, :], AX_X, ALU.max, apply_absolute_value=True))
            dve.wait_ge(w2_done, 1)
            for o in range(FC):
                link(nc.vector.tensor_reduce(mx[:, 3 + o:4 + o], bank[4 + o][:, :], AX_X, ALU.max,
                                             apply_absolute_value=True))
            nc.vector.tensor_tensor(mx[:, 3:4], mx[:, 3:4], mx[:, 4:5], ALU.max).then_inc(maxes_made, 1)
            dve.wait_ge(maxes_all, 5)
            link(nc.vector.scalar_tensor_tensor(out=mxa[:, 2:3], in0=mxa[:, 1:2], scalar=float(D), in1=mxa[:, 2:3],
                                                op0=ALU.mult, op1=ALU.add))
            link(nc.vector.tensor_scalar(mxa[:, 2:4], mxa[:, 2:4], 1e-10, None, ALU.max))
            powers(2, 2, link)
            link(nc.vector.tensor_tensor(cols[:, 4:5], invf[:, 2:3], invf[:, 3:4], ALU.mult))
            link(nc.vector.tensor_tensor(cols[:, 5:6], scf[:, 2:3], scf[:, 3:4], ALU.mult))
            link(nc.vector.tensor_scalar(scale3[:, 0:P], ones3[:, :], cols[0:3, 5:6], None, ALU.mult))
            for o in range(FC):
                link(nc.vector.tensor_scalar(W2m[:, 0, o, :], bank[4 + o][:, :], scf[:, 3:4], None, ALU.mult))
                nc.vector.scalar_tensor_tensor(out=W2m[:, 1, o, :], in0=bank[4 + o][:, :], scalar=scf[:, 3:4],
                                               in1=W2m[:, 0, o, :], op0=ALU.mult, op1=ALU.subtract).then_inc(w2_out, 1)

            def hidden_low(q, par, n, chunks=range(FC)):
                for o in chunks:
                    dve.wait_ge(h_out, FC * q + o + 1)
                    nc.vector.scalar_tensor_tensor(out=hT[:, par, 1, o, 0:n], in0=h32[:, o, 0:n], scalar=scf[:, 2:3],
                                                   in1=hT[:, par, 0, o, 0:n], op0=ALU.mult, op1=ALU.subtract
                                                   ).then_inc(low_made, 1)

            hidden_low(0, 0, Q4 * P)

            def out_tick(g, j):
                quad = quad_at(g, j)
                if exists(g, j):
                    t, b = tile_at(g, j), j % 2
                    dve.wait_ge(zq_made, t + 1)
                    dve.wait_ge(o_done, t + 1)
                    at_least(dve, zr_made, t - U + 1)
                    nc.vector.scalar_tensor_tensor(out=res[:, j, :], in0=bank[4 + b][:, :], scalar=cols[:, 4:5],
                                                   in1=zq[:, b, :], op0=ALU.mult, op1=ALU.add).then_inc(res_made, 1)
                    dve.wait_ge(res_made, t + 1)
                    if not (isinstance(quad, int) and quad == 0):
                        dve.wait_ge(two_made, quad)
                    nc.vector.bn_stats(st6[:, j % Q4, :], res[:, j, :]).then_inc(six_made, 1)
                if j % Q4 == 0 and not (isinstance(quad, int) and quad == 0):
                    n, par = 1 if isinstance(quad, int) and quad == NQ else Q4, (j // Q4 + 1) % 2
                    dve.wait_ge(r_std, quad)
                    nc.vector.reciprocal(rsr[:, par, 0:n], sd4[:, 0:n]).then_inc(r_rec, 1)
                    dve.wait_ge(r_rec, quad)
                    nc.vector.scalar_tensor_tensor(out=nbr[:, par, 0:n], in0=var4[:, par, 0:n, 0], scalar=-1.0,
                                                   in1=rsr[:, par, 0:n], op0=ALU.mult, op1=ALU.mult).then_inc(r_scale, 1)
                if j % Q4 in (1, 2) and not (isinstance(quad, int) and quad + 1 >= NQ):
                    hidden_low(quad + 1, (j // Q4 + 1) % 2, P if isinstance(quad, int) and quad + 1 == NQ - 1 else Q4 * P,
                               [j % Q4 - 1])
                last = isinstance(quad, int) and quad == NQ - 1
                if exists(g, j) and (j % Q4 == Q4 - 1 or last):
                    n = 1 if last else Q4
                    dve.wait_ge(six_made, Q4 * quad + n)
                    waited(dve)
                    for i in range(n):
                        ins = nc.vector.bn_aggr(var4[:, j // Q4, i, :], st6[:, i, :])
                    ins.then_inc(two_made, 1)
                g4, j4 = back(g, j, Q4)
                if exists(g4, j4):
                    t, b = tile_at(g4, j4), j4 % 2
                    dve.wait_ge(zr_made, t + 1)
                    nc.vector.tensor_tensor(zr[:, b, :], zr[:, b, :], lngb[:, :], ALU.mult).then_inc(gained, 1)

            row_ticks(dve, out_tick, T + Q4)

        @block.tensor
        def _(pe):
            def accumulate(dest, pairs, first=None, only=True):
                pairs = ([first] if first else []) + pairs
                for n, (lhs, rhs) in enumerate(pairs):
                    ins = nc.tensor.matmul(dest, lhs, rhs, start=(n == 0 and only), stop=(n == len(pairs) - 1),
                                           skip_group_check=not only)
                return ins

            pe.wait_ge(consts_made, 1)
            pe.wait_ge(start_made, 1)
            nc.tensor.matmul(bank[4][:, 0:NG], ones[0:1, :], srowf[:, :], start=True, stop=True).then_inc(start_spread, 1)

            def turn_tiles():
                pe.wait_ge(groups_made, 1)
                for c in range(SC):
                    ins = nc.tensor.matmul(bank[5][0:1, c * P:(c + 1) * P], ntile[:, c:c + 1], ident[:, :],
                                           start=True, stop=True)
                ins.then_inc(tiles_turned, 1)
                pe.wait_ge(tiles_out, 1)

            def turn_picked():
                for i in range(2):
                    nc.tensor.transpose(bank[4][:, i * P:(i + 1) * P], srcf[:, i * P:(i + 1) * P], ident[:, :])
                    nc.tensor.transpose(bank[4][:, (2 + i) * P:(3 + i) * P], rel[:, i * P:(i + 1) * P], ident[:, :])
                    ins = nc.tensor.transpose(bank[5][:, i * P:(i + 1) * P],
                                              pk[:, 2, i * P:(i + 1) * P].bitcast(F32), ident[:, :])
                return ins

            def turn_rows(loop, g, j, high, low, ring, base):
                t, b = tile_at(g, j), j % 2
                pe.wait_ge(loop.low, t + 1)
                at_least(pe, loop.turned_out, t - 1)
                for part, rows_ in enumerate((high, low)):
                    for c in range(C):
                        ins = nc.tensor.transpose(turned16(base + b)[:, part, c, :], rows_[:, j % ring, c * P:(c + 1) * P],
                                                  ident16[:, :])
                ins.then_inc(loop.turned, 1)

            def head_tick(g, j):
                if exists(g, j):
                    turn_rows(head, g, j, xh, xl, 4, 6)
                g1, j1 = back(g, j, 1)
                if exists(g1, j1):
                    t, b = tile_at(g1, j1), j1 % 2
                    if isinstance(t, int) and t == 0:
                        pe.wait_ge(low_made, 2)
                    n = t + 1 - TABLES_AT if isinstance(t, int) else SC
                    if -1 <= n < SC:
                        pe.wait_ge(f_used, t)
                        pe.wait_ge(y_low, t)
                        if n < 0:
                            turn_tiles()
                        else:
                            pe.wait_ge(picked, n + 1)
                            turn_picked().then_inc(turned, 1)
                            pe.wait_ge(tabled, n + 1)
                    pe.wait_ge(head.turned_out, t + 1)
                    at_least(pe, y_low, t)
                    accumulate(bank[4][:, :], [(xtb[:, b, p, c, :], Wg16[:, q, c, :]) for c in range(C)
                                               for p, q in PASSES]).then_inc(y_made, 1)
                    at_least(pe, f_used, t)
                    if isinstance(t, int) and t == 0:
                        pe.wait_ge(bias_spread, 16 * 3)
                    accumulate(bank[5][:, :], [(xtb[:, b, p, c, :], Wk16[:, q, c, :]) for c in range(C)
                                               for p, q in PASSES], first=(ones3[:, :], krows[:, :])).then_inc(f_done, 1)
                g2, j2 = back(g, j, 2)
                if exists(g2, j2):
                    t, b = tile_at(g2, j2), j2 % 2
                    pe.wait_ge(k_low, t + 1)
                    for c in range(C):
                        s = slice(c * P, (c + 1) * P)
                        for n, (p, q) in enumerate(PASSES):
                            ins = nc.tensor.matmul(bank[c][:, :], (kh, kl)[p][:, b, s], (xh, xl)[q][:, j2 % 4, :],
                                                   start=isinstance(t, int) and t == 0 and n == 0,
                                                   stop=isinstance(t, int) and t == T - 1 and n == 2,
                                                   skip_group_check=True)
                    ins.then_inc(m_done, 1)

            row_ticks(pe, head_tick, T + 2)

            def step(t, h, b, r):
                s = SA * t + r
                at, use = place(h, b, r)
                pe.wait_ge(weighted, s + 1)
                at_least(pe, edge_added, s - len(STEP_BANKS) + 1)
                for i in range(2):
                    pe.wait_ge(gathered[2 * at + i], 16 * use)
                accumulate(step_bank(b, r)[:, :],
                           [(hotw[:, (SA * b + r) % OHS, i, p, :], rows[:, 2 * at + i, q, :]) for i in range(2) for p, q in PASSES]
                           ).then_inc(stepped, 1)

            pe.wait_ge(k_summed, T)
            pe.wait_ge(y_low, T)
            pe.wait_ge(f_used, T)
            nc.tensor.matmul(bank[4][:, :], ones[:, :], ksacc[:, :], start=True, stop=True)
            for c in range(C):
                ins = nc.tensor.matmul(bank[5][:, c:c + 1], ksacc[:, c * P:(c + 1) * P], ones[:, 0:1], start=True, stop=True)
            ins.then_inc(ks_done, 1)
            pe.wait_ge(m_out, C)
            for f in range(C):
                for c in range(C):
                    ins = nc.tensor.transpose(bank[f][:, c * P:(c + 1) * P], M32[:, c, f * P:(f + 1) * P], ident[:, :])
            ins.then_inc(m_turned, 1)
            step(0, 0, 0, 0)
            pe.wait_ge(mt_out, C)
            pe.wait_ge(vp_loaded, 32)
            pe.wait_ge(kv_out, 1)
            for c in range(C):
                s = slice(c * P, (c + 1) * P)
                ins = accumulate(bank[4][:, s], [(Wv32[:, f, s], MT32[:, f, s]) for f in range(C)],
                                 first=(bvrow[:, s], ksb[0:1, s]))
            ins.then_inc(kv_done, 1)

            def mix(t, b):
                pe.wait_ge(q_out, t + 1)
                at_least(pe, mix_added, t - 1)
                if isinstance(t, int) and t == 0:
                    pe.wait_ge(kvp_low, C)
                accumulate(bank[2 + b][:, :], [(qT[:, b, p, c, :], KVP16[:, q, c, :]) for c in range(C)
                                               for p, q in PASSES]).then_inc(mix_done, 1)

            def q_product(t, h, b):
                pe.wait_ge(xt_in[b], 16 * h + 16)
                pe.wait_ge(f_used, T + t)
                accumulate(bank[0][:, :], [(xta[:, b, p, c, :], Wq16[:, q, c, :]) for c in range(C) for p, q in PASSES],
                           first=(ones3[:, :], qrows[:, :])).then_inc(f_done, 1)

            def turn_q(t):
                pe.wait_ge(q_low, t + 1)
                at_least(pe, q_out, t)
                for part in range(2):
                    for c in range(C):
                        ins = nc.tensor.transpose(turned16(1)[:, part, c, :], qhl[:, part, c * P:(c + 1) * P], ident16[:, :])
                ins.then_inc(q_turned, 1)

            def edge_pe(t, h, b):
                steps = lambda first, last: [step(t, h, b, r) for r in range(first, last)]
                if isinstance(t, int) and t == 0:
                    steps(1, 2)
                    pe.wait_ge(kv_out, C + 1)
                    steps(2, 4)
                    for c in range(C):
                        ins = accumulate(bank[c][:, :], [(kvt[:, c, :], Wp32[:, c, :])],
                                         first=(ksb[0:1, c * P:(c + 1) * P], mrow[:, :]))
                    ins.then_inc(kvp_done, 1)
                    steps(4, 6)
                    pe.wait_ge(kmax_row, 1)
                    nc.tensor.transpose(bank[5][0:1, 0:P], mx[:, 6:7], ident[:, :]).then_inc(kmax_turned, 1)
                    pe.wait_ge(kmax_row, 2)
                    nc.tensor.matmul(bank[5][:, P:P + 1], ones[0:1, :], mx[0:1, 7:8], start=True, stop=True
                                     ).then_inc(kmax_spread, 1)
                    pe.wait_ge(q_spread, 16 * 3)
                    pe.wait_ge(wq_low, 1)
                    pe.wait_ge(kvp_out, C)
                    q_product(t, h, b)
                    steps(6, SA)
                    turn_q(t)
                else:
                    q_product(t, h, b)
                    steps(0, MIX_AT)
                    mix(t - 1, 1 - b)
                    steps(MIX_AT, 6)
                    turn_q(t)
                    steps(6, SA)

            edge_tiles(pe, edge_pe)
            mix(T - 1, (T - 1) % 2)
            pe.wait_ge(edge_added, SA * T)
            unordered = pe.value_load(flag[0:1, 0:1], min_val=0, max_val=1)
            with pe.If(unordered > 0):
                with pe.Fori(0, NG) as n:
                    pe.wait_ge(u_picked, n + 1)
                    waited(pe)
                    turn_picked().then_inc(u_turned, 1)
                    pe.wait_ge(u_gathered, 32 * n + 32)
                    waited(pe)
                    with pe.Fori(0, T) as d:
                        s = T * n + d
                        pe.wait_ge(u_onehot, U_HOT * s + U_HOT)
                        waited(pe)
                        accumulate(bank[6][:, :], [(hotw[:, 0, i, p, :], rows[:, i, q, :]) for i in range(2)
                                                   for p, q in PASSES]).then_inc(u_stepped, 1)

            pe.wait_ge(edges_done, 1)
            pe.wait_ge(graw_loaded, 16)
            for f in range(C):
                for o in range(C):
                    ins = nc.tensor.transpose(bank[2 + f][:, o * P:(o + 1) * P], graw[:, o, f * P:(f + 1) * P], ident[:, :])
            ins.then_inc(graw_turned, 1)

            def last_norm():
                pe.wait_ge(small_loaded, 16 * 14)
                pe.wait_ge(ln_coefs, 1)
                nc.tensor.matmul(bank[6][:, :], lncoef[:, :], lnrows[:, :], start=True, stop=True).then_inc(ln_done, 1)
                nc.tensor.matmul(bank[7][:, :], lncoef[:, :], lbrows[:, :], start=True, stop=True).then_inc(ln_done, 1)

            def turn_g2():
                pe.wait_ge(ln_out, 2)
                for c in range(C):
                    ins = nc.tensor.transpose(bank[6][:, c * NE:(c + 1) * NE], g2raw[:, c * P:(c + 1) * P],
                                              ident[0:NE, 0:NE])
                ins.then_inc(ln_done, 1)

            def tail_tick(g, j):
                if exists(g, j):
                    turn_rows(tail, g, j, zh, zl, 2, 0)
                if isinstance(g, int) and g == 0 and j == 4:
                    last_norm()
                if isinstance(g, int) and g == 0 and j == 6:
                    turn_g2()
                if gate_exists(g, j):
                    q, m = gate_at(g, j)
                    par = ((j - Q4 - 1 - m) // Q4) % 2
                    last = isinstance(q, int) and q == NQ - 1
                    if m == 0:
                        if isinstance(q, int) and q == 0:
                            pe.wait_ge(high_made, 3 + C)
                            pe.wait_ge(low_made, 2 + C)
                        pe.wait_ge(tail.turned_out, T if last else Q4 * q + Q4)
                    at_least(pe, gf_out, C * (q - 1) + m + 1)
                    s = slice(m * P, (m + 1) * P)
                    n = LAST if last else D
                    if last:
                        pairs = [(G16[:, a, f, s], ztg[:, par, 0, b_, f, 0:LAST]) for f in range(C) for a, b_ in PASSES]
                    else:
                        pairs = [(G16[:, a, f, s], ztg[:, par, :, b_, f, :]) for f in range(C) for a, b_ in PASSES]
                    accumulate(bank[2 + m][:, 0:n], pairs).then_inc(gf_done, 1)

            row_ticks(pe, tail_tick, Q4 * NQ + 5)

            pe.wait_ge(ln_out, 3)
            pe.wait_ge(gate_in, C)
            accumulate(bank[6][:, 0:NE], [(geye[:, c, :], g2T[:, c, :]) for c in range(C)] + [(ones[0:1, :], gbr[:, :])]
                       ).then_inc(gate_done, 1)
            accumulate(bank[6][0:NE, NE:NE + 1], [(g2T[:, c, :], gcol[:, c:c + 1]) for c in range(C)]
                       + [(gbr[:, :], ones[0:1, 0:1])]).then_inc(gate_done, 1)
            pe.wait_ge(gate_out, NE)
            accumulate(bank[7][0:1, :], [(gT[:, :], tvb2[:, :]), (ones[0:1, 0:1], b2r[:, :])]).then_inc(gate_done, 1)
            pe.wait_ge(tv2_loaded, 16 * NE)
            for o in range(FC):
                for c in range(C):
                    s = slice(o * P, (o + 1) * P)
                    ins = accumulate(bank[4 + o][:, c * P:(c + 1) * P], [(W2raw[:, c, s], ident[:, :])]
                                     + [(tvW2[:, e, c, s], geye[:, e, :]) for e in range(NE)])
                if o == 0:
                    pe.wait_ge(gate_out, 2 * NE)
                    for f in range(C):
                        for m in range(FC):
                            turned_block = nc.tensor.transpose(bank[2 + f // 2][:, (f % 2) * F + m * P:(f % 2) * F + (m + 1) * P],
                                                               W1raw[:, m, f * P:(f + 1) * P], ident[:, :])
                    turned_block.then_inc(w1_done, 1)
            ins.then_inc(w2_done, 1)
            pe.wait_ge(high_made, 3 + C + C)
            pe.wait_ge(low_made, 2 + C + C)

            def hidden(q, par, n, chunks=range(FC)):
                for o in chunks:
                    at_least(pe, h_out, FC * (q - 1) + o + 1)
                    s = slice(o * P, (o + 1) * P)
                    if n == P:
                        pairs = [(W1m[:, a, f, s], xd[:, par, 0, b_, f, :]) for f in range(C) for a, b_ in PASSES]
                    else:
                        pairs = [(W1m[:, a, f, s], xd[:, par, :, b_, f, :]) for f in range(C) for a, b_ in PASSES]
                    accumulate(bank[2 + o][:, 0:n], pairs).then_inc(h_done, 1)

            pe.wait_ge(zd_in[0], 16)
            hidden(0, 0, Q4 * P)
            pe.wait_ge(w2_out, FC)
            pe.wait_ge(bias_spread, 16 * 6)

            def out_tick(g, j):
                quad = quad_at(g, j)
                if j % Q4 < FC and not (isinstance(quad, int) and quad + 1 >= NQ):
                    pe.wait_ge(zd_in[(j // Q4 + 1) % 2], 16 * (g + 1 + j // Q4))
                    hidden(quad + 1, (j // Q4 + 1) % 2, P if isinstance(quad, int) and quad + 1 == NQ - 1 else Q4 * P,
                           [j % Q4])
                if exists(g, j):
                    t, b = tile_at(g, j), j % 2
                    pe.wait_ge(low_made, H_LOW + FC * (quad + 1))
                    at_least(pe, res_made, t - 1)
                    s = slice((j % Q4) * P, (j % Q4 + 1) * P)
                    accumulate(bank[4 + b][:, :], [(hT[:, j // Q4, p, o, s], W2m[:, q, o, :]) for o in range(FC)
                                                   for p, q in PASSES], first=(scale3[:, 0:P], b2rows[:, :])
                               ).then_inc(o_done, 1)

            row_ticks(pe, out_tick, T)


_NAMES = ["x", "src", "dst", "edge_weight", "L0_gnn_weight", "L0_gnn_bias", "L0_mix_Wq", "L0_mix_bq", "L0_mix_Wk",
          "L0_mix_bk", "L0_mix_Wv", "L0_mix_bv", "L0_mix_Wp", "L0_mix_bp", "L0_ffn_gfc1_w", "L0_ffn_gfc1_b",
          "L0_ffn_gfc2_w", "L0_ffn_gfc2_b", "L0_ffn_W1", "L0_ffn_b1", "L0_ffn_W2", "L0_ffn_b2", "L0_ffn_ln_g",
          "L0_ffn_ln_b", "L0_ffn_tv_W1", "L0_ffn_tv_b1", "L0_ffn_tv_W2", "L0_ffn_tv_b2", "L0_ffn_tv_ln_g",
          "L0_ffn_tv_ln_b"]


def kernel(**inputs):
    import numpy as np
    from concourse import bacc
    from concourse.bass_utils import run_bass_kernel_spmd

    nc = bacc.Bacc("TRN2", target_bir_lowering=False, num_devices=1)
    arrays, args = {}, []
    for name in _NAMES:
        a = np.ascontiguousarray(inputs[name])
        arrays["in_" + name] = a
        args.append(nc.dram_tensor("in_" + name, a.shape, mybir.dt.from_np(a.dtype), kind="ExternalInput").ap())
    out = nc.dram_tensor("out", (N, D), F32, kind="ExternalOutput").ap()
    build(nc, *args, out)
    result = run_bass_kernel_spmd(nc, [arrays], core_ids=[0])
    return result.results[0]["out"]
```
